# Optimizing a Trainium2 kernel written in Bass

```python
import numpy as np
import jax
import jax.numpy as jnp

def _softmax(x, axis=-1):
    return jax.nn.softmax(x, axis=axis)

def _gelu(x):
    return jax.nn.gelu(x, approximate=True)

def _silu(x):
    return jax.nn.silu(x)

def _sigmoid(x):
    return jax.nn.sigmoid(x)

def _layernorm(x, axis=-1, eps=1e-05):
    m = jnp.mean(x, axis=axis, keepdims=True)
    v = jnp.var(x, axis=axis, keepdims=True)
    return (x - m) / jnp.sqrt(v + eps)

def _scatter_add(tgt, idx, src, axis=0):
    return tgt.at[idx].add(src)

def _segment_sum(src, seg, n):
    return jax.ops.segment_sum(src, seg, n)
kernel_name = 'mk_prb_d2_jaxref_r8_0319bd'

def setup_inputs(seed: int=0):
    np.random.seed(seed)
    _w = jnp.asarray

    def _L0_attn_setup():
        import jax, jax.numpy as jnp
        import numpy as np
        B, S, D = (4, 128, 256)
        H, G = (16, 2)
        HD = D // H

        def rotate_half(x):
            x1, x2 = (x[..., :x.shape[-1] // 2], x[..., x.shape[-1] // 2:])
            return jnp.concatenate([-x2, x1], axis=-1)
        key = jax.random.key(seed)
        ks = jax.random.split(key, 9)
        scale = 0.02
        return {'x': jax.random.normal(ks[0], (B, S, D), jnp.float32), 'wq': jax.random.normal(ks[1], (D, D), jnp.float32) * scale, 'bq': jnp.zeros((D,), jnp.float32), 'wk': jax.random.normal(ks[2], (D, G * HD), jnp.float32) * scale, 'bk': jnp.zeros((G * HD,), jnp.float32), 'wv': jax.random.normal(ks[3], (D, G * HD), jnp.float32) * scale, 'bv': jnp.zeros((G * HD,), jnp.float32), 'wo': jax.random.normal(ks[4], (D, D), jnp.float32) * scale, 'bo': jnp.zeros((D,), jnp.float32)}
    _L0_attn_in = _L0_attn_setup()

    def _L0_ffn_setup():
        import jax, jax.numpy as jnp
        import numpy as np
        N_BLOCKS = 16
        BLOCK_SIZE = 64
        TOP_K = N_BLOCKS // 4
        key = jax.random.key(seed)
        k1, k2, k3, k4, k5 = jax.random.split(key, 5)
        in_f, out_f = (256, 1024)
        x = jax.random.normal(k1, (2, 512, in_f), dtype=jnp.float32)
        Wr = jax.random.normal(k2, (N_BLOCKS, in_f), dtype=jnp.float32) * in_f ** (-0.5)
        br = jnp.zeros((N_BLOCKS,), dtype=jnp.float32)
        W1 = jax.random.normal(k3, (out_f, in_f), dtype=jnp.float32) * in_f ** (-0.5)
        W2 = jax.random.normal(k4, (in_f, out_f), dtype=jnp.float32) * out_f ** (-0.5)
        return {'x': x, 'Wr': Wr, 'br': br, 'W1': W1, 'W2': W2}
    _L0_ffn_in = _L0_ffn_setup()

    def _L1_attn_setup():
        import jax, jax.numpy as jnp
        import numpy as np
        EMBED = 256
        HEADS = 16
        HEAD_DIM = EMBED // HEADS
        CHUNK = 128
        BASE = 10000.0
        EPS = 1e-06

        def _alibi_log_decay(h):
            slopes = 2.0 ** (-8.0 * (jnp.arange(h, dtype=jnp.float32) + 1.0) / h)
            return -slopes

        def _lrpe_rotate(x):
            b, n, h, d = x.shape
            half = d // 2
            theta = BASE ** (-2.0 * jnp.arange(half, dtype=jnp.float32) / d)
            ang = jnp.arange(n, dtype=jnp.float32)[:, None] * theta[None, :]
            cos = jnp.cos(ang)[None, :, None, :]
            sin = jnp.sin(ang)[None, :, None, :]
            x1, x2 = (x[..., :half], x[..., half:])
            return jnp.concatenate([x1 * cos - x2 * sin, x1 * sin + x2 * cos], axis=-1)

        def _lightning_attn(q, k, v, log_lam):
            b, n, h, d = q.shape
            C = CHUNK
            nc = n // C
            qc = q.reshape(b, nc, C, h, d).transpose(1, 0, 2, 3, 4)
            kc = k.reshape(b, nc, C, h, d).transpose(1, 0, 2, 3, 4)
            vc = v.reshape(b, nc, C, h, d).transpose(1, 0, 2, 3, 4)
            i = jnp.arange(C, dtype=jnp.float32)
            diff = i[:, None] - i[None, :]
            D = jnp.where(diff[None] >= 0, jnp.exp(log_lam[:, None, None] * diff[None]), 0.0)
            decay_q = jnp.exp(log_lam[None, :] * (i[:, None] + 1.0))
            decay_k = jnp.exp(log_lam[None, :] * (C - 1.0 - i[:, None]))
            lam_C = jnp.exp(log_lam * C)

            def step(S, qkv):
                qi, ki, vi = qkv
                scores = jnp.einsum('bthd,bshd->bhts', qi, ki) * D[None]
                o_intra = jnp.einsum('bhts,bshd->bthd', scores, vi)
                o_inter = jnp.einsum('bthd,bhde->bthe', qi * decay_q[None, :, :, None], S)
                S_new = lam_C[None, :, None, None] * S + jnp.einsum('bshd,bshe->bhde', ki * decay_k[None, :, :, None], vi)
                return (S_new, o_intra + o_inter)
            S0 = jnp.zeros((b, h, d, d), q.dtype)
            _, o = jax.lax.scan(step, S0, (qc, kc, vc))
            return o.transpose(1, 0, 2, 3, 4).reshape(b, n, h, d)

        def _gated_group_rmsnorm(o, gate, weight):
            b, n, d = o.shape
            x = o * jax.nn.sigmoid(gate)
            xg = x.reshape(b, n, HEADS, HEAD_DIM)
            ms = jnp.mean(xg * xg, axis=-1, keepdims=True)
            xg = xg * jax.lax.rsqrt(ms + EPS)
            return xg.reshape(b, n, d) * weight
        key = jax.random.key(seed)
        ks = jax.random.split(key, 8)
        b, n, d = (2, 256, EMBED)
        std = 0.02
        return {'x': jax.random.normal(ks[0], (b, n, d), jnp.float32), 'Wq': jax.random.normal(ks[1], (d, d), jnp.float32) * std, 'Wk': jax.random.normal(ks[2], (d, d), jnp.float32) * std, 'Wv': jax.random.normal(ks[3], (d, d), jnp.float32) * std, 'Wo': jax.random.normal(ks[4], (d, d), jnp.float32) * std, 'Wg1': jax.random.normal(ks[5], (d, HEAD_DIM), jnp.float32) * std, 'Wg2': jax.random.normal(ks[6], (HEAD_DIM, d), jnp.float32) * std, 'norm_weight': jnp.ones((d,), jnp.float32)}
    _L1_attn_in = _L1_attn_setup()

    def _L1_ffn_setup():
        import jax, jax.numpy as jnp
        import numpy as np
        TOP_K = 2
        key = jax.random.key(seed)
        ks = jax.random.split(key, 5)
        B, S, D, M, E = (4, 256, 256, 256, 8)
        x = jax.random.normal(ks[0], (B, S, D), dtype=jnp.float32)
        gate_kernel = jax.random.normal(ks[1], (D, E), dtype=jnp.float32) / np.sqrt(D)
        wi_0 = jax.random.normal(ks[2], (E, D, M), dtype=jnp.float32) / np.sqrt(D)
        wi_1 = jax.random.normal(ks[3], (E, D, M), dtype=jnp.float32) / np.sqrt(D)
        wo = jax.random.normal(ks[4], (E, M, D), dtype=jnp.float32) / np.sqrt(M)
        return {'x': x, 'gate_kernel': gate_kernel, 'wi_0': wi_0, 'wi_1': wi_1, 'wo': wo}
    _L1_ffn_in = _L1_ffn_setup()
    _d = {'L0_attn_x': _L0_attn_in['x'], 'L0_attn_wq': _L0_attn_in['wq'], 'L0_attn_bq': _L0_attn_in['bq'], 'L0_attn_wk': _L0_attn_in['wk'], 'L0_attn_bk': _L0_attn_in['bk'], 'L0_attn_wv': _L0_attn_in['wv'], 'L0_attn_bv': _L0_attn_in['bv'], 'L0_attn_wo': _L0_attn_in['wo'], 'L0_attn_bo': _L0_attn_in['bo'], 'L0_ffn_Wr': _L0_ffn_in['Wr'], 'L0_ffn_br': _L0_ffn_in['br'], 'L0_ffn_W1': _L0_ffn_in['W1'], 'L0_ffn_W2': _L0_ffn_in['W2'], 'L1_attn_Wq': _L1_attn_in['Wq'], 'L1_attn_Wk': _L1_attn_in['Wk'], 'L1_attn_Wv': _L1_attn_in['Wv'], 'L1_attn_Wo': _L1_attn_in['Wo'], 'L1_attn_Wg1': _L1_attn_in['Wg1'], 'L1_attn_Wg2': _L1_attn_in['Wg2'], 'L1_attn_norm_weight': _L1_attn_in['norm_weight'], 'L1_ffn_gate_kernel': _L1_ffn_in['gate_kernel'], 'L1_ffn_wi_0': _L1_ffn_in['wi_0'], 'L1_ffn_wi_1': _L1_ffn_in['wi_1'], 'L1_ffn_wo': _L1_ffn_in['wo']}
    _x0 = _d['L0_attn_x']
    _d['L0_attn_x'] = jax.random.normal(jax.random.fold_in(jax.random.key(seed), 1), (4, 256, 256), dtype=_x0.dtype)
    del _x0
    return _d

def reference(L0_attn_x, L0_attn_wq, L0_attn_bq, L0_attn_wk, L0_attn_bk, L0_attn_wv, L0_attn_bv, L0_attn_wo, L0_attn_bo, L0_ffn_Wr, L0_ffn_br, L0_ffn_W1, L0_ffn_W2, L1_attn_Wq, L1_attn_Wk, L1_attn_Wv, L1_attn_Wo, L1_attn_Wg1, L1_attn_Wg2, L1_attn_norm_weight, L1_ffn_gate_kernel, L1_ffn_wi_0, L1_ffn_wi_1, L1_ffn_wo):

    def _L0_attn_ref(x, wq, bq, wk, bk, wv, bv, wo, bo):
        import jax, jax.numpy as jnp
        import numpy as np
        B, S, D = (4, 128, 256)
        H, G = (16, 2)
        HD = D // H

        def rotate_half(x):
            x1, x2 = (x[..., :x.shape[-1] // 2], x[..., x.shape[-1] // 2:])
            return jnp.concatenate([-x2, x1], axis=-1)
        b, s, d = x.shape
        hd = HD
        q = (x @ wq + bq).reshape(b, s, H, hd)
        k = (x @ wk + bk).reshape(b, s, G, hd)
        v = (x @ wv + bv).reshape(b, s, G, hd)
        inv_freq = 1.0 / 1250 ** (jnp.arange(0, hd, 2, dtype=jnp.float32) / hd)
        t = jnp.arange(s, dtype=jnp.float32)
        freqs = jnp.outer(t, inv_freq)
        freqs = jnp.concatenate([freqs, freqs], -1)
        sin = jnp.sin(freqs)[:, None, :]
        cos = jnp.cos(freqs)[:, None, :]
        q = q * cos + rotate_half(q) * sin
        q = q * hd ** (-0.5)
        k = k * cos + rotate_half(k) * sin
        reps = H // G
        k_exp = jnp.repeat(k, reps, axis=2)
        v_exp = jnp.repeat(v, reps, axis=2)
        scores = jnp.einsum('bqhd,bkhd->bhqk', q, k_exp) * hd ** (-0.5)
        attn = jax.nn.softmax(scores, axis=-1)
        out = jnp.einsum('bhqk,bkhd->bqhd', attn, v_exp).reshape(b, s, d)
        return out @ wo + bo

    def _L0_ffn_ref(x, Wr, br, W1, W2):
        import jax, jax.numpy as jnp
        import numpy as np
        N_BLOCKS = 16
        BLOCK_SIZE = 64
        TOP_K = N_BLOCKS // 4
        x_shape = x.shape
        in_f = x_shape[-1]
        xf = x.reshape(-1, in_f)
        n = xf.shape[0]
        prob = jax.nn.softmax(xf @ Wr.T + br, axis=-1)
        _, idx = jax.lax.top_k(prob, TOP_K)
        mask = jnp.zeros((n, N_BLOCKS), dtype=xf.dtype)
        mask = mask.at[jnp.arange(n)[:, None], idx].set(1.0)
        W1b = W1.reshape(N_BLOCKS, BLOCK_SIZE, in_f)
        h = jnp.einsum('nf,ibf->nib', xf, W1b)
        h = jax.nn.gelu(h, approximate=False) * mask[:, :, None]
        W2b = W2.reshape(in_f, N_BLOCKS, BLOCK_SIZE)
        y = jnp.einsum('nib,fib->nf', h, W2b)
        return y.reshape(x_shape)

    def _L1_attn_ref(x, Wq, Wk, Wv, Wo, Wg1, Wg2, norm_weight):
        import jax, jax.numpy as jnp
        import numpy as np
        EMBED = 256
        HEADS = 16
        HEAD_DIM = EMBED // HEADS
        CHUNK = 128
        BASE = 10000.0
        EPS = 1e-06

        def _alibi_log_decay(h):
            slopes = 2.0 ** (-8.0 * (jnp.arange(h, dtype=jnp.float32) + 1.0) / h)
            return -slopes

        def _lrpe_rotate(x):
            b, n, h, d = x.shape
            half = d // 2
            theta = BASE ** (-2.0 * jnp.arange(half, dtype=jnp.float32) / d)
            ang = jnp.arange(n, dtype=jnp.float32)[:, None] * theta[None, :]
            cos = jnp.cos(ang)[None, :, None, :]
            sin = jnp.sin(ang)[None, :, None, :]
            x1, x2 = (x[..., :half], x[..., half:])
            return jnp.concatenate([x1 * cos - x2 * sin, x1 * sin + x2 * cos], axis=-1)

        def _lightning_attn(q, k, v, log_lam):
            b, n, h, d = q.shape
            C = CHUNK
            nc = n // C
            qc = q.reshape(b, nc, C, h, d).transpose(1, 0, 2, 3, 4)
            kc = k.reshape(b, nc, C, h, d).transpose(1, 0, 2, 3, 4)
            vc = v.reshape(b, nc, C, h, d).transpose(1, 0, 2, 3, 4)
            i = jnp.arange(C, dtype=jnp.float32)
            diff = i[:, None] - i[None, :]
            D = jnp.where(diff[None] >= 0, jnp.exp(log_lam[:, None, None] * diff[None]), 0.0)
            decay_q = jnp.exp(log_lam[None, :] * (i[:, None] + 1.0))
            decay_k = jnp.exp(log_lam[None, :] * (C - 1.0 - i[:, None]))
            lam_C = jnp.exp(log_lam * C)

            def step(S, qkv):
                qi, ki, vi = qkv
                scores = jnp.einsum('bthd,bshd->bhts', qi, ki) * D[None]
                o_intra = jnp.einsum('bhts,bshd->bthd', scores, vi)
                o_inter = jnp.einsum('bthd,bhde->bthe', qi * decay_q[None, :, :, None], S)
                S_new = lam_C[None, :, None, None] * S + jnp.einsum('bshd,bshe->bhde', ki * decay_k[None, :, :, None], vi)
                return (S_new, o_intra + o_inter)
            S0 = jnp.zeros((b, h, d, d), q.dtype)
            _, o = jax.lax.scan(step, S0, (qc, kc, vc))
            return o.transpose(1, 0, 2, 3, 4).reshape(b, n, h, d)

        def _gated_group_rmsnorm(o, gate, weight):
            b, n, d = o.shape
            x = o * jax.nn.sigmoid(gate)
            xg = x.reshape(b, n, HEADS, HEAD_DIM)
            ms = jnp.mean(xg * xg, axis=-1, keepdims=True)
            xg = xg * jax.lax.rsqrt(ms + EPS)
            return xg.reshape(b, n, d) * weight
        b, n, d = x.shape
        q = (x @ Wq).reshape(b, n, HEADS, HEAD_DIM)
        k = (x @ Wk).reshape(b, n, HEADS, HEAD_DIM)
        v = (x @ Wv).reshape(b, n, HEADS, HEAD_DIM)
        q = jax.nn.silu(q)
        k = jax.nn.silu(k)
        q = _lrpe_rotate(q)
        k = _lrpe_rotate(k)
        log_lam = _alibi_log_decay(HEADS)
        o = _lightning_attn(q, k, v, log_lam).reshape(b, n, d)
        gate = x @ Wg1 @ Wg2
        o = _gated_group_rmsnorm(o, gate, norm_weight)
        return o @ Wo

    def _L1_ffn_ref(x, gate_kernel, wi_0, wi_1, wo):
        import jax, jax.numpy as jnp
        import numpy as np
        TOP_K = 2
        E = gate_kernel.shape[-1]
        gate_logits = jnp.einsum('bsd,de->bse', x, gate_kernel)
        top_k_weights, top_k_indices = jax.lax.top_k(gate_logits, TOP_K)
        top_k_weights = jax.nn.softmax(top_k_weights.astype(jnp.float32), axis=-1).astype(x.dtype)
        combine_w = jnp.sum(jax.nn.one_hot(top_k_indices, E, dtype=x.dtype) * top_k_weights[..., None], axis=-2)
        h0 = jnp.einsum('bsd,edm->bsem', x, wi_0)
        h1 = jnp.einsum('bsd,edm->bsem', x, wi_1)
        h = jax.nn.silu(h0) * h1 * combine_w[..., None]
        out = jnp.einsum('bsem,emd->bsd', h, wo)
        return out
    x = L0_attn_x
    xn = _layernorm(x, axis=-1)
    x = x + _L0_attn_ref(xn, L0_attn_wq, L0_attn_bq, L0_attn_wk, L0_attn_bk, L0_attn_wv, L0_attn_bv, L0_attn_wo, L0_attn_bo) + _L0_ffn_ref(xn, L0_ffn_Wr, L0_ffn_br, L0_ffn_W1, L0_ffn_W2)
    xn = _layernorm(x, axis=-1)
    x = x + _L1_attn_ref(xn, L1_attn_Wq, L1_attn_Wk, L1_attn_Wv, L1_attn_Wo, L1_attn_Wg1, L1_attn_Wg2, L1_attn_norm_weight) + _L1_ffn_ref(xn, L1_ffn_gate_kernel, L1_ffn_wi_0, L1_ffn_wi_1, L1_ffn_wo)
    return x

_drawn_inputs = setup_inputs


def setup_inputs(seed=0):
    import zlib

    import numpy as np

    out = dict(_drawn_inputs(seed))
    spreads = {'L0_attn_bq': (0.0, 2.0),
     'L0_attn_bk': (0.0, 2.0),
     'L0_attn_bv': (0.0, 0.1),
     'L0_attn_bo': (0.0, 0.1),
     'L0_ffn_br': (0.0, 0.1),
     'L1_attn_norm_weight': (1.0, 0.2)}
    factors = {'L0_attn_wq': 8.0, 'L0_attn_wk': 8.0, 'L1_attn_Wg1': 8.0, 'L1_attn_Wg2': 8.0}
    for name, (base, spread) in spreads.items():
        noise = np.random.default_rng([zlib.crc32(name.encode()), seed]).standard_normal(out[name].shape)
        drawn = base * np.exp(spread * noise) if base else spread * noise
        out[name] = jnp.asarray(drawn.astype(out[name].dtype))
    for name, factor in factors.items():
        out[name] = (out[name] * factor).astype(out[name].dtype)
    return out
```

```python
from contextlib import ExitStack

import numpy as np

import concourse.bass as bass
from concourse import mybir

F32 = mybir.dt.float32
F32R = mybir.dt.float32r
BF16 = mybir.dt.bfloat16
I32 = mybir.dt.int32
ALU = mybir.AluOpType
ACT = mybir.ActivationFunctionType
AX = mybir.AxisListType

P = 128
B, T, D = 4, 256, 256
NJ = T // P
NC = D // P
H, G, HD = 16, 2, 16
HPG = H // G
NBLK, BS, TOPK = 16, 64, 4
FF = NBLK * BS
E, TOPE = 8, 2
NTOK = B * T
EPS_LN = 1e-5
EPS_RMS = 1e-6
LOW = -3.0e38
HIGH = 3.0e38
Q_PARTS = (0, 0, 0, 1, 1, 2)
K_PARTS = (0, 1, 2, 0, 1, 0)
NPART = len(Q_PARTS)
KS = NPART * HD
KM = KS + 2

GROUPS = [
    [("wq", NC, D), ("wqp", NC, D), ("wk", NC, P), ("wkp", NC, P), ("wvr", NC, G * HD + NBLK)],
    [("w1", NC, FF)],
    [("w2", FF // P, D), ("wo", NC, D)],
    [("wq1", NC, D), ("wk1", NC, D), ("wv1", NC, D), ("wg1", NC, P), ("gk", NC, E), ("wo1", NC, D)],
]
PLACE = {}
_at = 0
for _g in GROUPS:
    for _n, _r, _c in _g:
        PLACE[_n] = (_at, _r, _c)
        _at += _r * _c
NW = _at
SPAN = [(PLACE[g[0][0]][0], PLACE[g[-1][0]][0] + g[-1][1] * g[-1][2]) for g in GROUPS]
EW = 3 * NC * D


class Signals(dict):

    def __init__(self, nc, ctx):
        super().__init__()
        self.nc, self.ctx = nc, ctx

    def __missing__(self, name):
        self[name] = self.ctx.enter_context(self.nc.semaphore(name))
        return self[name]


def build(nc, A, out):
    with ExitStack() as ctx:
        S = Signals(nc, ctx)

        def sb(name, shape, dt=F32):
            return ctx.enter_context(nc.sbuf_tensor(name, shape, dt))

        bank = [ctx.enter_context(nc.psum_tensor(f"bank{i}", [P, 512], F32)) for i in range(8)]
        qk_dram = nc.dram_tensor("qk_scratch", [3, 3, P, T], BF16, kind="Internal").ap()
        nm_dram = nc.dram_tensor("nm_scratch", [2 * H, T], BF16, kind="Internal").ap()
        qk1_dram = nc.dram_tensor("qk1_scratch", [3, 4, P, T], BF16, kind="Internal").ap()

        w_hi, w_lo = sb("w_hi", [P, NW], F32R), sb("w_lo", [P, NW], F32R)
        arena = sb("arena", [P, NW])
        e_stage = sb("e_stage", [P, 2, EW])
        consts = {}
        for name, shape, dt in [
            ("ident_f", [P, P], F32), ("ident_b", [P, P], BF16), ("cos0", [P, T], F32),
            ("sin0", [P, T], F32), ("bqk", [P, 3], F32), ("bqkp", [P, 3], F32),
            ("cos1", [P, NJ, D], F32), ("sin1", [P, NJ, D], F32), ("decay", [P, H, P], F32),
            ("decay_q", [P, NC, P], F32), ("decay_k", [P, D], F32), ("blockdiag", [P, NC, P], F32),
            ("sel_blk", [NBLK, FF // P, P], BF16), ("sel_exp", [P, E, P], BF16),
            ("wg2", [HD, D], F32),
        ]:
            consts[name] = sb("c_" + name, shape, dt)
        bv_b = sb("bv_b", [P, G * HD])
        br_b = sb("br_b", [P, NBLK])
        bo_b = sb("bo_b", [P, D])
        nw_b = sb("nw_b", [P, D])
        ident_f, ident_b = consts["ident_f"], consts["ident_b"]

        x_all = sb("x_all", [P, B * NJ, D])
        t_hi_all = sb("t_hi_all", [P, NC, NTOK], F32R)
        t_lo_all = sb("t_lo_all", [P, NC, NTOK], F32R)
        cw_t = sb("cw_t", [P, NTOK], BF16)
        tick = sb("tick", [P, 1])
        stats = sb("stats", [P, NJ, 6])
        mv = sb("mv", [P, NJ, 2])
        rs = sb("rs", [P, 4, NJ * H])
        xn = sb("xn", [P, NJ, D])
        t_hi, t_lo = sb("t_hi", [P, NC * T], F32R), sb("t_lo", [P, NC * T], F32R)
        qk_sp = sb("qk_sp", [P, 3, 4 * T], BF16)
        q_hat = sb("q_hat", [P, H, T], BF16)
        k_hat = sb("k_hat", [P, G, T], BF16)
        k_hat1 = sb("k_hat1", [P, H, T], BF16)
        v_aug = sb("v_aug", [P, NJ, G, 2 * HD])
        lg = sb("lg", [P, NJ, NBLK + 8])
        top = sb("top", [P, NJ, 8])
        rep = sb("rep", [P, NJ, NBLK + 8])
        mask = sb("mask", [P, NJ, NBLK], BF16)
        mask_t = sb("mask_t", [NBLK, T], BF16)
        h_hi, h_lo = sb("h_hi", [P, 2, 512], F32R), sb("h_lo", [P, 2, 512], F32R)
        nm = sb("nm", [P, NJ, H])
        nm_sp = sb("nm_sp", [P, NJ, 2 * H], BF16)
        nm_t = sb("nm_t", [2 * H, T], BF16)
        rden = sb("rden", [P, NJ, H])
        v1 = sb("v1", [P, NJ, D + HD])
        g1_t = sb("g1_t", [HD, T])
        lg1 = sb("lg1", [P, NJ, 16])
        cw = sb("cw", [P, NJ, 4, E])
        cw_sp = sb("cw_sp", [P, NJ, 3 * E], BF16)
        ms = sb("ms", [P, NJ * H])

        def part(at, n):
            return arena[:, at:at + n]

        buf_a, buf_b, buf_c, buf_r = (part(1024 * i, 1024) for i in range(4))
        ring = [part(4096 + 512 * i, 512) for i in range(4)]
        osb = [part(6144 + 512 * i, 512) for i in range(2)]
        hg = [part(7168, 512), ring[0]]
        hm = [ring[1], ring[2]]
        cat = part(7680, 512)
        kd = part(8192, 256)
        assert 8448 <= NW
        e_s, e_p, e_m, cwb = ([part(1024 * i + 512 * k, 512) for k in range(2)] for i in range(4))
        qd, state = osb[0][:, 0:D], osb[0][:, D:2 * D]
        zeros = part(4096, 512)
        e_hi, e_lo = ([full[:, PLACE["w1"][0] + k * EW:PLACE["w1"][0] + (k + 1) * EW] for k in range(2)] for full in (w_hi, w_lo))

        def w(name, part_of, row, c0, c1):
            at, _, n = PLACE[name]
            return part_of[:, at + row * n + c0:at + row * n + c1]

        def mm3(pe, dst, lhs, rhs, first, last, lone_start=False):
            for i, (a, b) in enumerate(((0, 0), (0, 1), (1, 0))):
                ins = pe.matmul(dst, lhs[a], rhs[b], start=first and i == 0, stop=last and i == 2,
                                skip_group_check=True)
            return ins

        def wx(name, row, c0, c1):
            return w(name, w_hi, row, c0, c1), w(name, w_lo, row, c0, c1)

        def tx(c, j=None):
            a, b = (c * T, (c + 1) * T) if j is None else (c * T + j * P, c * T + (j + 1) * P)
            return t_hi[:, a:b], t_lo[:, a:b]

        block = ctx.enter_context(nc.Block())
        ex_dram = A["experts"]

        @block.sync
        def _(sp):
            sp.dma_start(x_all[:, 0:NJ, :], A["x"][0:NJ * P, :].rearrange("(j p) d -> p j d", p=P)).then_inc(S["x_in"], 16)
            sp.dma_start(x_all[:, NJ:, :], A["x"][NJ * P:, :].rearrange("(j p) d -> p j d", p=P)).then_inc(S["x_in"], 16)
            for g, group in enumerate(GROUPS):
                for name, rows, cols in group:
                    at = PLACE[name][0]
                    sp.dma_start(arena[:, at:at + rows * cols].rearrange("p (r n) -> p r n", r=rows),
                                 A[name].rearrange("(r p) n -> p r n", p=P)).then_inc(S[f"w_in{g}"], 16)
            for k in range(2):
                sp.dma_start(e_stage[:, k, :], ex_dram[k]).then_inc(S[f"e_in{k}"], 16)
            with sp.Fori(0, B) as b:
                it = b + 1
                sp.wait_ge(S["qk_sp"], it)
                for s in range(3):
                    sp.dma_start(qk_dram[s].rearrange("c p t -> p c t"),
                                 qk_sp[:, s, 0:3 * T].rearrange("p (c t) -> p c t", c=3)).then_inc(S["qk_out"], 16)
                sp.wait_ge(S["qk_out"], it * 48)
                for n in range(NPART):
                    sp.dma_start(k_hat[n * HD:(n + 1) * HD, :, :],
                                 qk_dram[K_PARTS[n], 2, 0:G * HD].rearrange("(g d) t -> d g t", d=HD)).then_inc(S["k_in"], 16)
                    sp.dma_start(q_hat[n * HD:(n + 1) * HD, :, :],
                                 qk_dram[Q_PARTS[n], 0:2].rearrange("c (h d) t -> d (c h) t", d=HD)).then_inc(S["q_in"], 16)
                sp.wait_ge(S["nm_t"], it)
                sp.dma_start(nm_dram, nm_t[:]).then_inc(S["nm_out"], 16)
                sp.wait_ge(S["nm_out"], it * 16)
                sp.dma_start(q_hat[KS:KM, :, :], nm_dram.rearrange("(s h) t -> s h t", s=2)).then_inc(S["nm_in"], 16)
                sp.wait_ge(S["qk1_sp"], it)
                sp.dma_start(qk1_dram.rearrange("s c p t -> p (s c) t"),
                             qk_sp[:, :, :].rearrange("p s (c t) -> p (s c) t", c=4)).then_inc(S["qk1_out"], 16)
                sp.wait_ge(S["qk1_out"], it * 16)
                for n in range(NPART):
                    sp.dma_start(k_hat1[n * HD:(n + 1) * HD, :, :],
                                 qk1_dram[K_PARTS[n], 2:4].rearrange("c (h d) t -> d (c h) t", d=HD)).then_inc(S["k1_in"], 16)
                    sp.dma_start(q_hat[n * HD:(n + 1) * HD, :, :],
                                 qk1_dram[Q_PARTS[n], 0:2].rearrange("c (h d) t -> d (c h) t", d=HD)).then_inc(S["q1_in"], 16)
            with sp.Fori(1, E // 2) as e2:
                for k in range(2):
                    sp.wait_ge(S[f"e_split{k}"], e2)
                    sp.dma_start(e_stage[:, k, :], ex_dram[e2 * 2 + k]).then_inc(S[f"e_in{k}"], 16)
            for i in range(B):
                sp.wait_ge(S["y"], i + 1)
                sp.dma_start(out[i * T:(i + 1) * T, :].rearrange("(j p) d -> p j d", p=P),
                             x_all[:, i * NJ:(i + 1) * NJ, :]).then_inc(S["stored"], 16)
            sp.wait_ge(S["stored"], 16 * B)

        @block.gpsimd
        def _(pool):
            for name in consts:
                pool.dma_start(consts[name][:], A["c_" + name]).then_inc(S["c_in"], 16)
            for dst, name in ((bv_b, "bv"), (br_b, "br"), (bo_b, "bo"), (nw_b, "nw")):
                pool.dma_start(dst[:], A[name].partition_broadcast(P)).then_inc(S["c_in"], 16)
            pool.memset(v_aug[:], 1.0).then_inc(S["ones"], 1)
            pool.memset(v1[:], 0.0).then_inc(S["ones"], 1)
            pool.memset(lg[:], LOW).then_inc(S["ones"], 1)
            pool.memset(lg1[:], LOW).then_inc(S["ones"], 1)
            pool.wait_ge(S["ones"], 4)
            pool.memset(k_hat[KS:P, :, :], 1.0).then_inc(S["ones"], 1)
            pool.wait_ge(S["ones"], 5)
            pool.memset(cw_t[:], 0.0).then_inc(S["ones"], 1)
            with pool.Fori(0, B) as b:
                it = b + 1
                pool.wait_ge(S["t1_lo"], it)
                pool.wait_ge(S["t1_hi"], it)
                pool.tensor_copy(t_hi_all[:, :, bass.ds(b * T, T)],
                                 t_hi[:].bitcast(F32).rearrange("p (c t) -> p c t", c=NC)).then_inc(S["t1_kept"], 1)
                pool.tensor_copy(t_lo_all[:, :, bass.ds(b * T, T)],
                                 t_lo[:].bitcast(F32).rearrange("p (c t) -> p c t", c=NC)).then_inc(S["t1_kept"], 1)
            with pool.Fori(0, E // 2) as e2:
                for k in range(2):
                    pool.wait_ge(S[f"e_hi{k}"], e2 + 1)
                    pool.tensor_tensor(out=e_lo[k], in0=e_stage[:, k, :], in1=e_hi[k].bitcast(F32), op=ALU.subtract).then_inc(S[f"e_split{k}"], 1)

        @block.tensor
        def _(pe):
            def transposes(dst, src, sem, ident=ident_f):
                for c in range(NC):
                    for j in range(NJ):
                        last = pe.transpose(dst[:, c * T + j * P:c * T + (j + 1) * P],
                                            src[:, j, c * P:(c + 1) * P], ident[:])
                last.then_inc(S[sem], 1)

            pe.wait_ge(S["c_in"], 16 * (len(consts) + 4))
            pe.wait_ge(S["ones"], 6)
            for g in range(len(GROUPS)):
                pe.wait_ge(S["w_hi"], g + 1)
                pe.wait_ge(S["w_lo"], g + 1)
            with pe.Fori(0, B) as b:
                it = b + 1
                pe.wait_ge(S["xn"], it)
                transposes(bank[0], xn, "t_ps")
                pe.wait_ge(S["t_hi"], it)
                pe.wait_ge(S["t_lo"], it)
                for name, dst, n, at in (("wq", bank[1], 2, 0), ("wqp", bank[2], 2, 0), ("wk", bank[3], 1, 0), ("wkp", bank[3], 1, T)):
                    for s in range(n):
                        for c in range(NC):
                            last = mm3(pe, dst[:, at + s * T:at + (s + 1) * T], wx(name, c, s * P, (s + 1) * P), tx(c), c == 0, c == NC - 1)
                last.then_inc(S["qk_ps"], 1)
                NV = G * HD + NBLK
                for j in range(NJ):
                    for c in range(NC):
                        last = mm3(pe, bank[4][:, j * NV:(j + 1) * NV], tx(c, j), wx("wvr", c, 0, NV), c == 0, c == NC - 1)
                last.then_inc(S["vr_ps"], 1)
                H_BANK, M_BANK = (bank[5], bank[6]), (bank[7], bank[0])
                out0 = bank[1]

                def ffn_out(i):
                    pe.wait_ge(S["h_hi"], b * 4 + (i + 1))
                    pe.wait_ge(S["h_lo"], b * 4 + (i + 1))
                    if i == 0:
                        pe.wait_ge(S["rope"], it)
                    for j in range(NJ):
                        for m in range(2):
                            at = m * T + j * P
                            last = mm3(pe, out0[:, j * D:(j + 1) * D],
                                       (h_hi[:, i % 2, at:at + P], h_lo[:, i % 2, at:at + P]),
                                       wx("w2", 2 * i + m, 0, D), i == 0 and j == 0 and m == 0, False)
                    last.then_inc(S["ffn_out"], 1)

                for i in range(4):
                    if i == 0:
                        pe.wait_ge(S["mask"], it)
                        mt = bank[6][:].bitcast(BF16)
                        for j in range(NJ):
                            last = pe.transpose(mt[0:NBLK, j * P:(j + 1) * P], mask[:, j, :], ident_b[:])
                        last.then_inc(S["mask_ps"], 1)
                        pe.wait_ge(S["mask_t"], it)
                    if i >= 2:
                        pe.wait_ge(S["hm"], b * 4 + (i - 1))
                    for m in range(2):
                        for c in range(NC):
                            last = mm3(pe, H_BANK[i % 2][:, m * T:(m + 1) * T],
                                       wx("w1", c, (2 * i + m) * P, (2 * i + m + 1) * P), tx(c), c == 0, c == NC - 1)
                    last.then_inc(S["h_ps"], 1)
                    for m in range(2):
                        last = pe.matmul(M_BANK[i % 2][:, m * T:(m + 1) * T], consts["sel_blk"][:, 2 * i + m, :], mask_t[:, :],
                                         start=True, stop=True)
                    last.then_inc(S["m_ps"], 1)
                    if i >= 1:
                        ffn_out(i - 1)
                ffn_out(3)
                SC = (bank[2], bank[3], bank[6], bank[7])
                pe.wait_ge(S["q_in"], it * (16 * NPART))
                pe.wait_ge(S["k_in"], it * (16 * NPART))
                for h in range(H):
                    if h >= 4:
                        pe.wait_ge(S["max"], b * H + (h - 3))
                    for j in range(NJ):
                        last = pe.matmul(SC[h % 4][:, j * T:(j + 1) * T], q_hat[0:KS, h, j * P:(j + 1) * P],
                                         k_hat[0:KS, h // HPG, :], start=True, stop=True)
                    last.then_inc(S["s_ps"], 1)
                pe.wait_ge(S["nm_sp"], it)
                nt = bank[4][:].bitcast(BF16)
                for j in range(NJ):
                    last = pe.transpose(nt[0:2 * H, j * P:(j + 1) * P], nm_sp[:, j, :], ident_b[:])
                last.then_inc(S["nm_ps"], 1)
                O_BANK = (bank[5], bank[0])
                pe.wait_ge(S["nm_in"], it * 16)

                def probs_v(n):
                    u, kt = divmod(n, NJ)
                    g, quarter = divmod(u, 4)
                    pe.wait_ge(S["probs"], b * 16 + (n + 1))
                    pe.matmul(O_BANK[g][32 * quarter:32 * quarter + 32, :], v_aug[:, kt, g, :], ring[n % 4],
                              start=kt == 0, stop=kt == NJ - 1).then_inc(S["pv"], 1)

                for n in range(16):
                    u, kt = divmod(n, NJ)
                    g, quarter = divmod(u, 4)
                    if n >= 4:
                        pe.wait_ge(S["probs"], b * 16 + (n - 3))
                    pe.matmul(SC[n % 4][:, :], k_hat[0:KM, g, kt * P:(kt + 1) * P],
                              q_hat[0:KM, g * HPG + 2 * quarter:g * HPG + 2 * quarter + 2, :],
                              start=True, stop=True).then_inc(S["st_ps"], 1)
                    if n >= 3:
                        probs_v(n - 3)
                for n in range(13, 16):
                    probs_v(n)
                for g in range(G):
                    pe.wait_ge(S["osb"], b * G + (g + 1))
                    for h2 in range(2):
                        for j in range(NJ):
                            at = (g * 2 + h2) * P
                            last = pe.transpose(bank[2 + j][:, at:at + P], osb[g][:, h2 * T + j * P:h2 * T + (j + 1) * P], ident_f[:])
                last.then_inc(S["ot_ps"], 1)
                pe.wait_ge(S["cat"], it)
                transposes(bank[4], cat.rearrange("p (j d) -> p j d", j=NJ), "ct_ps")
                pe.wait_ge(S["c_hi"], it)
                pe.wait_ge(S["c_lo"], it)
                for j in range(NJ):
                    for c in range(NC):
                        last = mm3(pe, out0[:, j * D:(j + 1) * D], tx(c, j), wx("wo", c, 0, D), False, c == NC - 1)
                last.then_inc(S["out0"], 1)

                pe.wait_ge(S["xn1"], it)
                transposes(bank[0], xn, "t1_ps")
                pe.wait_ge(S["t1_hi"], it)
                pe.wait_ge(S["t1_lo"], it)
                for name, dst in (("wq1", bank[1]), ("wk1", bank[2]), ("wv1", bank[3])):
                    for j in range(NJ):
                        for c in range(NC):
                            last = mm3(pe, dst[:, j * D:(j + 1) * D], tx(c, j), wx(name, c, 0, D), c == 0, c == NC - 1)
                    last.then_inc(S[name + "_ps"], 1)
                for j in range(NJ):
                    for c in range(NC):
                        last = mm3(pe, bank[4][:, j * E:(j + 1) * E], tx(c, j), wx("gk", c, 0, E), c == 0, c == NC - 1)
                last.then_inc(S["lg1_ps"], 1)
                for c in range(NC):
                    last = mm3(pe, bank[5][:, 0:T], wx("wg1", c, 0, P), tx(c), c == 0, c == NC - 1)
                last.then_inc(S["g1_ps"], 1)
                pe.wait_ge(S["g1_t"], it)
                for j in range(NJ):
                    last = pe.matmul(bank[6][:, j * D:(j + 1) * D], g1_t[:, j * P:(j + 1) * P], consts["wg2"][:, :], start=True, stop=True)
                last.then_inc(S["gate_ps"], 1)
                pe.wait_ge(S["rot"], it)
                rot = buf_c.rearrange("p (q j d) -> p q j d", q=2, j=NJ)
                transposes(bank[0], rot[:, 0], "qt_ps")
                transposes(bank[7], rot[:, 1], "kt_ps")
                pe.wait_ge(S["cw_sp"], it)
                ct = bank[4][:].bitcast(BF16)
                for j in range(NJ):
                    last = pe.transpose(ct[0:3 * E, j * P:(j + 1) * P], cw_sp[:, j, :], ident_b[:])
                last.then_inc(S["cwt_ps"], 1)
                pe.wait_ge(S["kd"], it)
                pe.wait_ge(S["v1"], it)
                for c in range(NC):
                    last = pe.matmul(bank[5][:, c * P:(c + 1) * P], kd[:, c * P:(c + 1) * P], v1[:, 0, c * P:(c + 1) * P], start=True, stop=True)
                last.then_inc(S["kv_ps"], 1)
                pe.wait_ge(S["state"], it)
                pe.wait_ge(S["qd"], it)
                for c in range(NC):
                    last = pe.matmul(bank[5][:, (2 + c) * P:(3 + c) * P], qd[:, c * P:(c + 1) * P], state[:, c * P:(c + 1) * P], start=True, stop=True)
                last.then_inc(S["inter_ps"], 1)
                SC1 = (bank[1], bank[2], bank[3], bank[6])
                OI = (bank[0], bank[7])
                pe.wait_ge(S["q1_in"], it * (16 * NPART))
                pe.wait_ge(S["k1_in"], it * (16 * NPART))
                pe.wait_ge(S["tg"], it)

                def intra(n):
                    j, four = divmod(n, 4)
                    pe.wait_ge(S["sc"], b * 8 + (n + 1))
                    for i in range(4):
                        h = four * 4 + i
                        last = pe.matmul(OI[j][32 * i:32 * i + 32, four * P:(four + 1) * P], v1[:, j, h * HD:h * HD + 2 * HD],
                                         ring[n % 4][:, i * P:(i + 1) * P], start=True, stop=True, skip_group_check=True)
                    last.then_inc(S["oi"], 1)

                for n in range(8):
                    j, four = divmod(n, 4)
                    if n >= 4:
                        pe.wait_ge(S["sc"], b * 8 + (n - 3))
                    for i in range(4):
                        h = four * 4 + i
                        last = pe.matmul(SC1[n % 4][:, i * P:(i + 1) * P], k_hat1[0:KS, h, j * P:(j + 1) * P],
                                         q_hat[0:KS, h, j * P:(j + 1) * P], start=True, stop=True)
                    last.then_inc(S["s1_ps"], 1)
                    if n >= 2:
                        intra(n - 2)
                intra(6)
                intra(7)
                for j in range(NJ):
                    pe.wait_ge(S["oisb"], b * NJ + (j + 1))
                    for four in range(4):
                        last = pe.transpose(bank[1 + j][:, four * P:(four + 1) * P], osb[j][:, four * P:(four + 1) * P], ident_f[:])
                last.then_inc(S["oit_ps"], 1)
                pe.wait_ge(S["og"], it)
                transposes(bank[3], cat.rearrange("p (j d) -> p j d", j=NJ), "gt_ps")
                pe.wait_ge(S["g_hi"], it)
                pe.wait_ge(S["g_lo"], it)
                for j in range(NJ):
                    for c in range(NC):
                        last = mm3(pe, bank[4][:, j * D:(j + 1) * D], tx(c, j), wx("wo1", c, 0, D), c == 0, c == NC - 1)
                last.then_inc(S["out1"], 1)

            pe.wait_ge(S["zeros"], 1)
            acc = (bank[4], bank[5], bank[6], bank[7])
            for _ in range(2):
                for a in acc:
                    pe.matmul(a[:, :], zeros[0:1, 0:P], zeros[0:1, :], start=True, stop=False,
                              skip_group_check=True).then_inc(S["e_out"], 1)

            def sel_of(e):
                return consts["sel_exp"][:, bass.ds(e, 1), :].rearrange("p o n -> p (o n)")

            def two_experts(e2):
                def ew(k, which, row, c0, c1):
                    o = which * NC * D + row * D
                    return e_hi[k][:, o + c0:o + c1], e_lo[k][:, o + c0:o + c1]

                def expert_out(u):
                    k, n, m = u // 4, u // 2 % 2, u % 2
                    pe.wait_ge(S["eh_hi"], e2 * 8 + (u + 1))
                    pe.wait_ge(S["eh_lo"], e2 * 8 + (u + 1))
                    for t in range(4):
                        tile = n * 4 + t
                        last = mm3(pe, acc[tile // 2][:, (tile % 2) * D:(tile % 2 + 1) * D],
                                   (h_hi[:, u % 2, t * P:(t + 1) * P], h_lo[:, u % 2, t * P:(t + 1) * P]),
                                   ew(k, 2, m, 0, D), False, False)
                    last.then_inc(S["e_out"], 1)

                for u in range(8):
                    k, n, m = u // 4, u // 2 % 2, u % 2
                    cols = slice(n * 512, (n + 1) * 512)
                    if u % 4 == 0:
                        pe.wait_ge(S[f"e_split{k}"], e2 + 1)
                    if m == 0:
                        pe.matmul(bank[3][:, :], sel_of(e2 * 2 + k),
                                  cw_t[:, cols], start=True, stop=True).then_inc(S["cwb_ps"], 1)
                    for c in range(NC):
                        last = mm3(pe, bank[2 * (u % 2)][:, :], ew(k, 0, c, m * P, (m + 1) * P),
                                   (t_hi_all[:, c, cols], t_lo_all[:, c, cols]), c == 0, c == NC - 1)
                    last.then_inc(S["h0_ps"], 1)
                    if u >= 1:
                        pe.wait_ge(S["e_t"], e2 * 8 + u)
                    for c in range(NC):
                        last = mm3(pe, bank[1][:, :], ew(k, 1, c, m * P, (m + 1) * P),
                                   (t_hi_all[:, c, cols], t_lo_all[:, c, cols]), c == 0, c == NC - 1)
                    last.then_inc(S["h1_ps"], 1)
                    if u >= 1:
                        expert_out(u - 1)
                expert_out(7)

            with pe.Fori(0, E // 2 - 1) as e2:
                two_experts(e2)
            two_experts(E // 2 - 1)

        @block.scalar
        def _(act):
            cp = ACT.Copy
            for g, (a, z) in enumerate(SPAN):
                act.wait_ge(S[f"w_in{g}"], 16 * len(GROUPS[g]))
                act.activation(w_hi[:, a:z], arena[:, a:z], cp).then_inc(S["w_hi"], 1)
            with act.Fori(0, B) as b:
                it = b + 1
                act.wait_ge(S["t_ps"], it)
                act.activation(t_hi[:], bank[0][:], cp).then_inc(S["t_hi"], 1)
                act.wait_ge(S["mask_ps"], it)
                act.activation(mask_t[:], bank[6][:].bitcast(BF16)[0:NBLK, 0:T], cp).then_inc(S["mask_t"], 1)
                for i in range(4):
                    act.wait_ge(S["h_ps"], b * 4 + (i + 1))
                    if i >= 2:
                        act.wait_ge(S["hm"], b * 4 + (i - 1))
                    act.activation(hg[i % 2], (bank[5], bank[6])[i % 2][:], ACT.Gelu).then_inc(S["hg"], 1)
                    act.wait_ge(S["hm"], b * 4 + (i + 1))
                    if i >= 2:
                        act.wait_ge(S["ffn_out"], b * 4 + (i - 1))
                    act.activation(h_hi[:, i % 2, :], hm[i % 2], cp).then_inc(S["h_hi"], 1)
                act.wait_ge(S["nm_ps"], it)
                act.activation(nm_t[:], bank[4][:].bitcast(BF16)[0:2 * H, 0:T], cp).then_inc(S["nm_t"], 1)
                SC = (bank[2], bank[3], bank[6], bank[7])
                for n in range(16):
                    act.wait_ge(S["st_ps"], b * 16 + (n + 1))
                    if n >= 4:
                        act.wait_ge(S["pv"], b * 16 + (n - 3))
                    act.activation(ring[n % 4], SC[n % 4][:], ACT.Exp, scale=1.0 / HD).then_inc(S["probs"], 1)
                for g in range(G):
                    act.wait_ge(S["pv"], b * 16 + 8 * (g + 1))
                    act.activation(osb[g], (bank[5], bank[0])[g][:], cp).then_inc(S["osb"], 1)
                act.wait_ge(S["ct_ps"], it)
                act.activation(t_hi[:], bank[4][:], cp).then_inc(S["c_hi"], 1)
                act.wait_ge(S["t1_ps"], it)
                act.activation(t_hi[:], bank[0][:], cp).then_inc(S["t1_hi"], 1)
                act.wait_ge(S["wq1_ps"], it)
                act.activation(buf_a[:, 0:512], bank[1][:], ACT.Silu).then_inc(S["silu"], 1)
                act.wait_ge(S["wk1_ps"], it)
                act.activation(buf_a[:, 512:1024], bank[2][:], ACT.Silu).then_inc(S["silu"], 1)
                act.wait_ge(S["g1_ps"], it)
                act.activation(g1_t[:], bank[5][0:HD, 0:T], cp).then_inc(S["g1_t"], 1)
                act.activation(v1[:, :, 0:D], bank[3][:].rearrange("p (j d) -> p j d", j=NJ), cp).then_inc(S["v1"], 1)
                act.wait_ge(S["cw_d"], it)
                act.activation(cw[:, :, 1, :], cw[:, :, 0, :], ACT.Tanh, scale=0.5).then_inc(S["cw_tanh"], 1)
                act.wait_ge(S["gate_ps"], it)
                act.activation(hg[0], bank[6][:], ACT.Tanh, scale=0.5).then_inc(S["tg"], 1)
                act.wait_ge(S["cwt_ps"], it)
                act.activation(cw_t[0:3 * E, bass.ds(b * T, T)], bank[4][:].bitcast(BF16)[0:3 * E, 0:T], cp).then_inc(S["cw_t"], 1)
                act.wait_ge(S["inter_ps"], it)
                act.activation(buf_b[:, 0:D], bank[5][:, D:2 * D], cp).then_inc(S["inter"], 1)
                for j in range(NJ):
                    act.wait_ge(S["oi"], b * 8 + 4 * (j + 1))
                    act.activation(osb[j], (bank[0], bank[7])[j][:], cp).then_inc(S["oisb"], 1)
                act.wait_ge(S["gt_ps"], it)
                act.wait_ge(S["t1_kept"], it * 2)
                act.activation(t_hi[:], bank[3][:], cp).then_inc(S["g_hi"], 1)
            def high_part(k, pair):
                act.wait_ge(S[f"e_in{k}"], (pair + 1) * 16)
                act.activation(e_hi[k], e_stage[:, k, :], cp).then_inc(S[f"e_hi{k}"], 1)

            def two_experts(e2, more):
                for u in range(8):
                    act.wait_ge(S["h0_ps"], e2 * 8 + (u + 1))
                    act.activation(e_s[u % 2], (bank[0], bank[2])[u % 2][:], ACT.Silu).then_inc(S["e_s"], 1)
                    if u % 2 == 0:
                        act.activation(cwb[(u // 2) % 2], bank[3][:], cp).then_inc(S["cwb"], 1)
                    act.wait_ge(S["e_m"], e2 * 8 + (u + 1))
                    act.wait_ge(S["e_out"], e2 * 8 + (u + 7))
                    act.activation(h_hi[:, u % 2, :], e_m[u % 2], cp).then_inc(S["eh_hi"], 1)
                    if u == 1:
                        high_part(1, e2)
                    if u == 5 and more:
                        high_part(0, e2 + 1)

            act.wait_ge(S["ffn_out"], 4 * B)
            high_part(0, 0)
            with act.Fori(0, E // 2 - 1) as e2:
                two_experts(e2, True)
            two_experts(E // 2 - 1, False)

        @block.vector
        def _(dve):
            tt, ts, stt = dve.tensor_tensor, dve.tensor_scalar, dve.scalar_tensor_tensor

            def hold():
                dve.memset(tick[:], 0.0)

            def rsqrt(var, n, eps, it, name):
                v, y, t, r = (rs[:, i, 0:n] for i in range(4))
                q = S[name]
                k = 0

                def nxt():
                    dve.wait_ge(q, it * 13 + (k - 13))

                ts(v, var, eps, None, ALU.add).then_inc(q, 1); k = 1; nxt()
                ts(y.bitcast(I32), v.bitcast(I32), 1, None, ALU.logical_shift_right).then_inc(q, 1); k = 2; nxt()
                ts(r.bitcast(I32), y.bitcast(I32), -1.0, float(0x5F3759DF), ALU.mult, ALU.add).then_inc(q, 1); k = 3; nxt()
                ts(v, v, -0.5, None, ALU.mult).then_inc(q, 1); k = 4; nxt()
                for _ in range(3):
                    tt(t, r, r, ALU.mult).then_inc(q, 1); k += 1; nxt()
                    tt(t, t, v, ALU.mult).then_inc(q, 1); k += 1; nxt()
                    stt(r, t, 1.5, r, ALU.add, ALU.mult).then_inc(q, 1); k += 1; nxt()
                return r

            def layernorm(b, it, done):
                hold()
                for j in range(NJ):
                    dve.bn_stats(stats[:, j, :], x_all[:, bass.ds(b * NJ + j, 1), :].rearrange("p o d -> p (o d)")).then_inc(S[done + "_stats"], 1)
                dve.wait_ge(S[done + "_stats"], it * NJ)
                hold()
                for j in range(NJ):
                    last = dve.bn_aggr(mv[:, j, :], stats[:, j, :])
                last.then_inc(S[done + "_mv"], 1)
                dve.wait_ge(S[done + "_mv"], it)
                r = rsqrt(mv[:, :, 1], NJ, EPS_LN, it, done + "_rs")
                for j in range(NJ):
                    last = ts(xn[:, j, :], x_all[:, bass.ds(b * NJ + j, 1), :].rearrange("p o d -> p (o d)"),
                              mv[:, j, 0:1], r[:, j:j + 1], ALU.subtract, ALU.mult)
                last.then_inc(S[done], 1)

            def low_part(src, ps, sem, dep, it):
                dve.wait_ge(S[dep], it)
                tt(t_lo[:], ps, t_hi[:].bitcast(F32), ALU.subtract).then_inc(S[sem], 1)

            def bf16_parts(src, n, sem, it):
                q = S[sem + "_step"]
                dve.tensor_copy(qk_sp[:, 0, 0:n], src).then_inc(q, 1)
                dve.wait_ge(q, it * 3 - 2)
                tt(buf_r[:, 0:n], src, qk_sp[:, 0, 0:n], ALU.subtract).then_inc(q, 1)
                dve.wait_ge(q, it * 3 - 1)
                dve.tensor_copy(qk_sp[:, 1, 0:n], buf_r[:, 0:n]).then_inc(q, 1)
                dve.wait_ge(q, it * 3)
                tt(qk_sp[:, 2, 0:n], buf_r[:, 0:n], qk_sp[:, 1, 0:n], ALU.subtract).then_inc(S[sem], 1)

            for g, (a, z) in enumerate(SPAN):
                dve.wait_ge(S["w_hi"], g + 1)
                tt(w_lo[:, a:z], arena[:, a:z], w_hi[:, a:z].bitcast(F32), ALU.subtract).then_inc(S["w_lo"], 1)
            dve.wait_ge(S["w_lo"], len(GROUPS))
            dve.wait_ge(S["c_in"], 16 * (len(consts) + 4))
            dve.wait_ge(S["ones"], 6)
            dve.wait_ge(S["x_in"], 32)
            with dve.Fori(0, B) as b:
                it = b + 1
                layernorm(b, it, "xn")
                low_part(None, bank[0][:], "t_lo", "t_hi", it)
                dve.wait_ge(S["qk_ps"], it)
                src = (bank[1][:, 0:T], bank[1][:, T:2 * T], bank[3][:, 0:T])
                srcp = (bank[2][:, 0:T], bank[2][:, T:2 * T], bank[3][:, T:2 * T])
                for s in range(3):
                    stt(buf_a[:, s * T:(s + 1) * T], src[s], consts["bqk"][:, s:s + 1], consts["cos0"][:], ALU.add, ALU.mult)
                    last = stt(buf_b[:, s * T:(s + 1) * T], srcp[s], consts["bqkp"][:, s:s + 1], consts["sin0"][:], ALU.add, ALU.mult)
                last.then_inc(S["rope"], 1)
                dve.wait_ge(S["rope"], it)
                tt(buf_c[:, 0:3 * T], buf_a[:, 0:3 * T], buf_b[:, 0:3 * T], ALU.add).then_inc(S["roped"], 1)
                dve.wait_ge(S["roped"], it)
                bf16_parts(buf_c[:, 0:3 * T], 3 * T, "qk_sp", it)
                dve.wait_ge(S["vr_ps"], it)
                NV = G * HD + NBLK
                vr = bank[4][:, 0:NJ * NV].rearrange("p (j n) -> p j n", j=NJ)
                for j in range(NJ):
                    tt(v_aug[:, j, :, 0:HD], vr[:, j, 0:G * HD].rearrange("p (g d) -> p g d", g=G),
                       bv_b[:].rearrange("p (g d) -> p g d", g=G), ALU.add)
                    last = tt(lg[:, j, 0:NBLK], vr[:, j, G * HD:NV], br_b[:], ALU.add)
                last.then_inc(S["lg"], 1)
                dve.wait_ge(S["lg"], it)
                hold()
                for j in range(NJ):
                    last = dve.max(top[:, j, :], lg[:, j, 0:NBLK])
                last.then_inc(S["top"], 1)
                dve.wait_ge(S["top"], it)
                dve.memset(top[:, :, TOPK:8], LOW).then_inc(S["top4"], 1)
                dve.wait_ge(S["top4"], it)
                hold()
                for j in range(NJ):
                    last = dve.match_replace(rep[:, j, :], top[:, j, :], lg[:, j, :], HIGH)
                last.then_inc(S["rep"], 1)
                dve.wait_ge(S["rep"], it)
                tt(mask[:], rep[:, :, 0:NBLK], lg[:, :, 0:NBLK], ALU.is_gt).then_inc(S["mask"], 1)
                for i in range(4):
                    dve.wait_ge(S["m_ps"], b * 4 + (i + 1))
                    dve.wait_ge(S["hg"], b * 4 + (i + 1))
                    if i >= 2:
                        dve.wait_ge(S["h_hi"], b * 4 + (i - 1))
                    tt(hm[i % 2], (bank[7], bank[0])[i % 2][:], hg[i % 2], ALU.mult).then_inc(S["hm"], 1)
                    dve.wait_ge(S["h_hi"], b * 4 + (i + 1))
                    tt(h_lo[:, i % 2, :], hm[i % 2], h_hi[:, i % 2, :].bitcast(F32), ALU.subtract).then_inc(S["h_lo"], 1)
                SC = (bank[2], bank[3], bank[6], bank[7])
                for h in range(H):
                    dve.wait_ge(S["s_ps"], b * H + (h + 1))
                    dve.tensor_reduce(nm[:, :, h:h + 1], SC[h % 4][:].rearrange("p (j t) -> p j t", j=NJ), AX.X, ALU.max).then_inc(S["max"], 1)
                dve.wait_ge(S["max"], it * H)
                ts(nm_sp[:, :, 0:H], nm[:], -1.0, None, ALU.mult).then_inc(S["nm_hi"], 1)
                dve.wait_ge(S["nm_hi"], it)
                stt(nm_sp[:, :, H:2 * H], nm[:], -1.0, nm_sp[:, :, 0:H], ALU.mult, ALU.subtract).then_inc(S["nm_sp"], 1)
                dve.wait_ge(S["ot_ps"], it)
                for j in range(NJ):
                    o = bank[2 + j][:].rearrange("p (g h q e) -> p g h q e", g=G, h=2, q=4)
                    last = dve.reciprocal(rden[:, j, :].rearrange("p (g h q) -> p g h q", g=G, h=2), o[:, :, :, :, HD])
                last.then_inc(S["rden"], 1)
                dve.wait_ge(S["rden"], it)
                for j in range(NJ):
                    o = bank[2 + j][:].rearrange("p (g h q e) -> p g h q e", g=G, h=2, q=4)
                    r = rden[:, j, :].rearrange("p (g h q) -> p g h q", g=G, h=2)
                    dst = cat[:, j * D:(j + 1) * D].rearrange("p (g q h d) -> p g h q d", g=G, q=4, h=2)
                    for g in range(G):
                        last = tt(dst[:, g], o[:, g, :, :, 0:HD], r[:, g].unsqueeze(3).to_broadcast([P, 2, 4, HD]), ALU.mult)
                last.then_inc(S["cat"], 1)
                x_b = x_all[:, bass.ds(b * NJ, NJ), :]
                for j in range(NJ):
                    x_j = x_all[:, bass.ds(b * NJ + j, 1), :].rearrange("p o d -> p (o d)")
                    tt(x_j, x_j, bo_b[:], ALU.add).then_inc(S["x_bo"], 1)
                low_part(None, bank[4][:], "c_lo", "c_hi", it)
                dve.wait_ge(S["x_bo"], it * NJ)
                dve.wait_ge(S["out0"], it)
                tt(x_b, bank[1][:].rearrange("p (j d) -> p j d", j=NJ), x_b, ALU.add).then_inc(S["x1"], 1)
                dve.wait_ge(S["x1"], it)

                layernorm(b, it, "xn1")
                low_part(None, bank[0][:], "t1_lo", "t1_hi", it)
                dve.wait_ge(S["silu"], it * 2)
                for q in range(2):
                    s = buf_a[:, q * 512:(q + 1) * 512]
                    tt(buf_c[:, q * 512:(q + 1) * 512], s, consts["cos1"][:].rearrange("p j d -> p (j d)"), ALU.mult)
                    sv = s.rearrange("p (h s d) -> p h s d", s=2, d=HD // 2)
                    uv = buf_b[:, q * 512:(q + 1) * 512].rearrange("p (h s d) -> p h s d", s=2, d=HD // 2)
                    nv = consts["sin1"][:].rearrange("p j (h s d) -> p (j h) s d", s=2, d=HD // 2)
                    for half in range(2):
                        last = tt(uv[:, :, half, :], sv[:, :, 1 - half, :], nv[:, :, half, :], ALU.mult)
                last.then_inc(S["rot_uv"], 1)
                dve.wait_ge(S["rot_uv"], it)
                tt(buf_c, buf_c, buf_b, ALU.add).then_inc(S["rot"], 1)
                dve.wait_ge(S["rot"], it)
                tt(kd, buf_c[:, 512:512 + D], consts["decay_k"][:], ALU.mult).then_inc(S["kd"], 1)
                dve.wait_ge(S["lg1_ps"], it)
                dve.tensor_copy(lg1[:, :, 0:E], bank[4][:, 0:NJ * E].rearrange("p (j e) -> p j e", j=NJ)).then_inc(S["lg1"], 1)
                dve.wait_ge(S["lg1"], it)
                hold()
                for j in range(NJ):
                    last = dve.max(top[:, j, :], lg1[:, j, 0:E])
                last.then_inc(S["top_e"], 1)
                dve.wait_ge(S["top_e"], it)
                tt(cw[:, :, 2, 0:1], top[:, :, 0:1], top[:, :, 1:2], ALU.add).then_inc(S["top_sum"], 1)
                dve.wait_ge(S["top_sum"], it)
                dve.memset(top[:, :, TOPE:8], LOW).then_inc(S["top2"], 1)
                dve.wait_ge(S["top2"], it)
                hold()
                for j in range(NJ):
                    dve.match_replace(rep[:, j, 0:16], top[:, j, :], lg1[:, j, :], HIGH)
                    last = ts(cw[:, j, 0, :], lg1[:, j, 0:E], 2.0, cw[:, j, 2, 0:1], ALU.mult, ALU.subtract)
                last.then_inc(S["cw_d"], 1)
                dve.wait_ge(S["cw_d"], it)
                tt(cw[:, :, 2, :], rep[:, :, 0:E], lg1[:, :, 0:E], ALU.is_gt).then_inc(S["cw_sel"], 1)
                dve.wait_ge(S["cw_tanh"], it)
                ts(cw[:, :, 3, :], cw[:, :, 1, :], 0.5, 0.5, ALU.mult, ALU.add).then_inc(S["cw_sig"], 1)
                dve.wait_ge(S["cw_sig"], it)
                tt(cw[:, :, 0, :], cw[:, :, 3, :], cw[:, :, 2, :], ALU.mult).then_inc(S["cw"], 1)
                dve.wait_ge(S["cw"], it)
                dve.tensor_copy(cw_sp[:, :, 0:E], cw[:, :, 0, :]).then_inc(S["cw_h"], 1)
                dve.wait_ge(S["cw_h"], it)
                tt(cw[:, :, 1, :], cw[:, :, 0, :], cw_sp[:, :, 0:E], ALU.subtract).then_inc(S["cw_r"], 1)
                dve.wait_ge(S["cw_r"], it)
                dve.tensor_copy(cw_sp[:, :, E:2 * E], cw[:, :, 1, :]).then_inc(S["cw_m"], 1)
                dve.wait_ge(S["cw_m"], it)
                tt(cw_sp[:, :, 2 * E:3 * E], cw[:, :, 1, :], cw_sp[:, :, E:2 * E], ALU.subtract).then_inc(S["cw_sp"], 1)
                dve.wait_ge(S["qt_ps"], it)
                dve.tensor_copy(buf_a[:, 0:512], bank[0][:]).then_inc(S["qt"], 1)
                dve.wait_ge(S["kt_ps"], it)
                dve.tensor_copy(buf_a[:, 512:1024], bank[7][:]).then_inc(S["qt"], 1)
                dve.wait_ge(S["qt"], it * 2)
                bf16_parts(buf_a, 1024, "qk1_sp", it)
                tt(qd.rearrange("p (c t) -> p c t", c=NC), buf_a[:, 0:512].rearrange("p (c t) -> p c t", c=NC)[:, :, P:T],
                   consts["decay_q"][:], ALU.mult).then_inc(S["qd"], 1)
                dve.wait_ge(S["kv_ps"], it)
                tt(state.rearrange("p (c t) -> p c t", c=NC), bank[5][:, 0:D].rearrange("p (c t) -> p c t", c=NC), consts["blockdiag"][:], ALU.mult).then_inc(S["state"], 1)
                SC1 = (bank[1], bank[2], bank[3], bank[6])
                for n in range(8):
                    four = n % 4
                    dve.wait_ge(S["s1_ps"], b * 8 + (n + 1))
                    if n >= 4:
                        dve.wait_ge(S["oi"], b * 8 + (n - 3))
                    tt(ring[n % 4].rearrange("p (h t) -> p h t", h=4), SC1[n % 4][:].rearrange("p (h t) -> p h t", h=4),
                       consts["decay"][:, four * 4:(four + 1) * 4, :], ALU.mult).then_inc(S["sc"], 1)
                dve.wait_ge(S["tg"], it)
                ts(buf_c[:, 0:512], hg[0], 0.5, 0.5, ALU.mult, ALU.add).then_inc(S["gate"], 1)
                dve.wait_ge(S["oit_ps"], it)
                for j in range(NJ):
                    o = bank[1 + j][:].rearrange("p (h e) -> p h e", h=H)
                    last = dve.tensor_copy(buf_a[:, j * D:(j + 1) * D].rearrange("p (h e) -> p h e", h=H), o[:, :, 0:HD])
                last.then_inc(S["o1"], 1)
                dve.wait_ge(S["o1"], it)
                dve.wait_ge(S["inter"], it)
                tt(buf_a[:, D:2 * D], buf_a[:, D:2 * D], buf_b[:, 0:D], ALU.add).then_inc(S["o1_sum"], 1)
                dve.wait_ge(S["o1_sum"], it)
                dve.wait_ge(S["gate"], it)
                tt(buf_a[:, 0:512], buf_a[:, 0:512], buf_c[:, 0:512], ALU.mult).then_inc(S["gated"], 1)
                dve.wait_ge(S["gated"], it)
                tt(buf_c[:, 512:1024], buf_a[:, 0:512], buf_a[:, 0:512], ALU.mult).then_inc(S["sq"], 1)
                dve.wait_ge(S["sq"], it)
                dve.tensor_reduce(ms[:], buf_c[:, 512:1024].rearrange("p (h e) -> p h e", e=HD), AX.X, ALU.add).then_inc(S["ms"], 1)
                dve.wait_ge(S["ms"], it)
                ts(ms[:], ms[:], 1.0 / HD, None, ALU.mult).then_inc(S["ms_mean"], 1)
                dve.wait_ge(S["ms_mean"], it)
                r = rsqrt(ms[:], NJ * H, EPS_RMS, it, "rms_rs")
                tt(buf_c[:, 512:1024].rearrange("p (h e) -> p h e", e=HD), buf_a[:, 0:512].rearrange("p (h e) -> p h e", e=HD),
                   r.unsqueeze(2).to_broadcast([P, NJ * H, HD]), ALU.mult).then_inc(S["normed"], 1)
                dve.wait_ge(S["normed"], it)
                for j in range(NJ):
                    last = tt(cat[:, j * D:(j + 1) * D], buf_c[:, 512 + j * D:512 + (j + 1) * D], nw_b[:], ALU.mult)
                last.then_inc(S["og"], 1)
                dve.wait_ge(S["t1_kept"], it * 2)
                low_part(None, bank[3][:], "g_lo", "g_hi", it)
                dve.wait_ge(S["out1"], it)
                tt(x_b, bank[4][:].rearrange("p (j d) -> p j d", j=NJ), x_b, ALU.add).then_inc(S["x2"], 1)
                dve.wait_ge(S["x2"], it)
            dve.memset(zeros, 0.0).then_inc(S["zeros"], 1)
            def two_experts(e2):
                for u in range(8):
                    dve.wait_ge(S["e_s"], e2 * 8 + (u + 1))
                    dve.wait_ge(S["h1_ps"], e2 * 8 + (u + 1))
                    tt(e_p[u % 2], bank[1][:], e_s[u % 2], ALU.mult).then_inc(S["e_t"], 1)
                    dve.wait_ge(S["e_t"], e2 * 8 + (u + 1))
                    dve.wait_ge(S["cwb"], e2 * 4 + (u // 2 + 1))
                    tt(e_m[u % 2], e_p[u % 2], cwb[(u // 2) % 2], ALU.mult).then_inc(S["e_m"], 1)
                    dve.wait_ge(S["eh_hi"], e2 * 8 + (u + 1))
                    tt(h_lo[:, u % 2, :], e_m[u % 2], h_hi[:, u % 2, :].bitcast(F32), ALU.subtract).then_inc(S["eh_lo"], 1)

            with dve.Fori(0, E // 2 - 1) as e2:
                two_experts(e2)
            two_experts(E // 2 - 1)
            dve.wait_ge(S["e_out"], 8 * (E // 2 + 1))
            for i in range(B):
                x_i = x_all[:, i * NJ:(i + 1) * NJ, :].rearrange("p j d -> p (j d)")
                tt(x_i, bank[4 + i][:], x_i, ALU.add).then_inc(S["y"], 1)


def constants():
    f, bf = np.float32, np.dtype(mybir.dt.np(BF16))
    c = {"ident_f": np.eye(P, dtype=f), "ident_b": np.eye(P, dtype=bf)}
    d = np.arange(P) % HD
    inv0 = (f(1.0) / np.power(f(1250), np.arange(0, HD, 2, dtype=f) / f(HD))).astype(f)
    ang0 = (np.arange(T, dtype=f)[:, None] * inv0[None, :]).astype(f)
    ang0 = np.concatenate([ang0, ang0], -1)
    c["cos0"] = np.cos(ang0).astype(f).T[d]
    c["sin0"] = (np.sin(ang0).astype(f) * np.where(np.arange(HD) < HD // 2, f(-1), f(1))).T[d]
    inv1 = np.power(f(10000.0), f(-2.0) * np.arange(HD // 2, dtype=f) / f(HD)).astype(f)
    ang1 = (np.arange(T, dtype=f)[:, None] * inv1[None, :]).astype(f)
    cos1, sin1 = np.cos(ang1).astype(f), np.sin(ang1).astype(f)

    def tokens(a):
        return a.reshape(NJ, P, D).transpose(1, 0, 2)

    c["cos1"] = tokens(np.tile(np.concatenate([cos1, cos1], -1), (1, H)))
    c["sin1"] = tokens(np.tile(np.concatenate([-sin1, sin1], -1), (1, H)))
    lam = -(f(2.0) ** (f(-8.0) * (np.arange(H, dtype=f) + f(1.0)) / f(H)))
    i = np.arange(P, dtype=f)
    diff = i[None, :] - i[:, None]
    c["decay"] = np.where(diff[:, None, :] >= 0, np.exp(lam[None, :, None] * np.maximum(diff, 0)[:, None, :]), f(0))
    head = np.arange(D) // HD
    c["decay_q"] = np.exp(lam[head][:, None] * (i[None, :] + f(1))).reshape(NC, P, P).transpose(1, 0, 2)
    c["decay_k"] = np.exp(lam[head][None, :] * (f(P - 1) - i[:, None]))
    c["blockdiag"] = np.repeat((np.arange(P)[:, None] // HD == np.arange(P)[None, :] // HD)[:, None, :], NC, 1)
    blk = np.zeros((NBLK, FF // P, P))
    for m in range(FF // P):
        for p in range(P):
            blk[(m * P + p) // BS, m, p] = 1
    c["sel_blk"] = blk.astype(bf)
    sel = np.zeros((P, E, P))
    for part in range(3):
        for e in range(E):
            sel[part * E + e, e, :] = 1
    c["sel_exp"] = sel.astype(bf)
    return {"c_" + k: np.ascontiguousarray(v if v.dtype == bf else v.astype(f)) for k, v in c.items()}


def layout(x):
    x = {k: np.asarray(v) for k, v in x.items()}
    perm = np.arange(D).reshape(-1, 2, HD // 2)[:, ::-1].reshape(-1)
    permk = perm[:G * HD]
    wk, bk = x["L0_attn_wk"], x["L0_attn_bk"]
    bq = x["L0_attn_bq"]
    four = P // (G * HD)

    def bias(q, k):
        return np.stack([q[:P], q[P:], np.tile(k, four)], 1)

    ex = np.stack([x["L1_ffn_wi_0"], x["L1_ffn_wi_1"], x["L1_ffn_wo"]], 1)
    a = {
        "x": x["L0_attn_x"].reshape(NTOK, D),
        "wq": x["L0_attn_wq"], "wqp": x["L0_attn_wq"][:, perm],
        "wk": np.tile(wk, (1, four)), "wkp": np.tile(wk[:, permk], (1, four)),
        "wvr": np.concatenate([x["L0_attn_wv"], x["L0_ffn_Wr"].T], 1),
        "w1": x["L0_ffn_W1"].T, "w2": x["L0_ffn_W2"].T, "wo": x["L0_attn_wo"],
        "wq1": x["L1_attn_Wq"], "wk1": x["L1_attn_Wk"], "wv1": x["L1_attn_Wv"],
        "wg1": np.tile(x["L1_attn_Wg1"], (1, P // HD)), "gk": x["L1_ffn_gate_kernel"], "wo1": x["L1_attn_Wo"],
        "experts": ex.reshape(E, 3, NC, P, D).transpose(0, 3, 1, 2, 4).reshape(E, P, EW),
        "bv": x["L0_attn_bv"], "br": x["L0_ffn_br"], "bo": x["L0_attn_bo"], "nw": x["L1_attn_norm_weight"],
        "c_bqk": bias(bq, bk), "c_bqkp": bias(bq[perm], bk[permk]), "c_wg2": x["L1_attn_Wg2"],
    }
    return {k: np.ascontiguousarray(v) for k, v in a.items()}


def kernel(**inputs):
    import concourse.bacc as _bacc
    from concourse.bass_utils import run_bass_kernel_spmd as _run

    arrays = {f"in_{k}": v for k, v in {**layout(inputs), **constants()}.items()}
    nc = _bacc.Bacc("TRN2", target_bir_lowering=False, num_devices=1)
    aps = {k[3:]: nc.dram_tensor(k, v.shape, mybir.dt.from_np(v.dtype), kind="ExternalInput").ap() for k, v in arrays.items()}
    out = nc.dram_tensor("out_0", (NTOK, D), F32, kind="ExternalOutput").ap()
    build(nc, aps, out)
    r = _run(nc, [arrays], core_ids=[0])
    return r.results[0]["out_0"].reshape(B, T, D)
```

```python
from contextlib import ExitStack

import numpy as np

import concourse.bass as bass
from concourse import mybir

F32 = mybir.dt.float32
F32R = mybir.dt.float32r
BF16 = mybir.dt.bfloat16
I32 = mybir.dt.int32
ALU = mybir.AluOpType
ACT = mybir.ActivationFunctionType
AX = mybir.AxisListType

P = 128
B, T, D = 4, 256, 256
NJ = T // P
NC = D // P
H, G, HD = 16, 2, 16
HPG = H // G
NBLK, BS, TOPK = 16, 64, 4
FF = NBLK * BS
E, TOPE = 8, 2
NTOK = B * T
EPS_LN = 1e-5
EPS_RMS = 1e-6
LOW = -3.0e38
HIGH = 3.0e38
Q_PARTS = (0, 0, 0, 1, 1, 2)
K_PARTS = (0, 1, 2, 0, 1, 0)
NPART = len(Q_PARTS)
KS = NPART * HD
KM = KS + 2

GROUPS = [
    [("wq", NC, D), ("wqp", NC, D), ("wk", NC, P), ("wkp", NC, P), ("wvr", NC, G * HD + NBLK)],
    [("w1", NC, FF)],
    [("w2", FF // P, D), ("wo", NC, D)],
    [("wq1", NC, D), ("wk1", NC, D), ("wv1", NC, D), ("wg1", NC, P), ("gk", NC, E), ("wo1", NC, D)],
]
PLACE = {}
_at = 0
for _g in GROUPS:
    for _n, _r, _c in _g:
        PLACE[_n] = (_at, _r, _c)
        _at += _r * _c
NW = _at
SPAN = [(PLACE[g[0][0]][0], PLACE[g[-1][0]][0] + g[-1][1] * g[-1][2]) for g in GROUPS]
EW = 3 * NC * D


class Signals(dict):

    def __init__(self, nc, ctx):
        super().__init__()
        self.nc, self.ctx = nc, ctx

    def __missing__(self, name):
        self[name] = self.ctx.enter_context(self.nc.semaphore(name))
        return self[name]


def build(nc, A, out):
    with ExitStack() as ctx:
        S = Signals(nc, ctx)

        def sb(name, shape, dt=F32):
            return ctx.enter_context(nc.sbuf_tensor(name, shape, dt))

        bank = [ctx.enter_context(nc.psum_tensor(f"bank{i}", [P, 512], F32)) for i in range(8)]
        qk_dram = nc.dram_tensor("qk_scratch", [3, 3, P, T], BF16, kind="Internal").ap()
        nm_dram = nc.dram_tensor("nm_scratch", [2 * H, T], BF16, kind="Internal").ap()
        qk1_dram = nc.dram_tensor("qk1_scratch", [3, 4, P, T], BF16, kind="Internal").ap()

        w_hi, w_lo = sb("w_hi", [P, NW], F32R), sb("w_lo", [P, NW], F32R)
        arena = sb("arena", [P, NW])
        e_stage = sb("e_stage", [P, 2, EW])
        consts = {}
        for name, shape, dt in [
            ("ident_f", [P, P], F32), ("ident_b", [P, P], BF16), ("cos0", [P, T], F32),
            ("sin0", [P, T], F32), ("bqk", [P, 3], F32), ("bqkp", [P, 3], F32),
            ("cos1", [P, NJ, HD], F32), ("sin1", [P, NJ, HD], F32), ("decay", [P, H, P], F32),
            ("decay_q", [P, NC, P], F32), ("decay_k", [P, D], F32), ("blockdiag", [P, P], BF16),
            ("sel_blk", [NBLK, FF // P, P], BF16), ("sel_exp", [P, E, P], BF16),
            ("wg2", [HD, D], F32),
        ]:
            consts[name] = sb("c_" + name, shape, dt)
        bv_b = sb("bv_b", [P, G * HD])
        br_b = sb("br_b", [P, NBLK])
        bo_b = sb("bo_b", [P, D])
        nw_b = sb("nw_b", [P, D])
        ident_f, ident_b = consts["ident_f"], consts["ident_b"]

        x_all = sb("x_all", [P, B * NJ, D])
        t_hi_all = sb("t_hi_all", [P, NC, NTOK], F32R)
        t_lo_all = sb("t_lo_all", [P, NC, NTOK], F32R)
        cw_t = sb("cw_t", [P, NTOK], BF16)
        tick = sb("tick", [P, 1])
        stats = sb("stats", [P, NJ, 6])
        mv = sb("mv", [P, NJ, 2])
        rs = sb("rs", [P, 4, NJ * H])
        t_hi, t_lo = sb("t_hi", [P, NC * T], F32R), sb("t_lo", [P, NC * T], F32R)
        t1_hi, t1_lo = sb("t1_hi", [P, NC * T], F32R), sb("t1_lo", [P, NC * T], F32R)
        qk_sp = sb("qk_sp", [P, 3, 4 * T], BF16)
        q_hat = sb("q_hat", [P, H, T], BF16)
        q_hat1 = sb("q_hat1", [P, H, T], BF16)
        k_hat = sb("k_hat", [P, G, T], BF16)
        k_hat1 = sb("k_hat1", [P, H, T], BF16)
        v_aug = sb("v_aug", [P, NJ, G, 2 * HD])
        lg = sb("lg", [P, NJ, NBLK + 8])
        top = sb("top", [P, NJ, 8])
        rep = sb("rep", [P, NJ, NBLK + 8])
        mask = sb("mask", [P, NJ, NBLK], BF16)
        h_hi, h_lo = sb("h_hi", [P, 2, 512], F32R), sb("h_lo", [P, 2, 512], F32R)
        nm = sb("nm", [P, NJ, H])
        rden = nm
        nm_sp = sb("nm_sp", [P, NJ, 2 * H], BF16)

        def part(at, n=512):
            return arena[:, at:at + n]

        area0 = e_stage[:].rearrange("p k n -> p (k n)")
        a0, b0, c0 = (area0[:, 3 * T * i:3 * T * (i + 1)] for i in range(3))
        mask_t = area0[0:NBLK, 9 * T + 512:9 * T + 640].bitcast(BF16)
        nm_t = area0[0:2 * H, 9 * T + 640:9 * T + 768].bitcast(BF16)
        xn, cat = a0[:, 0:NJ * D], a0[:, 0:NJ * D]
        ring = [area0[:, 9 * T:9 * T + 512]] + [part(512 * i) for i in range(3)]
        osb = [part(1536), part(2048)]
        hg = [osb[0], ring[0]]
        hm = [ring[1], ring[2]]
        a1, b1, c1 = (part(2560 + 1024 * i, 1024) for i in range(3))
        xn1 = a1[:, 0:NJ * D]
        cat1 = a1[:, NJ * D:2 * NJ * D]
        ring1 = [part(5632 + 512 * i) for i in range(3)]
        kd = part(7168, D)
        v1 = part(7424, NJ * (D + HD)).rearrange("p (j n) -> p j n", j=NJ)
        g1_t = part(7968, T)[0:HD]
        lg1 = part(8224, NJ * 16).rearrange("p (j n) -> p j n", j=NJ)
        cw = part(8256, NJ * 4 * E).rearrange("p (j i e) -> p j i e", j=NJ, i=4)
        cw_sp = part(8320, NJ * 3 * E // 2).bitcast(BF16).rearrange("p (j e) -> p j e", j=NJ)
        ms = part(8352, NJ * H)
        qd, state = b1[:, 0:D], b1[:, D:2 * D]
        inter = b1[:, 0:D]
        osb1 = [b1[:, 512:1024], c1[:, 512:1024]]
        tg = c1[:, 0:512]
        e_s, e_p, e_m, cwb = ([part(1024 * i + 512 * k) for k in range(2)] for i in range(4))
        zeros = part(4096)
        e_hi, e_lo = ([full[:, PLACE["w1"][0] + k * EW:PLACE["w1"][0] + (k + 1) * EW] for k in range(2)] for full in (w_hi, w_lo))

        def w(name, part_of, row, c0, c1):
            at, _, n = PLACE[name]
            return part_of[:, at + row * n + c0:at + row * n + c1]

        def mm3(pe, dst, lhs, rhs, first, last, lone_start=False):
            for i, (a, b) in enumerate(((0, 0), (0, 1), (1, 0))):
                ins = pe.matmul(dst, lhs[a], rhs[b], start=first and i == 0, stop=last and i == 2,
                                skip_group_check=True)
            return ins

        def wx(name, row, c0, c1):
            return w(name, w_hi, row, c0, c1), w(name, w_lo, row, c0, c1)

        def tx(c, j=None, hi=t_hi, lo=t_lo):
            a, b = (c * T, (c + 1) * T) if j is None else (c * T + j * P, c * T + (j + 1) * P)
            return hi[:, a:b], lo[:, a:b]

        def tx1(c, j=None):
            return tx(c, j, t1_hi, t1_lo)

        EARLY = ("ident_f", "cos0", "sin0", "bqk", "bqkp")

        block = ctx.enter_context(nc.Block())
        ex_dram = A["experts"]

        @block.sync
        def _(sp):
            for i in range(B):
                sp.dma_start(x_all[:, i * NJ:(i + 1) * NJ, :],
                             A["x"][i * T:(i + 1) * T, :].rearrange("(j p) d -> p j d", p=P)).then_inc(S[f"x_in{min(i, 1)}"], 16)
                if i < len(GROUPS):
                    for name, rows, cols in GROUPS[i]:
                        at = PLACE[name][0]
                        sp.dma_start(arena[:, at:at + rows * cols].rearrange("p (r n) -> p r n", r=rows),
                                     A[name].rearrange("(r p) n -> p r n", p=P)).then_inc(S[f"w_in{i}"], 16)

            def q_k_stacked(it):
                sp.wait_ge(S["qk_sp"], it)
                for s in range(3):
                    sp.dma_start(qk_dram[s].rearrange("c p t -> p c t"),
                                 qk_sp[:, s, 0:3 * T].rearrange("p (c t) -> p c t", c=3)).then_inc(S["qk_out"], 16)
                sp.wait_ge(S["qk_out"], it * 48)
                for n in range(NPART):
                    sp.dma_start(k_hat[n * HD:(n + 1) * HD, :, :],
                                 qk_dram[K_PARTS[n], 2, 0:G * HD].rearrange("(g d) t -> d g t", d=HD)).then_inc(S["k_in"], 16)
                    sp.dma_start(q_hat[n * HD:(n + 1) * HD, :, :],
                                 qk_dram[Q_PARTS[n], 0:2].rearrange("c (h d) t -> d (c h) t", d=HD)).then_inc(S["q_in"], 16)

            def maxima(it):
                sp.wait_ge(S["nm_t"], it)
                sp.dma_start(nm_dram, nm_t).then_inc(S["nm_out"], 16)
                sp.wait_ge(S["nm_out"], it * 16)
                sp.dma_start(q_hat[KS:KM, :, :], nm_dram.rearrange("(s h) t -> s h t", s=2)).then_inc(S["nm_in"], 16)

            def q_k_stacked1(it):
                sp.wait_ge(S["qk1_sp"], it)
                sp.dma_start(qk1_dram.rearrange("s c p t -> p (s c) t"),
                             qk_sp[:, :, :].rearrange("p s (c t) -> p (s c) t", c=4)).then_inc(S["qk1_out"], 16)
                sp.wait_ge(S["qk1_out"], it * 16)
                for n in range(NPART):
                    sp.dma_start(k_hat1[n * HD:(n + 1) * HD, :, :],
                                 qk1_dram[K_PARTS[n], 2:4].rearrange("c (h d) t -> d (c h) t", d=HD)).then_inc(S["k1_in"], 16)
                    sp.dma_start(q_hat1[n * HD:(n + 1) * HD, :, :],
                                 qk1_dram[Q_PARTS[n], 0:2].rearrange("c (h d) t -> d (c h) t", d=HD)).then_inc(S["q1_in"], 16)

            q_k_stacked(1)
            maxima(1)
            with sp.Fori(1, B) as b:
                q_k_stacked(b + 1)
                q_k_stacked1(b)
                maxima(b + 1)
            sp.wait_ge(S["x1"], B)
            for k in range(2):
                sp.dma_start(e_stage[:, k, :], ex_dram[k]).then_inc(S[f"e_in{k}"], 16)
            q_k_stacked1(B)
            with sp.Fori(1, E // 2) as e2:
                for k in range(2):
                    sp.wait_ge(S[f"e_split{k}"], e2)
                    sp.dma_start(e_stage[:, k, :], ex_dram[e2 * 2 + k]).then_inc(S[f"e_in{k}"], 16)
            for i in range(B):
                sp.wait_ge(S["y"], i + 1)
                sp.dma_start(out[i * T:(i + 1) * T, :].rearrange("(j p) d -> p j d", p=P),
                             x_all[:, i * NJ:(i + 1) * NJ, :]).then_inc(S["stored"], 16)
            sp.wait_ge(S["stored"], 16 * B)

        @block.gpsimd
        def _(pool):
            for dst, name in ((bv_b, "bv"), (br_b, "br")):
                pool.dma_start(dst[:], A[name].partition_broadcast(P)).then_inc(S["b_in"], 16)
            pool.memset(v_aug[:], 1.0).then_inc(S["ones"], 1)
            pool.memset(lg[:], LOW).then_inc(S["ones"], 1)
            pool.wait_ge(S["ones"], 2)
            pool.memset(k_hat[KS:P, :, :], 1.0).then_inc(S["ones"], 1)
            pool.wait_ge(S["ones"], 3)
            pool.memset(cw_t[:], 0.0).then_inc(S["ones"], 1)
            for name in consts:
                if name not in EARLY:
                    pool.dma_start(consts[name][:], A["c_" + name]).then_inc(S["c1_in"], 16)
            for dst, name in ((bo_b, "bo"), (nw_b, "nw")):
                pool.dma_start(dst[:], A[name].partition_broadcast(P)).then_inc(S["c1_in"], 16)
            for g in range(1, len(GROUPS)):
                a, z = SPAN[g]
                pool.wait_ge(S["w_hi"], g + 1)
                pool.tensor_tensor(out=w_lo[:, a:z], in0=arena[:, a:z], in1=w_hi[:, a:z].bitcast(F32), op=ALU.subtract).then_inc(S["w_lo"], 1)
            pool.wait_ge(S["w_lo"], len(GROUPS) - 1)
            pool.memset(v1, 0.0).then_inc(S["ones1"], 1)
            pool.memset(lg1, LOW).then_inc(S["ones1"], 1)
            with pool.Fori(0, B) as b:
                it = b + 1
                pool.wait_ge(S["t1_lo"], it)
                pool.wait_ge(S["t1_hi"], it)
                pool.tensor_copy(t_hi_all[:, :, bass.ds(b * T, T)],
                                 t1_hi[:].bitcast(F32).rearrange("p (c t) -> p c t", c=NC)).then_inc(S["t1_kept"], 1)
                pool.tensor_copy(t_lo_all[:, :, bass.ds(b * T, T)],
                                 t1_lo[:].bitcast(F32).rearrange("p (c t) -> p c t", c=NC)).then_inc(S["t1_kept"], 1)
            with pool.Fori(0, E // 2) as e2:
                for k in range(2):
                    pool.wait_ge(S[f"e_hi{k}"], e2 + 1)
                    pool.tensor_tensor(out=e_lo[k], in0=e_stage[:, k, :], in1=e_hi[k].bitcast(F32), op=ALU.subtract).then_inc(S[f"e_split{k}"], 1)

        @block.tensor
        def _(pe):
            NV = G * HD + NBLK
            out0 = bank[1]

            def transposes(dst, src, sem, ident=ident_f):
                src = src.rearrange("p (j d) -> p j d", j=NJ)
                for c in range(NC):
                    for j in range(NJ):
                        last = pe.transpose(dst[:, c * T + j * P:c * T + (j + 1) * P],
                                            src[:, j, c * P:(c + 1) * P], ident[:])
                last.then_inc(S[sem], 1)

            def weights(g, first):
                if first:
                    pe.wait_ge(S["w_hi"], g + 1)
                    pe.wait_ge(S["w_lo0" if g == 0 else "w_lo"], max(g, 1))

            def a_turn(b, first=False):
                if first:
                    pe.wait_ge(S["c0_in"], 16 * len(EARLY))
                pe.wait_ge(S["xn"], b + 1)
                transposes(bank[0], xn, "t_ps")

            def a_qkv(b, first=False):
                weights(0, first)
                pe.wait_ge(S["t_hi"], b + 1)
                pe.wait_ge(S["t_lo"], b + 1)
                for name, dst, n, at in (("wq", bank[1], 2, 0), ("wqp", bank[2], 2, 0), ("wk", bank[3], 1, 0), ("wkp", bank[3], 1, T)):
                    for s in range(n):
                        for c in range(NC):
                            last = mm3(pe, dst[:, at + s * T:at + (s + 1) * T], wx(name, c, s * P, (s + 1) * P), tx(c), c == 0, c == NC - 1)
                last.then_inc(S["qk_ps"], 1)
                for j in range(NJ):
                    for c in range(NC):
                        last = mm3(pe, bank[4][:, j * NV:(j + 1) * NV], tx(c, j), wx("wvr", c, 0, NV), c == 0, c == NC - 1)
                last.then_inc(S["vr_ps"], 1)

            def a_mask(b, first=False):
                if first:
                    pe.wait_ge(S["c1_in"], 16 * (len(consts) - len(EARLY) + 2))
                    pe.wait_ge(S["ones"], 4)
                pe.wait_ge(S["mask"], b + 1)
                mt = bank[0][:].bitcast(BF16)
                for j in range(NJ):
                    last = pe.transpose(mt[0:NBLK, j * P:(j + 1) * P], mask[:, j, :], ident_b[:])
                last.then_inc(S["mask_ps"], 1)

            def a_ffn_out(b, i):
                pe.wait_ge(S["h_hi"], b * 4 + (i + 1))
                pe.wait_ge(S["h_lo"], b * 4 + (i + 1))
                for j in range(NJ):
                    for m in range(2):
                        at = m * T + j * P
                        last = mm3(pe, out0[:, j * D:(j + 1) * D],
                                   (h_hi[:, i % 2, at:at + P], h_lo[:, i % 2, at:at + P]),
                                   wx("w2", 2 * i + m, 0, D), i == 0 and j == 0 and m == 0, False)
                last.then_inc(S["ffn_out"], 1)

            def a_ffn(b, i, first=False):
                if i == 0:
                    weights(1, first)
                    weights(2, first)
                    pe.wait_ge(S["rope"], b + 1)
                    pe.wait_ge(S["mask_t"], b + 1)
                if i >= 1:
                    pe.wait_ge(S["hm"], b * 4 + i)
                for m in range(2):
                    for c in range(NC):
                        last = mm3(pe, bank[2][:, m * T:(m + 1) * T],
                                   wx("w1", c, (2 * i + m) * P, (2 * i + m + 1) * P), tx(c), c == 0, c == NC - 1)
                last.then_inc(S["h_ps"], 1)
                for m in range(2):
                    last = pe.matmul(bank[4][:, m * T:(m + 1) * T], consts["sel_blk"][:, 2 * i + m, :], mask_t[:, :],
                                     start=True, stop=True)
                last.then_inc(S["m_ps"], 1)
                if i == 0:
                    pe.wait_ge(S["q_in"], (b + 1) * (16 * NPART))
                    pe.wait_ge(S["k_in"], (b + 1) * (16 * NPART))
                for h in range(4 * i, 4 * i + 4):
                    if h >= 2:
                        pe.wait_ge(S["max"], b * H + (h - 1))
                    for j in range(NJ):
                        last = pe.matmul(bank[3 * (h % 2)][:, j * T:(j + 1) * T], q_hat[0:KS, h, j * P:(j + 1) * P],
                                         k_hat[0:KS, h // HPG, :], start=True, stop=True)
                    last.then_inc(S["s_ps"], 1)
                    if h % 4 == 1 and i >= 1:
                        a_ffn_out(b, i - 1)

            def a_maxima(b):
                pe.wait_ge(S["nm_sp"], b + 1)
                nt = bank[4][:].bitcast(BF16)
                for j in range(NJ):
                    last = pe.transpose(nt[0:2 * H, j * P:(j + 1) * P], nm_sp[:, j, :], ident_b[:])
                last.then_inc(S["nm_ps"], 1)

            def a_attend(b):
                pe.wait_ge(S["nm_in"], (b + 1) * 16)
                pe.wait_ge(S["nm_t"], b + 1)

                def probs_v(n):
                    u, kt = divmod(n, NJ)
                    g, quarter = divmod(u, 4)
                    pe.wait_ge(S["probs"], b * 16 + (n + 1))
                    pe.matmul(bank[2 + 2 * g][32 * quarter:32 * quarter + 32, :], v_aug[:, kt, g, :], ring[n % 4],
                              start=kt == 0, stop=kt == NJ - 1).then_inc(S["pv"], 1)

                for n in range(16):
                    u, kt = divmod(n, NJ)
                    g, quarter = divmod(u, 4)
                    if n >= 2:
                        pe.wait_ge(S["probs"], b * 16 + (n - 1))
                    pe.matmul(bank[3 * (n % 2)][:, :], k_hat[0:KM, g, kt * P:(kt + 1) * P],
                              q_hat[0:KM, g * HPG + 2 * quarter:g * HPG + 2 * quarter + 2, :],
                              start=True, stop=True).then_inc(S["st_ps"], 1)
                    if n >= 2:
                        probs_v(n - 2)
                probs_v(14)
                probs_v(15)

            def a_turn_back(b):
                for g in range(G):
                    pe.wait_ge(S["osb"], b * G + (g + 1))
                    for h2 in range(2):
                        for j in range(NJ):
                            at = (g * 2 + h2) * P
                            last = pe.transpose(bank[3 * j][:, at:at + P], osb[g][:, h2 * T + j * P:h2 * T + (j + 1) * P], ident_f[:])
                last.then_inc(S["ot_ps"], 1)

            def a_project(b):
                pe.wait_ge(S["cat"], b + 1)
                transposes(bank[2], cat, "ct_ps")
                pe.wait_ge(S["c_hi"], b + 1)
                pe.wait_ge(S["c_lo"], b + 1)
                for j in range(NJ):
                    for c in range(NC):
                        last = mm3(pe, out0[:, j * D:(j + 1) * D], tx(c, j), wx("wo", c, 0, D), False, c == NC - 1)
                last.then_inc(S["out0"], 1)

            def b_turn(b):
                pe.wait_ge(S["xn1"], b + 1)
                transposes(bank[5], xn1, "t1_ps")

            def b_qkv(b):
                pe.wait_ge(S["t1_hi"], b + 1)
                pe.wait_ge(S["t1_lo"], b + 1)
                for name, dst in (("wq1", bank[6]), ("wk1", bank[7]), ("wv1", bank[5])):
                    for j in range(NJ):
                        for c in range(NC):
                            last = mm3(pe, dst[:, j * D:(j + 1) * D], tx1(c, j), wx(name, c, 0, D), c == 0, c == NC - 1)
                    last.then_inc(S[name + "_ps"], 1)
                pe.wait_ge(S["silu"], b * 2 + 1)
                for j in range(NJ):
                    for c in range(NC):
                        mm3(pe, bank[6][:, j * E:(j + 1) * E], tx1(c, j), wx("gk", c, 0, E), c == 0, c == NC - 1)
                for c in range(NC):
                    last = mm3(pe, bank[6][:, T:2 * T], wx("wg1", c, 0, P), tx1(c), c == 0, c == NC - 1)
                last.then_inc(S["g1_ps"], 1)

            def b_gate(b):
                pe.wait_ge(S["g1_t"], b + 1)
                pe.wait_ge(S["silu"], b * 2 + 2)
                for j in range(NJ):
                    last = pe.matmul(bank[7][:, j * D:(j + 1) * D], g1_t[:, j * P:(j + 1) * P], consts["wg2"][:, :], start=True, stop=True)
                last.then_inc(S["gate_ps"], 1)

            def b_turn_qk(b):
                pe.wait_ge(S["v1"], b + 1)
                pe.wait_ge(S["rot"], b + 1)
                transposes(bank[6], c1[:, 0:512], "qt_ps")
                transposes(bank[5], c1[:, 512:1024], "kt_ps")

            def b_state(b):
                pe.wait_ge(S["cw_sp"], b + 1)
                pe.wait_ge(S["tg"], b + 1)
                ct = bank[7][:].bitcast(BF16)
                for j in range(NJ):
                    last = pe.transpose(ct[0:3 * E, j * P:(j + 1) * P], cw_sp[:, j, :], ident_b[:])
                last.then_inc(S["cwt_ps"], 1)
                pe.wait_ge(S["cw_t"], b + 1)
                for c in range(NC):
                    last = pe.matmul(bank[7][:, c * P:(c + 1) * P], kd[:, c * P:(c + 1) * P], v1[:, 0, c * P:(c + 1) * P], start=True, stop=True)
                last.then_inc(S["kv_ps"], 1)
                pe.wait_ge(S["state"], b + 1)
                for c in range(NC):
                    last = pe.matmul(bank[7][:, (2 + c) * P:(3 + c) * P], qd[:, c * P:(c + 1) * P], state[:, c * P:(c + 1) * P], start=True, stop=True)
                last.then_inc(S["inter_ps"], 1)

            def b_attend(b):
                pe.wait_ge(S["q1_in"], (b + 1) * (16 * NPART))
                pe.wait_ge(S["k1_in"], (b + 1) * (16 * NPART))
                pe.wait_ge(S["inter"], b + 1)

                def intra(n):
                    j, four = divmod(n, 4)
                    if n == 4:
                        pe.wait_ge(S["oisb"], b * NJ + 1)
                    pe.wait_ge(S["sc"], b * 8 + (n + 1))
                    for i in range(4):
                        h = four * 4 + i
                        last = pe.matmul(bank[7][32 * i:32 * i + 32, four * P:(four + 1) * P], v1[:, j, h * HD:h * HD + 2 * HD],
                                         ring1[n % 3][:, i * P:(i + 1) * P], start=True, stop=True, skip_group_check=True)
                    last.then_inc(S["oi"], 1)

                for n in range(8):
                    j, four = divmod(n, 4)
                    if n >= 2:
                        pe.wait_ge(S["sc"], b * 8 + (n - 1))
                    for i in range(4):
                        h = four * 4 + i
                        last = pe.matmul(bank[5 + n % 2][:, i * P:(i + 1) * P], k_hat1[0:KS, h, j * P:(j + 1) * P],
                                         q_hat1[0:KS, h, j * P:(j + 1) * P], start=True, stop=True)
                    last.then_inc(S["s1_ps"], 1)
                    if n >= 2:
                        intra(n - 2)
                intra(6)
                intra(7)

            def b_turn_back(b):
                for j in range(NJ):
                    pe.wait_ge(S["oisb"], b * NJ + (j + 1))
                    if j == 0:
                        pe.wait_ge(S["sc"], b * 8 + 8)
                    for four in range(4):
                        last = pe.transpose(bank[5 + j][:, four * P:(four + 1) * P], osb1[j][:, four * P:(four + 1) * P], ident_f[:])
                last.then_inc(S["oit_ps"], 1)

            def b_project(b):
                pe.wait_ge(S["og"], b + 1)
                transposes(bank[7], cat1, "gt_ps")
                pe.wait_ge(S["g_hi"], b + 1)
                pe.wait_ge(S["g_lo"], b + 1)
                for j in range(NJ):
                    for c in range(NC):
                        last = mm3(pe, bank[5][:, j * D:(j + 1) * D], tx1(c, j), wx("wo1", c, 0, D), c == 0, c == NC - 1)
                last.then_inc(S["out1"], 1)

            a_turn(0, True)
            a_qkv(0, True)
            a_mask(0, True)
            for i in range(4):
                a_ffn(0, i, True)
            a_ffn_out(0, 3)
            a_maxima(0)
            a_attend(0)
            a_turn_back(0)
            a_project(0)
            weights(3, True)
            pe.wait_ge(S["ones1"], 2)
            with pe.Fori(1, B) as b:
                a_turn(b)
                b_turn(b - 1)
                a_qkv(b)
                b_qkv(b - 1)
                a_mask(b)
                b_gate(b - 1)
                a_ffn(b, 0)
                a_ffn(b, 1)
                b_turn_qk(b - 1)
                a_ffn(b, 2)
                a_ffn(b, 3)
                a_ffn_out(b, 3)
                a_maxima(b)
                b_state(b - 1)
                b_attend(b - 1)
                b_turn_back(b - 1)
                a_attend(b)
                a_turn_back(b)
                b_project(b - 1)
                a_project(b)
            b_turn(B - 1)
            b_qkv(B - 1)
            b_gate(B - 1)
            b_turn_qk(B - 1)
            b_state(B - 1)
            b_attend(B - 1)
            b_turn_back(B - 1)
            b_project(B - 1)

            pe.wait_ge(S["zeros"], 1)
            acc = (bank[4], bank[5], bank[6], bank[7])
            for _ in range(2):
                for a in acc:
                    pe.matmul(a[:, :], zeros[0:1, 0:P], zeros[0:1, :], start=True, stop=False,
                              skip_group_check=True).then_inc(S["e_out"], 1)

            def sel_of(e):
                return consts["sel_exp"][:, bass.ds(e, 1), :].rearrange("p o n -> p (o n)")

            def two_experts(e2):
                def ew(k, which, row, c0, c1):
                    o = which * NC * D + row * D
                    return e_hi[k][:, o + c0:o + c1], e_lo[k][:, o + c0:o + c1]

                def expert_out(u):
                    k, n, m = u // 4, u // 2 % 2, u % 2
                    pe.wait_ge(S["eh_hi"], e2 * 8 + (u + 1))
                    pe.wait_ge(S["eh_lo"], e2 * 8 + (u + 1))
                    for t in range(4):
                        tile = n * 4 + t
                        last = mm3(pe, acc[tile // 2][:, (tile % 2) * D:(tile % 2 + 1) * D],
                                   (h_hi[:, u % 2, t * P:(t + 1) * P], h_lo[:, u % 2, t * P:(t + 1) * P]),
                                   ew(k, 2, m, 0, D), False, False)
                    last.then_inc(S["e_out"], 1)

                for u in range(8):
                    k, n, m = u // 4, u // 2 % 2, u % 2
                    cols = slice(n * 512, (n + 1) * 512)
                    if u % 4 == 0:
                        pe.wait_ge(S[f"e_split{k}"], e2 + 1)
                    if m == 0:
                        pe.matmul(bank[3][:, :], sel_of(e2 * 2 + k),
                                  cw_t[:, cols], start=True, stop=True).then_inc(S["cwb_ps"], 1)
                    for c in range(NC):
                        last = mm3(pe, bank[2 * (u % 2)][:, :], ew(k, 0, c, m * P, (m + 1) * P),
                                   (t_hi_all[:, c, cols], t_lo_all[:, c, cols]), c == 0, c == NC - 1)
                    last.then_inc(S["h0_ps"], 1)
                    if u >= 1:
                        pe.wait_ge(S["e_t"], e2 * 8 + u)
                    for c in range(NC):
                        last = mm3(pe, bank[1][:, :], ew(k, 1, c, m * P, (m + 1) * P),
                                   (t_hi_all[:, c, cols], t_lo_all[:, c, cols]), c == 0, c == NC - 1)
                    last.then_inc(S["h1_ps"], 1)
                    if u >= 1:
                        expert_out(u - 1)
                expert_out(7)

            with pe.Fori(0, E // 2 - 1) as e2:
                two_experts(e2)
            two_experts(E // 2 - 1)

        @block.scalar
        def _(act):
            cp = ACT.Copy

            def copy(dst, src, done, *waits):
                for name, value in waits:
                    act.wait_ge(S[name], value)
                act.activation(dst, src, cp).then_inc(S[done], 1)

            def high_group(g):
                a, z = SPAN[g]
                copy(w_hi[:, a:z], arena[:, a:z], "w_hi", (f"w_in{g}", 16 * len(GROUPS[g])))

            def a_turn(b):
                copy(t_hi[:], bank[0][:], "t_hi", ("t_ps", b + 1))

            def a_mask(b):
                copy(mask_t, bank[0][:].bitcast(BF16)[0:NBLK, 0:T], "mask_t", ("mask_ps", b + 1))

            def a_ffn(b, i):
                act.wait_ge(S["h_ps"], b * 4 + (i + 1))
                act.activation(hg[i % 2], bank[2][:], ACT.Gelu).then_inc(S["hg"], 1)
                if i >= 2:
                    act.wait_ge(S["ffn_out"], b * 4 + (i - 1))
                copy(h_hi[:, i % 2, :], hm[i % 2], "h_hi", ("hm", b * 4 + (i + 1)))

            def a_maxima(b):
                copy(nm_t, bank[4][:].bitcast(BF16)[0:2 * H, 0:T], "nm_t", ("nm_ps", b + 1))

            def a_attend(b):
                for n in range(16):
                    act.wait_ge(S["st_ps"], b * 16 + (n + 1))
                    if n >= 4:
                        act.wait_ge(S["pv"], b * 16 + (n - 3))
                    act.activation(ring[n % 4], bank[3 * (n % 2)][:], ACT.Exp, scale=1.0 / HD).then_inc(S["probs"], 1)
                    if n == 10:
                        copy(osb[0], bank[2][:], "osb", ("pv", b * 16 + 8))
                copy(osb[1], bank[4][:], "osb", ("pv", b * 16 + 16))

            def a_project(b):
                copy(t_hi[:], bank[2][:], "c_hi", ("ct_ps", b + 1))

            def b_turn(b):
                copy(t1_hi[:], bank[5][:], "t1_hi", ("t1_ps", b + 1))

            def b_qkv(b):
                act.wait_ge(S["wq1_ps"], b + 1)
                act.activation(a1[:, 0:512], bank[6][:], ACT.Silu).then_inc(S["silu"], 1)
                act.wait_ge(S["wk1_ps"], b + 1)
                act.activation(a1[:, 512:1024], bank[7][:], ACT.Silu).then_inc(S["silu"], 1)
                copy(v1[:, :, 0:D], bank[5][:].rearrange("p (j d) -> p j d", j=NJ), "v1", ("wv1_ps", b + 1))
                copy(g1_t, bank[6][0:HD, T:2 * T], "g1_t", ("g1_ps", b + 1))

            def b_gate(b):
                act.wait_ge(S["gate_ps"], b + 1)
                act.wait_ge(S["kt_ps"], b + 1)
                act.wait_ge(S["kd"], b + 1)
                act.activation(tg, bank[7][:], ACT.Tanh, scale=0.5).then_inc(S["tg"], 1)

            def b_state(b):
                act.wait_ge(S["cw_d"], b + 1)
                act.activation(cw[:, :, 1, :], cw[:, :, 0, :], ACT.Tanh, scale=0.5).then_inc(S["cw_tanh"], 1)
                copy(cw_t[0:3 * E, bass.ds(b * T, T)], bank[7][:].bitcast(BF16)[0:3 * E, 0:T], "cw_t", ("cwt_ps", b + 1))
                copy(inter, bank[7][:, D:2 * D], "inter", ("inter_ps", b + 1))

            def b_attend(b):
                for j in range(NJ):
                    copy(osb1[j], bank[7][:], "oisb", ("oi", b * 8 + 4 * (j + 1)))

            def b_project(b):
                copy(t1_hi[:], bank[7][:], "g_hi", ("gt_ps", b + 1), ("t1_kept", (b + 1) * 2))

            for name in EARLY:
                act.dma_start(consts[name][:], A["c_" + name]).then_inc(S["c0_in"], 16)
            high_group(0)
            a_turn(0)
            high_group(1)
            a_mask(0)
            high_group(2)
            for i in range(4):
                a_ffn(0, i)
            high_group(3)
            a_maxima(0)
            a_attend(0)
            a_project(0)
            act.wait_ge(S["ones1"], 2)
            with act.Fori(1, B) as b:
                a_turn(b)
                b_turn(b - 1)
                b_qkv(b - 1)
                a_mask(b)
                a_ffn(b, 0)
                a_ffn(b, 1)
                b_gate(b - 1)
                a_ffn(b, 2)
                a_ffn(b, 3)
                a_maxima(b)
                b_state(b - 1)
                b_attend(b - 1)
                a_attend(b)
                b_project(b - 1)
                a_project(b)
            b_turn(B - 1)
            b_qkv(B - 1)
            b_gate(B - 1)
            b_state(B - 1)
            b_attend(B - 1)
            b_project(B - 1)
            def high_part(k, pair):
                act.wait_ge(S[f"e_in{k}"], (pair + 1) * 16)
                act.activation(e_hi[k], e_stage[:, k, :], cp).then_inc(S[f"e_hi{k}"], 1)

            def two_experts(e2, more):
                for u in range(8):
                    act.wait_ge(S["h0_ps"], e2 * 8 + (u + 1))
                    act.activation(e_s[u % 2], (bank[0], bank[2])[u % 2][:], ACT.Silu).then_inc(S["e_s"], 1)
                    if u % 2 == 0:
                        act.activation(cwb[(u // 2) % 2], bank[3][:], cp).then_inc(S["cwb"], 1)
                    act.wait_ge(S["e_m"], e2 * 8 + (u + 1))
                    act.wait_ge(S["e_out"], e2 * 8 + (u + 7))
                    act.activation(h_hi[:, u % 2, :], e_m[u % 2], cp).then_inc(S["eh_hi"], 1)
                    if u == 1:
                        high_part(1, e2)
                    if u == 5 and more:
                        high_part(0, e2 + 1)

            act.wait_ge(S["ffn_out"], 4 * B)
            high_part(0, 0)
            with act.Fori(0, E // 2 - 1) as e2:
                two_experts(e2, True)
            two_experts(E // 2 - 1, False)

        @block.vector
        def _(dve):
            tt, ts, stt = dve.tensor_tensor, dve.tensor_scalar, dve.scalar_tensor_tensor
            NV = G * HD + NBLK

            def hold():
                dve.memset(tick[:], 0.0)

            def rsqrt(var, n, eps, it, name):
                v, y, t, r = (rs[:, i, 0:n] for i in range(4))
                steps = [
                    lambda: ts(v, var, eps, None, ALU.add),
                    lambda: ts(y.bitcast(I32), v.bitcast(I32), 1, None, ALU.logical_shift_right),
                    lambda: ts(r.bitcast(I32), y.bitcast(I32), -1.0, float(0x5F3759DF), ALU.mult, ALU.add),
                    lambda: ts(v, v, -0.5, None, ALU.mult),
                ] + [
                    lambda: tt(t, r, r, ALU.mult),
                    lambda: tt(t, t, v, ALU.mult),
                    lambda: stt(r, t, 1.5, r, ALU.add, ALU.mult),
                ] * 3
                for k, step in enumerate(steps):
                    step().then_inc(S[name], 1)
                    dve.wait_ge(S[name], (it - 1) * len(steps) + (k + 1))
                return r

            def layernorm(b, dst, done):
                it = b + 1
                x = [x_all[:, bass.ds(b * NJ + j, 1), :].rearrange("p o d -> p (o d)") for j in range(NJ)]
                hold()
                for j in range(NJ):
                    dve.bn_stats(stats[:, j, :], x[j]).then_inc(S[done + "_stats"], 1)
                dve.wait_ge(S[done + "_stats"], it * NJ)
                hold()
                for j in range(NJ):
                    last = dve.bn_aggr(mv[:, j, :], stats[:, j, :])
                last.then_inc(S[done + "_mv"], 1)
                dve.wait_ge(S[done + "_mv"], it)
                r = rsqrt(mv[:, :, 1], NJ, EPS_LN, it, done + "_rs")
                for j in range(NJ):
                    last = ts(dst[:, j * D:(j + 1) * D], x[j], mv[:, j, 0:1], r[:, j:j + 1], ALU.subtract, ALU.mult)
                last.then_inc(S[done], 1)

            def low_part(lo, ps, hi, done, hi_done, it):
                dve.wait_ge(S[hi_done], it)
                tt(lo[:], ps, hi[:].bitcast(F32), ALU.subtract).then_inc(S[done], 1)

            def bf16_parts(src, work, n, sem, it):
                q = S[sem + "_step"]
                dve.tensor_copy(qk_sp[:, 0, 0:n], src).then_inc(q, 1)
                dve.wait_ge(q, it * 3 - 2)
                tt(work[:, 0:n], src, qk_sp[:, 0, 0:n], ALU.subtract).then_inc(q, 1)
                dve.wait_ge(q, it * 3 - 1)
                dve.tensor_copy(qk_sp[:, 1, 0:n], work[:, 0:n]).then_inc(q, 1)
                dve.wait_ge(q, it * 3)
                tt(qk_sp[:, 2, 0:n], work[:, 0:n], qk_sp[:, 1, 0:n], ALU.subtract).then_inc(S[sem], 1)

            def a_rope(b):
                it = b + 1
                dve.wait_ge(S["qk_ps"], it)
                src = (bank[1][:, 0:T], bank[1][:, T:2 * T], bank[3][:, 0:T])
                srcp = (bank[2][:, 0:T], bank[2][:, T:2 * T], bank[3][:, T:2 * T])
                for s in range(3):
                    stt(a0[:, s * T:(s + 1) * T], src[s], consts["bqk"][:, s:s + 1], consts["cos0"][:], ALU.add, ALU.mult)
                    last = stt(b0[:, s * T:(s + 1) * T], srcp[s], consts["bqkp"][:, s:s + 1], consts["sin0"][:], ALU.add, ALU.mult)
                last.then_inc(S["rope"], 1)
                dve.wait_ge(S["rope"], it)
                tt(c0, a0, b0, ALU.add).then_inc(S["roped"], 1)
                dve.wait_ge(S["roped"], it)
                bf16_parts(c0, a0, 3 * T, "qk_sp", it)

            def a_router(b):
                it = b + 1
                dve.wait_ge(S["vr_ps"], it)
                vr = bank[4][:, 0:NJ * NV].rearrange("p (j n) -> p j n", j=NJ)
                for j in range(NJ):
                    tt(v_aug[:, j, :, 0:HD], vr[:, j, 0:G * HD].rearrange("p (g d) -> p g d", g=G),
                       bv_b[:].rearrange("p (g d) -> p g d", g=G), ALU.add)
                    last = tt(lg[:, j, 0:NBLK], vr[:, j, G * HD:NV], br_b[:], ALU.add)
                last.then_inc(S["lg"], 1)
                dve.wait_ge(S["lg"], it)
                hold()
                for j in range(NJ):
                    last = dve.max(top[:, j, :], lg[:, j, 0:NBLK])
                last.then_inc(S["top"], 1)
                dve.wait_ge(S["top"], it)
                dve.memset(top[:, :, TOPK:8], LOW).then_inc(S["top4"], 1)
                dve.wait_ge(S["top4"], it)
                hold()
                for j in range(NJ):
                    last = dve.match_replace(rep[:, j, :], top[:, j, :], lg[:, j, :], HIGH)
                last.then_inc(S["rep"], 1)
                dve.wait_ge(S["rep"], it)
                tt(mask[:], rep[:, :, 0:NBLK], lg[:, :, 0:NBLK], ALU.is_gt).then_inc(S["mask"], 1)

            def a_ffn(b, i):
                dve.wait_ge(S["m_ps"], b * 4 + (i + 1))
                dve.wait_ge(S["hg"], b * 4 + (i + 1))
                if i >= 2:
                    dve.wait_ge(S["h_hi"], b * 4 + (i - 1))
                tt(hm[i % 2], bank[4][:], hg[i % 2], ALU.mult).then_inc(S["hm"], 1)
                for h in range(4 * i, 4 * i + 4):
                    dve.wait_ge(S["s_ps"], b * H + (h + 1))
                    dve.tensor_reduce(nm[:, :, h:h + 1], bank[3 * (h % 2)][:].rearrange("p (j t) -> p j t", j=NJ), AX.X, ALU.max).then_inc(S["max"], 1)
                    if h % 4 == 1:
                        dve.wait_ge(S["h_hi"], b * 4 + (i + 1))
                        tt(h_lo[:, i % 2, :], hm[i % 2], h_hi[:, i % 2, :].bitcast(F32), ALU.subtract).then_inc(S["h_lo"], 1)

            def a_maxima(b):
                dve.wait_ge(S["max"], (b + 1) * H)
                ts(nm_sp[:, :, 0:H], nm[:], -1.0, None, ALU.mult).then_inc(S["nm_hi"], 1)
                dve.wait_ge(S["nm_hi"], b + 1)
                stt(nm_sp[:, :, H:2 * H], nm[:], -1.0, nm_sp[:, :, 0:H], ALU.mult, ALU.subtract).then_inc(S["nm_sp"], 1)

            def a_bias(b):
                for j in range(NJ):
                    x_j = x_all[:, bass.ds(b * NJ + j, 1), :].rearrange("p o d -> p (o d)")
                    tt(x_j, x_j, bo_b[:], ALU.add).then_inc(S["x_bo"], 1)

            def a_normalize(b):
                dve.wait_ge(S["ot_ps"], b + 1)
                for j in range(NJ):
                    o = bank[3 * j][:].rearrange("p (g h q e) -> p g h q e", g=G, h=2, q=4)
                    last = dve.reciprocal(rden[:, j, :].rearrange("p (g h q) -> p g h q", g=G, h=2), o[:, :, :, :, HD])
                last.then_inc(S["rden"], 1)
                dve.wait_ge(S["rden"], b + 1)
                for j in range(NJ):
                    o = bank[3 * j][:].rearrange("p (g h q e) -> p g h q e", g=G, h=2, q=4)
                    r = rden[:, j, :].rearrange("p (g h q) -> p g h q", g=G, h=2)
                    dst = cat[:, j * D:(j + 1) * D].rearrange("p (g q h d) -> p g h q d", g=G, q=4, h=2)
                    for g in range(G):
                        last = tt(dst[:, g], o[:, g, :, :, 0:HD], r[:, g].unsqueeze(3).to_broadcast([P, 2, 4, HD]), ALU.mult)
                last.then_inc(S["cat"], 1)

            def a_residual(b):
                low_part(t_lo, bank[2][:], t_hi, "c_lo", "c_hi", b + 1)
                x_b = x_all[:, bass.ds(b * NJ, NJ), :]
                dve.wait_ge(S["x_bo"], (b + 1) * NJ)
                dve.wait_ge(S["out0"], b + 1)
                tt(x_b, bank[1][:].rearrange("p (j d) -> p j d", j=NJ), x_b, ALU.add).then_inc(S["x1"], 1)

            def b_rotate(b):
                it = b + 1
                dve.wait_ge(S["g1_t"], it)
                dve.tensor_copy(lg1[:, :, 0:E], bank[6][:, 0:NJ * E].rearrange("p (j e) -> p j e", j=NJ)).then_inc(S["lg1"], 1)
                dve.wait_ge(S["silu"], it * 2)
                for q in range(2):
                    for j in range(NJ):
                        cols = slice(q * 512 + j * D, q * 512 + (j + 1) * D)
                        s, u, v = (t[:, cols].rearrange("p (h e) -> p h e", h=H) for t in (a1, c1, b1))
                        cos, sin = (consts[n][:, j, :].unsqueeze(1).to_broadcast([P, H, HD]) for n in ("cos1", "sin1"))
                        tt(u, s, cos, ALU.mult)
                        for x, y in ((slice(0, HD // 2), slice(HD // 2, HD)), (slice(HD // 2, HD), slice(0, HD // 2))):
                            last = tt(v[:, :, x], s[:, :, y], sin[:, :, x], ALU.mult)
                last.then_inc(S["rot_uv"], 1)
                dve.wait_ge(S["rot_uv"], it)
                tt(c1, c1, b1, ALU.add).then_inc(S["rot"], 1)
                dve.wait_ge(S["rot"], it)
                tt(kd, c1[:, 512:512 + D], consts["decay_k"][:], ALU.mult).then_inc(S["kd"], 1)

            def b_parts(b):
                it = b + 1
                dve.wait_ge(S["qt_ps"], it)
                dve.tensor_copy(a1[:, 0:512], bank[6][:]).then_inc(S["qt"], 1)
                dve.wait_ge(S["kt_ps"], it)
                dve.tensor_copy(a1[:, 512:1024], bank[5][:]).then_inc(S["qt"], 1)
                dve.wait_ge(S["qt"], it * 2)
                bf16_parts(a1, b1, 1024, "qk1_sp", it)
                dve.wait_ge(S["qk1_sp"], it)
                tt(qd.rearrange("p (c t) -> p c t", c=NC), a1[:, 0:512].rearrange("p (c t) -> p c t", c=NC)[:, :, P:T],
                   consts["decay_q"][:], ALU.mult).then_inc(S["qd"], 1)

            def b_combine(b):
                it = b + 1
                dve.wait_ge(S["lg1"], it)
                hold()
                for j in range(NJ):
                    last = dve.max(top[:, j, :], lg1[:, j, 0:E])
                last.then_inc(S["top_e"], 1)
                dve.wait_ge(S["top_e"], it)
                tt(cw[:, :, 2, 0:1], top[:, :, 0:1], top[:, :, 1:2], ALU.add).then_inc(S["top_sum"], 1)
                dve.wait_ge(S["top_sum"], it)
                dve.memset(top[:, :, TOPE:8], LOW).then_inc(S["top2"], 1)
                dve.wait_ge(S["top2"], it)
                hold()
                for j in range(NJ):
                    dve.match_replace(rep[:, j, 0:16], top[:, j, :], lg1[:, j, :], HIGH)
                    last = ts(cw[:, j, 0, :], lg1[:, j, 0:E], 2.0, cw[:, j, 2, 0:1], ALU.mult, ALU.subtract)
                last.then_inc(S["cw_d"], 1)
                dve.wait_ge(S["cw_d"], it)
                tt(cw[:, :, 2, :], rep[:, :, 0:E], lg1[:, :, 0:E], ALU.is_gt).then_inc(S["cw_sel"], 1)
                dve.wait_ge(S["cw_tanh"], it)
                ts(cw[:, :, 3, :], cw[:, :, 1, :], 0.5, 0.5, ALU.mult, ALU.add).then_inc(S["cw_sig"], 1)
                dve.wait_ge(S["cw_sig"], it)
                tt(cw[:, :, 0, :], cw[:, :, 3, :], cw[:, :, 2, :], ALU.mult).then_inc(S["cw"], 1)
                dve.wait_ge(S["cw"], it)
                dve.tensor_copy(cw_sp[:, :, 0:E], cw[:, :, 0, :]).then_inc(S["cw_h"], 1)
                dve.wait_ge(S["cw_h"], it)
                tt(cw[:, :, 1, :], cw[:, :, 0, :], cw_sp[:, :, 0:E], ALU.subtract).then_inc(S["cw_r"], 1)
                dve.wait_ge(S["cw_r"], it)
                dve.tensor_copy(cw_sp[:, :, E:2 * E], cw[:, :, 1, :]).then_inc(S["cw_m"], 1)
                dve.wait_ge(S["cw_m"], it)
                tt(cw_sp[:, :, 2 * E:3 * E], cw[:, :, 1, :], cw_sp[:, :, E:2 * E], ALU.subtract).then_inc(S["cw_sp"], 1)

            def b_state(b):
                dve.wait_ge(S["qd"], b + 1)
                dve.wait_ge(S["kv_ps"], b + 1)
                for c in range(NC):
                    last = tt(state[:, c * P:(c + 1) * P], bank[7][:, c * P:(c + 1) * P], consts["blockdiag"][:], ALU.mult)
                last.then_inc(S["state"], 1)

            def b_attend(b):
                for n in range(8):
                    four = n % 4
                    dve.wait_ge(S["s1_ps"], b * 8 + (n + 1))
                    if n >= 3:
                        dve.wait_ge(S["oi"], b * 8 + (n - 2))
                    tt(ring1[n % 3].rearrange("p (h t) -> p h t", h=4), bank[5 + n % 2][:].rearrange("p (h t) -> p h t", h=4),
                       consts["decay"][:, four * 4:(four + 1) * 4, :], ALU.mult).then_inc(S["sc"], 1)
                dve.wait_ge(S["tg"], b + 1)
                ts(tg, tg, 0.5, 0.5, ALU.mult, ALU.add).then_inc(S["gate"], 1)

            def b_gated_norm(b):
                it = b + 1
                o_sb = a1[:, 0:512]
                dve.wait_ge(S["oit_ps"], it)
                dve.wait_ge(S["inter"], it)
                dve.wait_ge(S["gate"], it)
                for j in range(NJ):
                    o = bank[5 + j][:].rearrange("p (h e) -> p h e", h=H)[:, :, 0:HD]
                    o_j = o_sb[:, j * D:(j + 1) * D].rearrange("p (h e) -> p h e", h=H)
                    if j == 0:
                        tt(o_j, o, tg[:, 0:D].rearrange("p (h e) -> p h e", h=H), ALU.mult).then_inc(S["gated"], 1)
                    else:
                        tt(o_j, o, inter.rearrange("p (h e) -> p h e", h=H), ALU.add).then_inc(S["o1_sum"], 1)
                dve.wait_ge(S["o1_sum"], it)
                tt(o_sb[:, D:2 * D], o_sb[:, D:2 * D], tg[:, D:2 * D], ALU.mult).then_inc(S["gated"], 1)
                dve.wait_ge(S["gated"], it * 2)
                tt(c1[:, 512:1024], o_sb, o_sb, ALU.mult).then_inc(S["sq"], 1)
                dve.wait_ge(S["sq"], it)
                dve.tensor_reduce(ms, c1[:, 512:1024].rearrange("p (h e) -> p h e", e=HD), AX.X, ALU.add).then_inc(S["ms"], 1)
                dve.wait_ge(S["ms"], it)
                ts(ms, ms, 1.0 / HD, None, ALU.mult).then_inc(S["ms_mean"], 1)
                dve.wait_ge(S["ms_mean"], it)
                r = rsqrt(ms, NJ * H, EPS_RMS, it, "rms_rs")
                tt(c1[:, 512:1024].rearrange("p (h e) -> p h e", e=HD), o_sb.rearrange("p (h e) -> p h e", e=HD),
                   r.unsqueeze(2).to_broadcast([P, NJ * H, HD]), ALU.mult).then_inc(S["normed"], 1)
                dve.wait_ge(S["normed"], it)
                for j in range(NJ):
                    last = tt(cat1[:, j * D:(j + 1) * D], c1[:, 512 + j * D:512 + (j + 1) * D], nw_b[:], ALU.mult)
                last.then_inc(S["og"], 1)

            def b_residual(b):
                dve.wait_ge(S["t1_kept"], (b + 1) * 2)
                low_part(t1_lo, bank[7][:], t1_hi, "g_lo", "g_hi", b + 1)
                x_b = x_all[:, bass.ds(b * NJ, NJ), :]
                dve.wait_ge(S["out1"], b + 1)
                tt(x_b, bank[5][:].rearrange("p (j d) -> p j d", j=NJ), x_b, ALU.add).then_inc(S["x2"], 1)

            dve.wait_ge(S["x_in0"], 16)
            layernorm(0, xn, "xn")
            a, z = SPAN[0]
            dve.wait_ge(S["w_hi"], 1)
            tt(w_lo[:, a:z], arena[:, a:z], w_hi[:, a:z].bitcast(F32), ALU.subtract).then_inc(S["w_lo0"], 1)
            low_part(t_lo, bank[0][:], t_hi, "t_lo", "t_hi", 1)
            dve.wait_ge(S["c0_in"], 16 * len(EARLY))
            dve.wait_ge(S["b_in"], 16 * 2)
            a_rope(0)
            dve.wait_ge(S["ones"], 4)
            a_router(0)
            for i in range(4):
                a_ffn(0, i)
            a_maxima(0)
            dve.wait_ge(S["c1_in"], 16 * (len(consts) - len(EARLY) + 2))
            a_bias(0)
            a_normalize(0)
            a_residual(0)
            dve.wait_ge(S["x_in1"], 16 * (B - 1))
            dve.wait_ge(S["x1"], 1)
            dve.wait_ge(S["w_lo"], len(GROUPS) - 1)
            dve.wait_ge(S["ones1"], 2)
            with dve.Fori(1, B) as b:
                layernorm(b, xn, "xn")
                layernorm(b - 1, xn1, "xn1")
                low_part(t_lo, bank[0][:], t_hi, "t_lo", "t_hi", b + 1)
                low_part(t1_lo, bank[5][:], t1_hi, "t1_lo", "t1_hi", b)
                a_rope(b)
                a_router(b)
                b_rotate(b - 1)
                a_ffn(b, 0)
                a_ffn(b, 1)
                b_parts(b - 1)
                a_ffn(b, 2)
                a_ffn(b, 3)
                a_maxima(b)
                b_combine(b - 1)
                b_state(b - 1)
                b_attend(b - 1)
                a_bias(b)
                b_gated_norm(b - 1)
                a_normalize(b)
                b_residual(b - 1)
                a_residual(b)
                dve.wait_ge(S["x1"], b + 1)
            layernorm(B - 1, xn1, "xn1")
            low_part(t1_lo, bank[5][:], t1_hi, "t1_lo", "t1_hi", B)
            b_rotate(B - 1)
            b_parts(B - 1)
            b_combine(B - 1)
            b_state(B - 1)
            b_attend(B - 1)
            b_gated_norm(B - 1)
            b_residual(B - 1)
            dve.wait_ge(S["x2"], B)
            dve.memset(zeros, 0.0).then_inc(S["zeros"], 1)
            def two_experts(e2):
                for u in range(8):
                    dve.wait_ge(S["e_s"], e2 * 8 + (u + 1))
                    dve.wait_ge(S["h1_ps"], e2 * 8 + (u + 1))
                    tt(e_p[u % 2], bank[1][:], e_s[u % 2], ALU.mult).then_inc(S["e_t"], 1)
                    dve.wait_ge(S["e_t"], e2 * 8 + (u + 1))
                    dve.wait_ge(S["cwb"], e2 * 4 + (u // 2 + 1))
                    tt(e_m[u % 2], e_p[u % 2], cwb[(u // 2) % 2], ALU.mult).then_inc(S["e_m"], 1)
                    dve.wait_ge(S["eh_hi"], e2 * 8 + (u + 1))
                    tt(h_lo[:, u % 2, :], e_m[u % 2], h_hi[:, u % 2, :].bitcast(F32), ALU.subtract).then_inc(S["eh_lo"], 1)

            with dve.Fori(0, E // 2 - 1) as e2:
                two_experts(e2)
            two_experts(E // 2 - 1)
            dve.wait_ge(S["e_out"], 8 * (E // 2 + 1))
            for i in range(B):
                x_i = x_all[:, i * NJ:(i + 1) * NJ, :].rearrange("p j d -> p (j d)")
                tt(x_i, bank[4 + i][:], x_i, ALU.add).then_inc(S["y"], 1)


def constants():
    f, bf = np.float32, np.dtype(mybir.dt.np(BF16))
    c = {"ident_f": np.eye(P, dtype=f), "ident_b": np.eye(P, dtype=bf)}
    d = np.arange(P) % HD
    inv0 = (f(1.0) / np.power(f(1250), np.arange(0, HD, 2, dtype=f) / f(HD))).astype(f)
    ang0 = (np.arange(T, dtype=f)[:, None] * inv0[None, :]).astype(f)
    ang0 = np.concatenate([ang0, ang0], -1)
    c["cos0"] = np.cos(ang0).astype(f).T[d]
    c["sin0"] = (np.sin(ang0).astype(f) * np.where(np.arange(HD) < HD // 2, f(-1), f(1))).T[d]
    inv1 = np.power(f(10000.0), f(-2.0) * np.arange(HD // 2, dtype=f) / f(HD)).astype(f)
    ang1 = (np.arange(T, dtype=f)[:, None] * inv1[None, :]).astype(f)
    cos1, sin1 = np.cos(ang1).astype(f), np.sin(ang1).astype(f)

    def tokens(a):
        return a.reshape(NJ, P, HD).transpose(1, 0, 2)

    c["cos1"] = tokens(np.concatenate([cos1, cos1], -1))
    c["sin1"] = tokens(np.concatenate([-sin1, sin1], -1))
    lam = -(f(2.0) ** (f(-8.0) * (np.arange(H, dtype=f) + f(1.0)) / f(H)))
    i = np.arange(P, dtype=f)
    diff = i[None, :] - i[:, None]
    c["decay"] = np.where(diff[:, None, :] >= 0, np.exp(lam[None, :, None] * np.maximum(diff, 0)[:, None, :]), f(0))
    head = np.arange(D) // HD
    c["decay_q"] = np.exp(lam[head][:, None] * (i[None, :] + f(1))).reshape(NC, P, P).transpose(1, 0, 2)
    c["decay_k"] = np.exp(lam[head][None, :] * (f(P - 1) - i[:, None]))
    c["blockdiag"] = (np.arange(P)[:, None] // HD == np.arange(P)[None, :] // HD).astype(bf)
    blk = np.zeros((NBLK, FF // P, P))
    for m in range(FF // P):
        for p in range(P):
            blk[(m * P + p) // BS, m, p] = 1
    c["sel_blk"] = blk.astype(bf)
    sel = np.zeros((P, E, P))
    for part in range(3):
        for e in range(E):
            sel[part * E + e, e, :] = 1
    c["sel_exp"] = sel.astype(bf)
    return {"c_" + k: np.ascontiguousarray(v if v.dtype == bf else v.astype(f)) for k, v in c.items()}


def layout(x):
    x = {k: np.asarray(v) for k, v in x.items()}
    perm = np.arange(D).reshape(-1, 2, HD // 2)[:, ::-1].reshape(-1)
    permk = perm[:G * HD]
    wk, bk = x["L0_attn_wk"], x["L0_attn_bk"]
    bq = x["L0_attn_bq"]
    four = P // (G * HD)

    def bias(q, k):
        return np.stack([q[:P], q[P:], np.tile(k, four)], 1)

    ex = np.stack([x["L1_ffn_wi_0"], x["L1_ffn_wi_1"], x["L1_ffn_wo"]], 1)
    a = {
        "x": x["L0_attn_x"].reshape(NTOK, D),
        "wq": x["L0_attn_wq"], "wqp": x["L0_attn_wq"][:, perm],
        "wk": np.tile(wk, (1, four)), "wkp": np.tile(wk[:, permk], (1, four)),
        "wvr": np.concatenate([x["L0_attn_wv"], x["L0_ffn_Wr"].T], 1),
        "w1": x["L0_ffn_W1"].T, "w2": x["L0_ffn_W2"].T, "wo": x["L0_attn_wo"],
        "wq1": x["L1_attn_Wq"], "wk1": x["L1_attn_Wk"], "wv1": x["L1_attn_Wv"],
        "wg1": np.tile(x["L1_attn_Wg1"], (1, P // HD)), "gk": x["L1_ffn_gate_kernel"], "wo1": x["L1_attn_Wo"],
        "experts": ex.reshape(E, 3, NC, P, D).transpose(0, 3, 1, 2, 4).reshape(E, P, EW),
        "bv": x["L0_attn_bv"], "br": x["L0_ffn_br"], "bo": x["L0_attn_bo"], "nw": x["L1_attn_norm_weight"],
        "c_bqk": bias(bq, bk), "c_bqkp": bias(bq[perm], bk[permk]), "c_wg2": x["L1_attn_Wg2"],
    }
    return {k: np.ascontiguousarray(v) for k, v in a.items()}


def kernel(**inputs):
    import concourse.bacc as _bacc
    from concourse.bass_utils import run_bass_kernel_spmd as _run

    arrays = {f"in_{k}": v for k, v in {**layout(inputs), **constants()}.items()}
    nc = _bacc.Bacc("TRN2", target_bir_lowering=False, num_devices=1)
    aps = {k[3:]: nc.dram_tensor(k, v.shape, mybir.dt.from_np(v.dtype), kind="ExternalInput").ap() for k, v in arrays.items()}
    out = nc.dram_tensor("out_0", (NTOK, D), F32, kind="ExternalOutput").ap()
    build(nc, aps, out)
    r = _run(nc, [arrays], core_ids=[0])
    return r.results[0]["out_0"].reshape(B, T, D)
```

```python
from contextlib import ExitStack

import numpy as np

import concourse.bass as bass
from concourse import mybir

F32 = mybir.dt.float32
F32R = mybir.dt.float32r
BF16 = mybir.dt.bfloat16
I32 = mybir.dt.int32
ALU = mybir.AluOpType
ACT = mybir.ActivationFunctionType
AX = mybir.AxisListType

P = 128
B, T, D = 4, 256, 256
NJ = T // P
NC = D // P
H, G, HD = 16, 2, 16
HPG = H // G
NBLK, BS, TOPK = 16, 64, 4
FF = NBLK * BS
E, TOPE = 8, 2
NTOK = B * T
EPS_LN = 1e-5
EPS_RMS = 1e-6
LOW = -3.0e38
HIGH = 3.0e38
Q_PARTS = (0, 0, 0, 1, 1, 2)
K_PARTS = (0, 1, 2, 0, 1, 0)
NPART = len(Q_PARTS)
KS = NPART * HD
KM = KS + 2

GROUPS = [
    [("wq", NC, D), ("wqp", NC, D), ("wk", NC, P), ("wkp", NC, P), ("wvr", NC, G * HD + NBLK)],
    [("w1", NC, FF)],
    [("w2", FF // P, D), ("wo", NC, D)],
    [("wq1", NC, D), ("wk1", NC, D), ("wv1", NC, D), ("wg1", NC, P), ("gk", NC, E), ("wo1", NC, D)],
]
PLACE = {}
_at = 0
for _g in GROUPS:
    for _n, _r, _c in _g:
        PLACE[_n] = (_at, _r, _c)
        _at += _r * _c
NW = _at
SPAN = [(PLACE[g[0][0]][0], PLACE[g[-1][0]][0] + g[-1][1] * g[-1][2]) for g in GROUPS]
SLOTS = 4
HALF = NTOK // 2
UNITS = 2 * E * NC
ORDER = list(range(E)) + list(range(SLOTS, E)) + list(range(SLOTS))
LOADS = ORDER[:E] + ORDER[E + SLOTS:]
EW = 3 * NC * D


class Signals(dict):

    def __init__(self, nc, ctx):
        super().__init__()
        self.nc, self.ctx = nc, ctx

    def __missing__(self, name):
        self[name] = self.ctx.enter_context(self.nc.semaphore(name))
        return self[name]


def build(nc, A, out):
    with ExitStack() as ctx:
        S = Signals(nc, ctx)

        def sb(name, shape, dt=F32):
            return ctx.enter_context(nc.sbuf_tensor(name, shape, dt))

        bank = [ctx.enter_context(nc.psum_tensor(f"bank{i}", [P, 512], F32)) for i in range(8)]
        qk_dram = nc.dram_tensor("qk_scratch", [3, 3, P, T], BF16, kind="Internal").ap()
        cw_dram = nc.dram_tensor("cw_scratch", [E, NTOK], F32, kind="Internal").ap()
        nm_dram = nc.dram_tensor("nm_scratch", [2 * H, T], BF16, kind="Internal").ap()
        qk1_dram = nc.dram_tensor("qk1_scratch", [3, 4, P, T], BF16, kind="Internal").ap()

        w_hi, w_lo = sb("w_hi", [P, NW], F32R), sb("w_lo", [P, NW], F32R)
        arena = sb("arena", [P, NW])
        e_stage = sb("e_stage", [P, 2, EW])
        consts = {}
        for name, shape, dt in [
            ("ident_f", [P, P], F32), ("ident_b", [P, P], BF16), ("cos0", [P, T], F32),
            ("sin0", [P, T], F32), ("bqk", [P, 3], F32), ("bqkp", [P, 3], F32),
            ("cos1", [P, NJ, HD], F32), ("sin1", [P, NJ, HD], F32), ("decay", [P, H, P], F32),
            ("decay_q", [P, NC, P], F32), ("decay_k", [P, D], F32), ("blockdiag", [P, P], BF16),
            ("sel_blk", [NBLK, FF // P, P], BF16),
            ("wg2", [HD, D], F32),
        ]:
            consts[name] = sb("c_" + name, shape, dt)
        bv_b = sb("bv_b", [P, G * HD])
        br_b = sb("br_b", [P, NBLK])
        bo_b = sb("bo_b", [P, D])
        nw_c = sb("nw_c", [P, NC])
        ident_f, ident_b = consts["ident_f"], consts["ident_b"]

        x_all = sb("x_all", [P, B * NJ, D])
        t_hi_all = sb("t_hi_all", [P, NC, NTOK], F32R)
        t_lo_all = sb("t_lo_all", [P, NC, NTOK], F32R)
        cw_t = sb("cw_t", [E, NTOK])
        tick = sb("tick", [P, 1])
        stats = sb("stats", [P, B * NJ, 6])
        mv = sb("mv", [P, NJ, 2])
        mv0 = sb("mv0", [P, B * NJ, 2])
        rstd0 = sb("rstd0", [P, B * NJ])
        rs = sb("rs", [P, 4, NJ * H + NJ])
        t_hi, t_lo = sb("t_hi", [P, NC * T], F32R), sb("t_lo", [P, NC * T], F32R)
        t1_hi, t1_lo = sb("t1_hi", [P, NC * T], F32R), sb("t1_lo", [P, NC * T], F32R)
        qk_sp = sb("qk_sp", [P, 3, 4 * T], BF16)
        q_hat = sb("q_hat", [P, H, T], BF16)
        q_hat1 = sb("q_hat1", [P, H, T], BF16)
        k_hat = sb("k_hat", [P, G, T], BF16)
        k_hat1 = sb("k_hat1", [P, H, T], BF16)
        v_aug = sb("v_aug", [P, NJ, G, 2 * HD])
        lg = sb("lg", [P, NJ, NBLK + 8])
        top = sb("top", [P, NJ, 8])
        rep = sb("rep", [P, NJ, NBLK + 8])
        mask = sb("mask", [P, NJ, NBLK], BF16)
        h_hi, h_lo = sb("h_hi", [P, 2, 512], F32R), sb("h_lo", [P, 2, 512], F32R)
        nm = sb("nm", [P, NJ, H])
        rden = nm

        def part(at, n=512):
            return arena[:, at:at + n]

        area0 = e_stage[:].rearrange("p k n -> p (k n)")
        a0, b0, c0 = (area0[:, 3 * T * i:3 * T * (i + 1)] for i in range(3))
        mask_t = area0[0:NBLK, 9 * T + 512:9 * T + 640].bitcast(BF16)
        nm_t = area0[0:2 * H, 9 * T + 640:9 * T + 768].bitcast(BF16)
        nm_sp = c0[:, 0:NJ * H].bitcast(BF16).rearrange("p (j h) -> p j h", j=NJ)
        cat, xn = a0[:, 0:NJ * D], b0[:, 0:NJ * D]
        ring = [area0[:, 9 * T:9 * T + 512]] + [part(512 * i) for i in range(3)]
        osb = [part(1536), part(2048)]
        hg = [osb[0], ring[0]]
        hm = [ring[1], ring[2]]
        a1, b1, c1 = (part(2560 + 1024 * i, 1024) for i in range(3))
        xn1 = b1[:, 0:NJ * D]
        cat1 = a1[:, NJ * D:2 * NJ * D]
        ring1 = [part(5632 + 512 * i) for i in range(3)]
        kd = part(7168, D)
        v1 = part(7424, NJ * (D + HD)).rearrange("p (j n) -> p j n", j=NJ)
        g1_t = part(7968, T)[0:HD]
        lg1 = part(8224, NJ * 16).rearrange("p (j n) -> p j n", j=NJ)
        cw = part(8256, NJ * 4 * E).rearrange("p (j i e) -> p j i e", j=NJ, i=4)
        ms = part(8352, NJ * H)
        qd, state = b1[:, 0:D], b1[:, D:2 * D]
        inter = b1[:, 0:D]
        osb1 = [b1[:, 512:1024], c1[:, 512:1024]]
        tg = c1[:, 0:512]
        e_s, e_p = ([part(1024 * i + 512 * k) for k in range(2)] for i in range(2))
        cwb = q_hat[:].rearrange("p h t -> p (h t)").bitcast(F32).rearrange("p (e t) -> p e t", e=SLOTS)
        e_hi, e_lo = ([full[:, k * EW:(k + 1) * EW] for k in range(SLOTS)] for full in (w_hi, w_lo))

        def w(name, part_of, row, c0, c1):
            at, _, n = PLACE[name]
            return part_of[:, at + row * n + c0:at + row * n + c1]

        def mm3(pe, dst, lhs, rhs, first, last, lone_start=False):
            for i, (a, b) in enumerate(((0, 0), (0, 1), (1, 0))):
                ins = pe.matmul(dst, lhs[a], rhs[b], start=first and i == 0, stop=last and i == 2,
                                skip_group_check=True)
            return ins

        def wx(name, row, c0, c1):
            return w(name, w_hi, row, c0, c1), w(name, w_lo, row, c0, c1)

        def tx(c, j=None, hi=t_hi, lo=t_lo):
            a, b = (c * T, (c + 1) * T) if j is None else (c * T + j * P, c * T + (j + 1) * P)
            return hi[:, a:b], lo[:, a:b]

        def tx1(c, j=None):
            return tx(c, j, t1_hi, t1_lo)

        HALVES = ((slice(0, HD // 2), slice(HD // 2, HD)), (slice(HD // 2, HD), slice(0, HD // 2)))

        def rotation(q):
            tiles = [t[:, q * 512:(q + 1) * 512].rearrange("p (j h e) -> p j h e", j=NJ, h=H) for t in (a1, c1, b1)]
            tables = [consts[n][:].unsqueeze(2).to_broadcast([P, NJ, H, HD]) for n in ("cos1", "sin1")]
            return tiles + tables

        EARLY = ("ident_f", "cos0", "sin0", "bqk", "bqkp")

        BESIDE = 11

        AT = dict(gate=3, qk=3, combine=4, state=5, inter=6, attend=7, gated=9, roots=11, cat=13, project=14)

        SPLIT_AFTER = [(s, 2 * (s - SLOTS) + 3 + (E if s >= E else 0)) for s in range(SLOTS, len(LOADS))]

        block = ctx.enter_context(nc.Block())
        ex_dram = A["experts"]

        @block.sync
        def _(sp):
            for i in range(B):
                sp.dma_start(x_all[:, i * NJ:(i + 1) * NJ, :],
                             A["x"][i * T:(i + 1) * T, :].rearrange("(j p) d -> p j d", p=P)).then_inc(S[f"x_in{min(i, 1)}"], 16)
                if i < len(GROUPS):
                    for name, rows, cols in GROUPS[i]:
                        at = PLACE[name][0]
                        sp.dma_start(arena[:, at:at + rows * cols].rearrange("p (r n) -> p r n", r=rows),
                                     A[name].rearrange("(r p) n -> p r n", p=P)).then_inc(S[f"w_in{i}"], 16)

            def q_k_stacked(it, first=False):
                if not first:
                    sp.wait_ge(S["qk_sp"], it)
                for s in range(3):
                    if first:
                        sp.wait_ge(*((S["qk_sp_step"], 1), (S["qk_sp_step"], 3), (S["qk_sp"], 1))[s])
                    if s == 2 and not first:
                        sp.wait_ge(S["st_ps"], (it - 1) * 16)
                    sp.dma_start(qk_dram[s].rearrange("c p t -> p c t"),
                                 qk_sp[:, s, 0:3 * T].rearrange("p (c t) -> p c t", c=3)).then_inc(S["qk_out"], 16)
                sp.wait_ge(S["qk_out"], it * 48)
                for n in range(NPART):
                    sp.dma_start(k_hat[n * HD:(n + 1) * HD, :, :],
                                 qk_dram[K_PARTS[n], 2, 0:G * HD].rearrange("(g d) t -> d g t", d=HD)).then_inc(S["k_in"], 16)
                    sp.dma_start(q_hat[n * HD:(n + 1) * HD, :, :],
                                 qk_dram[Q_PARTS[n], 0:2].rearrange("c (h d) t -> d (c h) t", d=HD)).then_inc(S["q_in"], 16)

            def q_k_stacked1(it):
                for s, (name, count) in enumerate((("qt_hi", 2), ("qk1_step", 2), ("qk1_sp", 1))):
                    sp.wait_ge(S[name], it * count)
                    sp.dma_start(qk1_dram[s].rearrange("c p t -> p c t"),
                                 qk_sp[:, s, :].rearrange("p (c t) -> p c t", c=4)).then_inc(S["qk1_out"], 16)
                sp.wait_ge(S["qk1_out"], it * 48)
                for n in range(NPART):
                    sp.dma_start(k_hat1[n * HD:(n + 1) * HD, :, :],
                                 qk1_dram[K_PARTS[n], 2:4].rearrange("c (h d) t -> d (c h) t", d=HD)).then_inc(S["k1_in"], 16)
                    sp.dma_start(q_hat1[n * HD:(n + 1) * HD, :, :],
                                 qk1_dram[Q_PARTS[n], 0:2].rearrange("c (h d) t -> d (c h) t", d=HD)).then_inc(S["q1_in"], 16)

            q_k_stacked(1, True)
            q_k_stacked(2)
            with sp.Fori(1, B - 1) as b:
                q_k_stacked1(b)
                q_k_stacked(b + 2)
            q_k_stacked1(B - 1)

            def expert(s):
                if s >= 2:
                    sp.wait_ge(S[f"e_split{s % 2}"], s // 2)
                elif s == 1:
                    sp.wait_ge(S["ct_ps"], B)
                sp.dma_start(e_stage[:, (s + 1) % 2, :], ex_dram[LOADS[s]]).then_inc(S[f"e_in{s % 2}"], 16)

            def combine_out(half):
                sp.wait_ge(S["cw_t"], (half + 1) * B // 2)
                cols = slice(half * HALF, (half + 1) * HALF)
                sp.dma_start(cw_dram[:, cols], cw_t[:, cols]).then_inc(S["cw_out"], 16)
                sp.wait_ge(S["cw_out"], 16 * (half + 1))

            def combine_in(q):
                if q >= 2:
                    sp.wait_ge(S["e_p"], 4 * (q - 1))
                half, e = q // (E // 2), ORDER[2 * q]
                sp.dma_start(cwb[:, 2 * (q % 2):2 * (q % 2) + 2, :],
                             cw_dram[e:e + 2, half * HALF:(half + 1) * HALF].partition_broadcast(P)).then_inc(S[f"cwb{q % 2}"], 16)

            sp.wait_ge(S["ot_ps"], B)
            expert(0)
            expert(1)
            combine_out(0)
            combine_in(0)
            combine_in(1)
            expert(2)
            expert(3)
            expert(4)
            q_k_stacked1(B)
            expert(5)
            combine_in(2)
            expert(6)
            combine_in(3)
            expert(7)
            combine_out(1)
            combine_in(4)
            combine_in(5)
            for i in range(B // 2):
                sp.wait_ge(S["y"], i + 1)
                sp.dma_start(out[i * T:(i + 1) * T, :].rearrange("(j p) d -> p j d", p=P),
                             x_all[:, i * NJ:(i + 1) * NJ, :]).then_inc(S["stored"], 16)
            expert(8)
            expert(9)
            combine_in(6)
            expert(10)
            expert(11)
            combine_in(7)
            for i in range(B // 2, B):
                sp.wait_ge(S["y"], i + 1)
                sp.dma_start(out[i * T:(i + 1) * T, :].rearrange("(j p) d -> p j d", p=P),
                             x_all[:, i * NJ:(i + 1) * NJ, :]).then_inc(S["stored"], 16)
            sp.wait_ge(S["stored"], 16 * B)

        @block.gpsimd
        def _(pool):
            for dst, name in ((bv_b, "bv"), (br_b, "br")):
                pool.dma_start(dst[:], A[name].partition_broadcast(P)).then_inc(S["b_in"], 16)
            pool.memset(v_aug[:], 1.0).then_inc(S["ones"], 1)
            pool.memset(lg[:], LOW).then_inc(S["ones"], 1)
            pool.wait_ge(S["ones"], 2)
            pool.memset(k_hat[KS:P, :, :], 1.0).then_inc(S["ones"], 1)
            for name in consts:
                if name not in EARLY:
                    pool.dma_start(consts[name][:], A["c_" + name]).then_inc(S["c1_in"], 16)
            pool.dma_start(bo_b[:], A["bo"].partition_broadcast(P)).then_inc(S["c1_in"], 16)
            pool.dma_start(nw_c[:], A["nw"]).then_inc(S["c1_in"], 16)
            def keep(b):
                it = b + 1
                pool.wait_ge(S["t1_lo"], it)
                pool.wait_ge(S["t1_hi"], it)
                pool.tensor_copy(t_hi_all[:, :, bass.ds(b * T, T)],
                                 t1_hi[:].bitcast(F32).rearrange("p (c t) -> p c t", c=NC)).then_inc(S["t1_kept"], 1)
                pool.tensor_copy(t_lo_all[:, :, bass.ds(b * T, T)],
                                 t1_lo[:].bitcast(F32).rearrange("p (c t) -> p c t", c=NC)).then_inc(S["t1_kept"], 1)

            def unit(n):
                if n % 4 == 0:
                    pool.wait_ge(S[f"cwb{n // 4 % 2}"], 16 * (n // 8 + 1))
                if n >= 2:
                    pool.wait_ge(S["eh_lo"], n - 1)
                pool.wait_ge(S["e_s"], n + 1)
                pool.tensor_tensor(out=e_p[n % 2], in0=e_s[n % 2], in1=cwb[:, n // 2 % SLOTS, :], op=ALU.mult).then_inc(S["e_p"], 1)

            def expert_low(s, a, z, done):
                pool.tensor_tensor(out=e_lo[s % SLOTS][:, a:z], in0=e_stage[:, (s + 1) % 2, a:z], in1=e_hi[s % SLOTS][:, a:z].bitcast(F32), op=ALU.subtract).then_inc(S[done], 1)

            def bias(b):
                x_b = x_all[:, bass.ds(b * NJ, NJ), :]
                pool.wait_ge(S["xn"], b + 1)
                pool.tensor_tensor(out=x_b, in0=x_b, in1=bo_b[:].unsqueeze(1).to_broadcast([P, NJ, D]), op=ALU.add).then_inc(S["x_bo"], 1)

            def rotate_k(b):
                it = b + 1
                s, u, v, cos, sin = rotation(1)
                pool.wait_ge(S["silu"], it * 2)
                pool.tensor_tensor(out=u, in0=s, in1=cos, op=ALU.mult)
                for x, y in HALVES:
                    last = pool.tensor_tensor(out=v[:, :, :, x], in0=s[:, :, :, y], in1=sin[:, :, :, x], op=ALU.mult)
                last.then_inc(S["rotk_uv"], 1)
                pool.wait_ge(S["rotk_uv"], it)
                pool.tensor_tensor(out=c1[:, 512:1024], in0=c1[:, 512:1024], in1=b1[:, 512:1024], op=ALU.add).then_inc(S["rotk"], 1)
                pool.wait_ge(S["rotk"], it)
                pool.tensor_tensor(out=kd, in0=c1[:, 512:512 + D], in1=consts["decay_k"][:], op=ALU.mult).then_inc(S["kd"], 1)

            def hidden_low(b, first):
                for i in range(first, first + 2):
                    pool.wait_ge(S["h_hi"], b * 4 + (i + 1))
                    pool.tensor_tensor(out=h_lo[:, i % 2, :], in0=hm[i % 2], in1=h_hi[:, i % 2, :].bitcast(F32), op=ALU.subtract).then_inc(S["h_lo"], 1)

            def group_low(g):
                a, z = SPAN[g]
                pool.wait_ge(S["w_hi"], g + 1)
                pool.tensor_tensor(out=w_lo[:, a:z], in0=arena[:, a:z], in1=w_hi[:, a:z].bitcast(F32), op=ALU.subtract).then_inc(S["w_lo"], 1)

            pool.wait_ge(S["ones"], 3)
            group_low(1)
            group_low(2)
            at = PLACE["wo1"][0]
            wo1 = arena[:, at:at + NC * D].rearrange("p (c n) -> p c n", c=NC)
            pool.wait_ge(S["c1_in"], 16 * (len(consts) - len(EARLY) + 2))
            pool.wait_ge(S["w_in3"], 16 * len(GROUPS[3]))
            pool.tensor_tensor(out=wo1, in0=wo1, in1=nw_c[:].unsqueeze(2).to_broadcast([P, NC, D]), op=ALU.mult).then_inc(S["wo1_weighted"], 1)
            bias(0)
            hidden_low(0, 0)
            hidden_low(0, 2)
            group_low(3)
            pool.wait_ge(S["w_lo"], len(GROUPS) - 1)
            pool.memset(v1, 0.0).then_inc(S["ones1"], 1)
            pool.memset(lg1, LOW).then_inc(S["ones1"], 1)
            with pool.Fori(1, B) as b:
                keep(b - 1)
                hidden_low(b, 0)
                rotate_k(b - 1)
                bias(b)
                hidden_low(b, 2)
            pool.wait_ge(S["e_hi"], 1)
            expert_low(0, 0, NC * D, "first_wi_0")
            expert_low(0, NC * D, EW, "e_split0")
            keep(B - 1)
            unit(0)
            unit(1)
            rotate_k(B - 1)
            unit(2)
            unit(3)
            pool.wait_ge(S["e_hi"], 4)
            expert_low(3, 0, EW, "e_split1")
            for n in range(4, UNITS):
                unit(n)

        @block.tensor
        def _(pe):
            NV = G * HD + NBLK
            out0 = bank[1]

            def transposes(dst, src, sem, ident=ident_f):
                src = src.rearrange("p (j d) -> p j d", j=NJ)
                for c in range(NC):
                    for j in range(NJ):
                        last = pe.transpose(dst[:, c * T + j * P:c * T + (j + 1) * P],
                                            src[:, j, c * P:(c + 1) * P], ident[:])
                last.then_inc(S[sem], 1)

            def weights(g, first):
                if first:
                    pe.wait_ge(S["w_hi"], g + 1)
                    pe.wait_ge(S["w_lo0" if g == 0 else "w_lo"], max(g, 1))

            def a_turn(b, first=False):
                if first:
                    pe.wait_ge(S["c0_in"], 16 * len(EARLY))
                else:
                    pe.wait_ge(S["nm_t"], b)
                pe.wait_ge(S["xn"], b + 1)
                transposes(bank[4], xn, "t_ps")

            def a_qkv(b, first=False, beside=None):
                weights(0, first)
                if beside is not None:
                    pe.wait_ge(S["qt_hi"], beside * 2 + 2)
                pe.wait_ge(S["t_hi"], b + 1)
                pe.wait_ge(S["t_lo"], b + 1)
                for name, dst, n, at in (("wq", bank[4], 2, 0), ("wqp", bank[5], 2, 0), ("wk", bank[6], 1, 0), ("wkp", bank[6], 1, T)):
                    for s in range(n):
                        for c in range(NC):
                            last = mm3(pe, dst[:, at + s * T:at + (s + 1) * T], wx(name, c, s * P, (s + 1) * P), tx(c), c == 0, c == NC - 1)
                last.then_inc(S["qk_ps"], 1)

            def a_vr(b, vr=bank[4]):
                for j in range(NJ):
                    for c in range(NC):
                        last = mm3(pe, vr[:, j * NV:(j + 1) * NV], tx(c, j), wx("wvr", c, 0, NV), c == 0, c == NC - 1)
                last.then_inc(S["vr_ps"], 1)

            def a_mask(b, first=False):
                if first:
                    pe.wait_ge(S["c1_in"], 16 * (len(consts) - len(EARLY) + 2))
                    pe.wait_ge(S["ones"], 3)
                pe.wait_ge(S["mask"], b + 1)
                mt = bank[0][:].bitcast(BF16)
                for j in range(NJ):
                    last = pe.transpose(mt[0:NBLK, j * P:(j + 1) * P], mask[:, j, :], ident_b[:])
                last.then_inc(S["mask_ps"], 1)

            def a_ffn_out(b, i):
                pe.wait_ge(S["h_hi"], b * 4 + (i + 1))
                pe.wait_ge(S["h_lo"], b * 4 + (i + 1))
                for j in range(NJ):
                    for m in range(2):
                        at = m * T + j * P
                        last = mm3(pe, out0[:, j * D:(j + 1) * D],
                                   (h_hi[:, i % 2, at:at + P], h_lo[:, i % 2, at:at + P]),
                                   wx("w2", 2 * i + m, 0, D), i == 0 and j == 0 and m == 0, False)
                last.then_inc(S["ffn_out"], 1)

            def a_hidden(b, i, first=False):
                if i == 0:
                    weights(1, first)
                    pe.wait_ge(S["mask_t"], b + 1)
                if i >= 1:
                    pe.wait_ge(S["hm"], b * 4 + i)
                for m in range(2):
                    for c in range(NC):
                        last = mm3(pe, bank[2][:, m * T:(m + 1) * T],
                                   wx("w1", c, (2 * i + m) * P, (2 * i + m + 1) * P), tx(c), c == 0, c == NC - 1)
                last.then_inc(S["h_ps"], 1)
                for m in range(2):
                    last = pe.matmul(bank[4][:, m * T:(m + 1) * T], consts["sel_blk"][:, 2 * i + m, :], mask_t[:, :],
                                     start=True, stop=True)
                last.then_inc(S["m_ps"], 1)

            def a_scores(b, pair):
                if pair == 0:
                    pe.wait_ge(S["q_in"], (b + 1) * (16 * NPART))
                    pe.wait_ge(S["k_in"], (b + 1) * (16 * NPART))
                for h in range(2 * pair, 2 * pair + 2):
                    if h >= 2:
                        pe.wait_ge(S["max"], b * H + (h - 1))
                    for j in range(NJ):
                        last = pe.matmul(bank[3 * (h % 2)][:, j * T:(j + 1) * T], q_hat[0:KS, h, j * P:(j + 1) * P],
                                         k_hat[0:KS, h // HPG, :], start=True, stop=True)
                    last.then_inc(S["s_ps"], 1)

            def a_maxima(b):
                pe.wait_ge(S["nm_sp"], b + 1)
                nt = bank[4][:].bitcast(BF16)
                for j in range(NJ):
                    last = pe.transpose(nt[0:2 * H, j * P:(j + 1) * P], nm_sp[:, j, :], ident_b[:])
                last.then_inc(S["nm_ps"], 1)

            def attend(b, more=True, beside=None):
                pe.wait_ge(S["nm_in"], (b + 1) * 16)
                for n in range(18):
                    if n < 16:
                        a_score(b, n)
                    if n == 8 and beside is not None:
                        b_inter(beside)
                    if n == 10 and more:
                        pe.wait_ge(S["rope"], b + 2)
                    if n >= 2:
                        a_probs_v(b, n - 2)
                    if beside is not None and n >= BESIDE:
                        b_step(beside, n - BESIDE)

            def a_score(b, n):
                u, kt = divmod(n, NJ)
                g, quarter = divmod(u, 4)
                if n >= 2:
                    pe.wait_ge(S["probs"], b * 16 + (n - 1))
                pe.matmul(bank[3 * (n % 2)][:, :], k_hat[0:KM, g, kt * P:(kt + 1) * P],
                          q_hat[0:KM, g * HPG + 2 * quarter:g * HPG + 2 * quarter + 2, :],
                          start=True, stop=True).then_inc(S["st_ps"], 1)

            def a_probs_v(b, n):
                u, kt = divmod(n, NJ)
                g, quarter = divmod(u, 4)
                pe.wait_ge(S["probs"], b * 16 + (n + 1))
                pe.matmul(bank[2 + 2 * g][32 * quarter:32 * quarter + 32, :], v_aug[:, kt, g, :], ring[n % 4],
                          start=kt == 0, stop=kt == NJ - 1).then_inc(S["pv"], 1)

            def a_turn_back(b):
                for g in range(G):
                    pe.wait_ge(S["osb"], b * G + (g + 1))
                    for h2 in range(2):
                        for j in range(NJ):
                            at = (g * 2 + h2) * P
                            last = pe.transpose(bank[3 * j][:, at:at + P], osb[g][:, h2 * T + j * P:h2 * T + (j + 1) * P], ident_f[:])
                last.then_inc(S["ot_ps"], 1)

            def a_turn_cat(b):
                pe.wait_ge(S["cat"], b + 1)
                transposes(bank[2], cat, "ct_ps")

            def a_project(b):
                pe.wait_ge(S["c_hi"], b + 1)
                pe.wait_ge(S["c_lo"], b + 1)
                for j in range(NJ):
                    for c in range(NC):
                        last = mm3(pe, out0[:, j * D:(j + 1) * D], tx(c, j, h_hi[:, 0, :], h_lo[:, 0, :]), wx("wo", c, 0, D), False, c == NC - 1)
                last.then_inc(S["out0"], 1)

            def b_turn(b):
                pe.wait_ge(S["xn1"], b + 1)
                transposes(bank[6], xn1, "t1_ps")

            def b_ready(b):
                pe.wait_ge(S["t1_hi"], b + 1)
                pe.wait_ge(S["t1_lo"], b + 1)

            def b_product(b, name):
                dst = bank[{"wq1": 6, "wk1": 7, "wv1": 5}[name]]
                for j in range(NJ):
                    for c in range(NC):
                        last = mm3(pe, dst[:, j * D:(j + 1) * D], tx1(c, j), wx(name, c, 0, D), c == 0, c == NC - 1)
                last.then_inc(S[name + "_ps"], 1)

            def b_narrow(b):
                pe.wait_ge(S["silu"], b * 2 + 1)
                for j in range(NJ):
                    for c in range(NC):
                        mm3(pe, bank[6][:, j * E:(j + 1) * E], tx1(c, j), wx("gk", c, 0, E), c == 0, c == NC - 1)
                for c in range(NC):
                    last = mm3(pe, bank[6][:, T:2 * T], wx("wg1", c, 0, P), tx1(c), c == 0, c == NC - 1)
                last.then_inc(S["g1_ps"], 1)

            def b_gate(b):
                pe.wait_ge(S["g1_t"], b + 1)
                pe.wait_ge(S["silu"], b * 2 + 2)
                for j in range(NJ):
                    last = pe.matmul(bank[7][:, j * D:(j + 1) * D], g1_t[:, j * P:(j + 1) * P], consts["wg2"][:, :], start=True, stop=True)
                last.then_inc(S["gate_ps"], 1)

            def b_turn_qk(b):
                pe.wait_ge(S["v1"], b + 1)
                pe.wait_ge(S["rot"], b + 1)
                pe.wait_ge(S["rotk"], b + 1)
                transposes(bank[6], c1[:, 0:512], "qt_ps")
                transposes(bank[5], c1[:, 512:1024], "kt_ps")

            def b_turn_combine(b):
                pe.wait_ge(S["cw"], b + 1)
                pe.wait_ge(S["tg"], b + 1)
                for j in range(NJ):
                    last = pe.transpose(bank[7][0:E, j * P:(j + 1) * P], cw[:, j, 0, :], ident_f[:])
                last.then_inc(S["cwt_ps"], 1)

            def b_state(b):
                pe.wait_ge(S["cw_t"], b + 1)
                for c in range(NC):
                    last = pe.matmul(bank[7][:, c * P:(c + 1) * P], kd[:, c * P:(c + 1) * P], v1[:, 0, c * P:(c + 1) * P], start=True, stop=True)
                last.then_inc(S["kv_ps"], 1)

            def b_inter(b):
                pe.wait_ge(S["state"], b + 1)
                for c in range(NC):
                    last = pe.matmul(bank[7][:, (2 + c) * P:(3 + c) * P], qd[:, c * P:(c + 1) * P], state[:, c * P:(c + 1) * P], start=True, stop=True)
                last.then_inc(S["inter_ps"], 1)

            def b_score(b, n):
                j, four = divmod(n, 4)
                if n == 0:
                    pe.wait_ge(S["q1_in"], (b + 1) * (16 * NPART))
                    pe.wait_ge(S["k1_in"], (b + 1) * (16 * NPART))
                if n >= 2:
                    pe.wait_ge(S["sc"], b * 8 + (n - 1))
                for i in range(4):
                    h = four * 4 + i
                    last = pe.matmul(bank[5 + n % 2][:, i * P:(i + 1) * P], k_hat1[0:KS, h, j * P:(j + 1) * P],
                                     q_hat1[0:KS, h, j * P:(j + 1) * P], start=True, stop=True)
                last.then_inc(S["s1_ps"], 1)

            def b_intra(b, n):
                j, four = divmod(n, 4)
                if n == 0:
                    pe.wait_ge(S["inter"], b + 1)
                if n == 4:
                    pe.wait_ge(S["oisb"], b * NJ + 1)
                pe.wait_ge(S["sc"], b * 8 + (n + 1))
                for i in range(4):
                    h = four * 4 + i
                    last = pe.matmul(bank[7][32 * i:32 * i + 32, four * P:(four + 1) * P], v1[:, j, h * HD:h * HD + 2 * HD],
                                     ring1[n % 3][:, i * P:(i + 1) * P], start=True, stop=True, skip_group_check=True)
                last.then_inc(S["oi"], 1)

            def b_step(b, n):
                if n < 8:
                    b_score(b, n)
                if n >= 2:
                    b_intra(b, n - 2)

            def b_turn_back(b):
                for j in range(NJ):
                    pe.wait_ge(S["oisb"], b * NJ + (j + 1))
                    if j == 0:
                        pe.wait_ge(S["sc"], b * 8 + 8)
                    for four in range(4):
                        last = pe.transpose(bank[5 + j][:, four * P:(four + 1) * P], osb1[j][:, four * P:(four + 1) * P], ident_f[:])
                last.then_inc(S["oit_ps"], 1)

            def b_turn_cat(b):
                pe.wait_ge(S["og"], b + 1)
                transposes(bank[7], cat1, "gt_ps")

            def b_project(b, hi=h_hi[:, 1, :], lo=h_lo[:, 1, :]):
                pe.wait_ge(S["g_hi"], b + 1)
                pe.wait_ge(S["g_lo"], b + 1)
                for j in range(NJ):
                    for c in range(NC):
                        last = mm3(pe, bank[5][:, j * D:(j + 1) * D], tx(c, j, hi, lo), wx("wo1", c, 0, D), c == 0, c == NC - 1)
                last.then_inc(S["out1"], 1)

            def unit_hidden(n):
                slot, m = n // 2 % SLOTS, n % 2
                half = n // (E * NC)
                cols = slice(half * HALF, (half + 1) * HALF)
                if n == 0:
                    pe.wait_ge(S["x1"], B)
                if n % (E * NC) == 0:
                    pe.wait_ge(S["t1_kept"], (half + 1) * B)
                if n == 0:
                    pe.wait_ge(S["first_wi_0"], 1)
                elif m == 0 and (n < E * NC or n >= UNITS - SLOTS * NC):
                    s = n // 2 - (SLOTS if n >= E * NC else 0)
                    pe.wait_ge(S[f"e_split{s % 2}"], s // 2 + 1)
                if n >= 2:
                    pe.wait_ge(S["e_m"], n - 1)
                for which in range(2):
                    if which == 1 and n == 0:
                        pe.wait_ge(S["e_split0"], 1)
                    elif which == 1:
                        pe.wait_ge(S["e_s"], n)
                    for c in range(NC):
                        last = mm3(pe, bank[(2 * n + which) % 3][:, :], ew(slot, which, c, m * P, (m + 1) * P),
                                   (t_hi_all[:, c, cols], t_lo_all[:, c, cols]), c == 0, c == NC - 1)
                    last.then_inc(S[f"h{which}_ps"], 1)

            def ew(slot, which, row, c0, c1):
                o = which * NC * D + row * D
                return e_hi[slot][:, o + c0:o + c1], e_lo[slot][:, o + c0:o + c1]

            def unit_out(n):
                slot, m = n // 2 % SLOTS, n % 2
                half = n // (E * NC)
                if n == E * NC:
                    pe.wait_ge(S["x2"], B)
                pe.wait_ge(S["eh_hi"], n + 1)
                pe.wait_ge(S["eh_lo"], n + 1)
                for t in range(HALF // P):
                    last = mm3(pe, bank[3 + 2 * half + t // 2][:, (t % 2) * D:(t % 2 + 1) * D],
                               (h_hi[:, n % 2, t * P:(t + 1) * P], h_lo[:, n % 2, t * P:(t + 1) * P]),
                               ew(slot, 2, m, 0, D), n % (E * NC) == 0 and t % 2 == 0, n % (E * NC) == E * NC - 1)
                last.then_inc(S["e_out"], 1)

            def units(a, z):
                for n in range(a, z):
                    unit_hidden(n)
                    if n >= 1:
                        unit_out(n - 1)

            a_turn(0, True)
            a_qkv(0, True)
            a_vr(0, bank[0])
            a_mask(0, True)
            a_hidden(0, 0, True)
            a_hidden(0, 1)
            weights(2, True)
            a_scores(0, 0)
            a_scores(0, 1)
            a_hidden(0, 2)
            a_ffn_out(0, 0)
            a_scores(0, 2)
            a_scores(0, 3)
            a_hidden(0, 3)
            a_ffn_out(0, 1)
            a_scores(0, 4)
            a_scores(0, 5)
            a_scores(0, 6)
            a_ffn_out(0, 2)
            a_scores(0, 7)
            a_ffn_out(0, 3)
            a_maxima(0)
            a_turn(1)
            a_qkv(1)
            attend(0)
            a_turn_back(0)
            a_vr(1)
            a_turn_cat(0)
            a_mask(1)
            a_project(0)
            a_hidden(1, 0)
            a_hidden(1, 1)
            a_scores(1, 0)
            b_turn(0)
            weights(3, True)
            pe.wait_ge(S["ones1"], 2)

            def two_layers(b, more):
                b_ready(b - 1)
                for pair, name in enumerate(("wq1", "wk1", "wv1"), 1):
                    b_product(b - 1, name)
                    a_scores(b, pair)
                b_narrow(b - 1)
                a_hidden(b, 2)
                a_ffn_out(b, 0)
                b_gate(b - 1)
                a_scores(b, 4)
                a_hidden(b, 3)
                a_ffn_out(b, 1)
                a_scores(b, 5)
                b_turn_qk(b - 1)
                a_scores(b, 6)
                a_ffn_out(b, 2)
                a_scores(b, 7)
                a_ffn_out(b, 3)
                a_maxima(b)
                if more:
                    a_turn(b + 1)
                b_turn_combine(b - 1)
                b_state(b - 1)
                if more:
                    a_qkv(b + 1, beside=b - 1)
                attend(b, more, b - 1)
                b_step(b - 1, 7)
                a_turn_back(b)
                b_step(b - 1, 8)
                if more:
                    a_vr(b + 1)
                b_step(b - 1, 9)
                a_turn_cat(b)
                if more:
                    a_mask(b + 1)
                a_project(b)
                b_turn_back(b - 1)
                if more:
                    a_hidden(b + 1, 0)
                    a_hidden(b + 1, 1)
                    a_scores(b + 1, 0)
                else:
                    unit_hidden(0)
                b_turn(b)
                b_turn_cat(b - 1)
                if not more:
                    unit_hidden(1)
                b_project(b - 1)

            with pe.Fori(1, B - 1) as b:
                two_layers(b, True)
            two_layers(B - 1, False)

            b_ready(B - 1)
            b_product(B - 1, "wq1")
            b_product(B - 1, "wk1")
            pe.wait_ge(S["x2"], B - 1)
            b_product(B - 1, "wv1")
            b_narrow(B - 1)
            unit_out(0)
            units(2, AT["gate"])
            b_gate(B - 1)
            units(AT["gate"], AT["qk"])
            b_turn_qk(B - 1)
            units(AT["qk"], AT["combine"])
            b_turn_combine(B - 1)
            units(AT["combine"], AT["state"])
            b_state(B - 1)
            units(AT["state"], AT["inter"])
            b_inter(B - 1)
            units(AT["inter"], AT["attend"])
            b_step(B - 1, 0)
            b_step(B - 1, 1)
            units(AT["attend"], AT["attend"] + 1)
            for n in range(2, 10):
                b_step(B - 1, n)
            b_turn_back(B - 1)
            units(AT["attend"] + 1, AT["cat"])
            b_turn_cat(B - 1)
            units(AT["cat"], AT["project"])
            b_project(B - 1, t1_hi, t1_lo)
            units(AT["project"], UNITS)
            unit_out(UNITS - 1)

        @block.scalar
        def _(act):
            cp = ACT.Copy

            def copy(dst, src, done, *waits):
                for name, value in waits:
                    act.wait_ge(S[name], value)
                act.activation(dst, src, cp).then_inc(S[done], 1)

            def high_group(g):
                a, z = SPAN[g]
                copy(w_hi[:, a:z], arena[:, a:z], "w_hi", (f"w_in{g}", 16 * len(GROUPS[g])))

            def a_turn(b):
                copy(t_hi[:], bank[4][:], "t_hi", ("t_ps", b + 1))

            def a_mask(b):
                copy(mask_t, bank[0][:].bitcast(BF16)[0:NBLK, 0:T], "mask_t", ("mask_ps", b + 1))

            def a_gelu(b, i):
                act.wait_ge(S["h_ps"], b * 4 + (i + 1))
                act.activation(hg[i % 2], bank[2][:], ACT.Gelu).then_inc(S["hg"], 1)

            def a_high(b, i):
                if i >= 2:
                    act.wait_ge(S["ffn_out"], b * 4 + (i - 1))
                copy(h_hi[:, i % 2, :], hm[i % 2], "h_hi", ("hm", b * 4 + (i + 1)))

            def a_ffn(b, i):
                a_gelu(b, i)
                a_high(b, i)

            def a_maxima(b):
                copy(nm_t, bank[4][:].bitcast(BF16)[0:2 * H, 0:T], "nm_t", ("nm_ps", b + 1))
                act.wait_ge(S["nm_t"], b + 1)
                act.dma_start(nm_dram, nm_t).then_inc(S["nm_out"], 16)

            def a_maxima_in(b):
                act.wait_ge(S["nm_out"], (b + 1) * 16)
                act.dma_start(q_hat[KS:KM, :, :], nm_dram.rearrange("(s h) t -> s h t", s=2)).then_inc(S["nm_in"], 16)

            def attend(b, beside=None):
                for n in range(16):
                    act.wait_ge(S["st_ps"], b * 16 + (n + 1))
                    if n >= 4:
                        act.wait_ge(S["pv"], b * 16 + (n - 3))
                    act.activation(ring[n % 4], bank[3 * (n % 2)][:], ACT.Exp, scale=1.0 / HD).then_inc(S["probs"], 1)
                    if n == 8 and beside is not None:
                        b_inter(beside)
                    if n == 10:
                        copy(osb[0], bank[2][:], "osb", ("pv", b * 16 + 8))
                if beside is not None:
                    b_chunk(beside, 0)
                copy(osb[1], bank[4][:], "osb", ("pv", b * 16 + 16))
                if beside is not None:
                    b_chunk(beside, 1)

            def a_project(b):
                copy(h_hi[:, 0, :], bank[2][:], "c_hi", ("ct_ps", b + 1))

            def b_turn(b):
                copy(t1_hi[:], bank[6][:], "t1_hi", ("t1_ps", b + 1))

            def b_qkv(b):
                act.wait_ge(S["wq1_ps"], b + 1)
                act.activation(a1[:, 0:512], bank[6][:], ACT.Silu).then_inc(S["silu"], 1)
                act.wait_ge(S["wk1_ps"], b + 1)
                act.activation(a1[:, 512:1024], bank[7][:], ACT.Silu).then_inc(S["silu"], 1)
                copy(v1[:, :, 0:D], bank[5][:].rearrange("p (j d) -> p j d", j=NJ), "v1", ("wv1_ps", b + 1))
                copy(g1_t, bank[6][0:HD, T:2 * T], "g1_t", ("g1_ps", b + 1))

            def b_features(b):
                for k, (sem, src) in enumerate((("qt_ps", bank[6]), ("kt_ps", bank[5]))):
                    copy(a1[:, 512 * k:512 * (k + 1)], src[:], "qt", (sem, b + 1))
                    copy(qk_sp[:, 0, 512 * k:512 * (k + 1)], src[:], "qt_hi")

            def b_gate(b):
                act.wait_ge(S["gate_ps"], b + 1)
                act.wait_ge(S["kt_ps"], b + 1)
                act.wait_ge(S["kd"], b + 1)
                act.activation(tg, bank[7][:], ACT.Tanh, scale=0.5).then_inc(S["tg"], 1)

            def b_tanh(b):
                act.wait_ge(S["cw_d"], b + 1)
                act.activation(cw[:, :, 1, :], cw[:, :, 0, :], ACT.Tanh, scale=0.5).then_inc(S["cw_tanh"], 1)

            def b_combine(b):
                copy(cw_t[:, bass.ds(b * T, T)], bank[7][0:E, 0:T], "cw_t", ("cwt_ps", b + 1))

            def b_inter(b):
                copy(inter, bank[7][:, D:2 * D], "inter", ("inter_ps", b + 1))

            def b_chunk(b, j):
                copy(osb1[j], bank[7][:], "oisb", ("oi", b * 8 + 4 * (j + 1)))

            def b_attend(b):
                for j in range(NJ):
                    b_chunk(b, j)

            def b_project(b):
                copy(h_hi[:, 1, :], bank[7][:], "g_hi", ("gt_ps", b + 1))

            for name in EARLY:
                act.dma_start(consts[name][:], A["c_" + name]).then_inc(S["c0_in"], 16)
            high_group(0)
            a_turn(0)
            high_group(1)
            a_mask(0)
            high_group(2)
            a_ffn(0, 0)
            a_ffn(0, 1)
            act.wait_ge(S["wo1_weighted"], 1)
            high_group(3)
            a_ffn(0, 2)
            a_ffn(0, 3)
            a_maxima(0)
            a_turn(1)
            a_maxima_in(0)
            attend(0)
            a_project(0)
            a_mask(1)
            a_gelu(1, 0)
            a_high(1, 0)
            a_gelu(1, 1)
            b_turn(0)
            a_high(1, 1)

            def expert_high(s):
                act.wait_ge(S[f"e_in{s % 2}"], (s // 2 + 1) * 16)
                if s >= SLOTS:
                    act.wait_ge(S["e_out"], 2 * (s - SLOTS) + 2 + (E if s >= E else 0))
                act.activation(e_hi[s % SLOTS], e_stage[:, (s + 1) % 2, :], cp).then_inc(S["e_hi"], 1)

            def unit_silu(n):
                act.wait_ge(S["h0_ps"], n + 1)
                if n >= 2:
                    act.wait_ge(S["e_p"], n - 1)
                act.activation(e_s[n % 2], bank[2 * n % 3][:], ACT.Silu).then_inc(S["e_s"], 1)

            def unit_high(n):
                act.wait_ge(S["e_m"], n + 1)
                if n >= 2:
                    act.wait_ge(S["e_out"], n - 1)
                elif n == 1:
                    act.wait_ge(S["out1"], B - 1)
                act.activation(h_hi[:, n % 2, :], e_p[n % 2], cp).then_inc(S["eh_hi"], 1)
                for s, at in SPLIT_AFTER:
                    if n == at:
                        expert_high(s)

            def units(a, z):
                for n in range(a, z):
                    unit_silu(n)
                    unit_high(n)

            def two_layers(b, more):
                b_qkv(b - 1)
                a_ffn(b, 2)
                a_ffn(b, 3)
                act.wait_ge(S["qk_out"], (b + 1) * 48)
                b_features(b - 1)
                a_maxima(b)
                b_tanh(b - 1)
                if more:
                    a_turn(b + 1)
                b_gate(b - 1)
                b_combine(b - 1)
                a_maxima_in(b)
                attend(b, b - 1)
                a_project(b)
                if more:
                    a_mask(b + 1)
                    a_gelu(b + 1, 0)
                    a_high(b + 1, 0)
                    a_gelu(b + 1, 1)
                else:
                    expert_high(0)
                    unit_silu(0)
                b_turn(b)
                b_project(b - 1)
                if more:
                    act.wait_ge(S["out1"], b)
                    a_high(b + 1, 1)

            with act.Fori(1, B - 1) as b:
                two_layers(b, True)
            two_layers(B - 1, False)

            unit_silu(1)
            expert_high(1)
            unit_high(0)
            b_qkv(B - 1)
            unit_high(1)
            expert_high(2)
            unit_silu(2)
            b_tanh(B - 1)
            unit_high(2)
            units(3, AT["gate"])
            b_features(B - 1)
            unit_silu(AT["gate"])
            b_gate(B - 1)
            expert_high(3)
            unit_high(AT["gate"])
            b_combine(B - 1)
            units(AT["combine"], AT["inter"])
            b_inter(B - 1)
            units(AT["inter"], AT["attend"])
            unit_silu(AT["attend"])
            b_attend(B - 1)
            unit_high(AT["attend"])
            units(AT["attend"] + 1, AT["cat"])
            copy(t1_hi[:], bank[7][:], "g_hi", ("gt_ps", B), ("t1_kept", B * 2))
            units(AT["cat"], UNITS)

        @block.vector
        def _(dve):
            tt, ts, stt = dve.tensor_tensor, dve.tensor_scalar, dve.scalar_tensor_tensor
            NV = G * HD + NBLK

            def hold():
                dve.memset(tick[:], 0.0)

            def rsqrt(a, z, it, name, dst=None):
                v, y, t, r = (rs[:, i, a:z] for i in range(4))
                dst = r if dst is None else dst
                steps = [
                    lambda: ts(y.bitcast(I32), v.bitcast(I32), 1, None, ALU.logical_shift_right),
                    lambda: ts(r.bitcast(I32), y.bitcast(I32), -1.0, float(0x5F3759DF), ALU.mult, ALU.add),
                    lambda: ts(v, v, -0.5, None, ALU.mult),
                ]
                for k in range(3):
                    steps += [
                        lambda: tt(t, r, r, ALU.mult),
                        lambda: tt(t, t, v, ALU.mult),
                        lambda k=k: stt(r if k < 2 else dst, t, 1.5, r, ALU.add, ALU.mult),
                    ]
                for k, step in enumerate(steps):
                    step().then_inc(S[name], 1)
                    dve.wait_ge(S[name], (it - 1) * len(steps) + (k + 1))

            def x_tile(b, j):
                return x_all[:, bass.ds(b * NJ + j, 1), :].rearrange("p o d -> p (o d)")

            def a_statistics(first, n, name):
                for j in range(first, first + n):
                    last = dve.bn_stats(stats[:, j, :], x_all[:, j, :])
                last.then_inc(S[name + "_stats"], 1)
                dve.wait_ge(S[name + "_stats"], 1)
                for j in range(first, first + n):
                    last = dve.bn_aggr(mv0[:, j, :], stats[:, j, :])
                last.then_inc(S[name + "_mv"], 1)
                dve.wait_ge(S[name + "_mv"], 1)
                ts(rs[:, 0, 0:n], mv0[:, first:first + n, 1], EPS_LN, None, ALU.add).then_inc(S[name + "_var"], 1)
                dve.wait_ge(S[name + "_var"], 1)
                rsqrt(0, n, 1, name + "_rs", rstd0[:, first:first + n])

            def a_normed(b):
                for j in range(NJ):
                    last = ts(xn[:, j * D:(j + 1) * D], x_tile(b, j), mv0[:, bass.ds(b * NJ + j, 1), 0:1].rearrange("p o d -> p (o d)"),
                              rstd0[:, bass.ds(b * NJ + j, 1)], ALU.subtract, ALU.mult)
                last.then_inc(S["xn"], 1)

            def b_statistics(b):
                hold()
                for j in range(NJ):
                    last = dve.bn_stats(stats[:, j, :], x_tile(b, j))
                last.then_inc(S["xn1_stats"], 1)

            def b_variance(b):
                it = b + 1
                dve.wait_ge(S["xn1_stats"], it)
                hold()
                for j in range(NJ):
                    last = dve.bn_aggr(mv[:, j, :], stats[:, j, :])
                last.then_inc(S["xn1_mv"], 1)
                dve.wait_ge(S["xn1_mv"], it)
                ts(rs[:, 0, NJ * H:], mv[:, :, 1], EPS_LN, None, ALU.add).then_inc(S["xn1_var"], 1)
                dve.wait_ge(S["xn1_var"], it)

            def b_normed(b):
                for j in range(NJ):
                    last = ts(xn1[:, j * D:(j + 1) * D], x_tile(b, j), mv[:, j, 0:1], rs[:, 3, NJ * H + j:NJ * H + j + 1], ALU.subtract, ALU.mult)
                last.then_inc(S["xn1"], 1)

            def low_part(lo, ps, hi, done, hi_done, it):
                dve.wait_ge(S[hi_done], it)
                tt(lo[:], ps, hi[:].bitcast(F32), ALU.subtract).then_inc(S[done], 1)

            def bf16_parts(src, work, n, sem, it):
                q = S[sem + "_step"]
                dve.tensor_copy(qk_sp[:, 0, 0:n], src).then_inc(q, 1)
                dve.wait_ge(q, it * 3 - 2)
                tt(work[:, 0:n], src, qk_sp[:, 0, 0:n], ALU.subtract).then_inc(q, 1)
                dve.wait_ge(q, it * 3 - 1)
                dve.tensor_copy(qk_sp[:, 1, 0:n], work[:, 0:n]).then_inc(q, 1)
                dve.wait_ge(q, it * 3)
                tt(qk_sp[:, 2, 0:n], work[:, 0:n], qk_sp[:, 1, 0:n], ALU.subtract).then_inc(S[sem], 1)

            def a_rope(b, first=False):
                it = b + 1
                dve.wait_ge(S["qk_ps"], it)
                src = (bank[4][:, 0:T], bank[4][:, T:2 * T], bank[6][:, 0:T])
                srcp = (bank[5][:, 0:T], bank[5][:, T:2 * T], bank[6][:, T:2 * T])
                for s in range(3):
                    stt(a0[:, s * T:(s + 1) * T], src[s], consts["bqk"][:, s:s + 1], consts["cos0"][:], ALU.add, ALU.mult)
                    last = stt(b0[:, s * T:(s + 1) * T], srcp[s], consts["bqkp"][:, s:s + 1], consts["sin0"][:], ALU.add, ALU.mult)
                last.then_inc(S["rope"], 1)
                dve.wait_ge(S["rope"], it)
                if not (isinstance(b, int) and b == 0):
                    dve.wait_ge(S["nm_ps"], b)
                tt(c0, a0, b0, ALU.add).then_inc(S["roped"], 1)
                dve.wait_ge(S["roped"], it)
                if not first:
                    dve.wait_ge(S["qk1_out"], (b - 1) * 48)
                bf16_parts(c0, a0, 3 * T, "qk_sp", it)

            def a_router(b, vr=bank[4]):
                it = b + 1
                dve.wait_ge(S["vr_ps"], it)
                vr = vr[:, 0:NJ * NV].rearrange("p (j n) -> p j n", j=NJ)
                for j in range(NJ):
                    tt(v_aug[:, j, :, 0:HD], vr[:, j, 0:G * HD].rearrange("p (g d) -> p g d", g=G),
                       bv_b[:].rearrange("p (g d) -> p g d", g=G), ALU.add)
                    last = tt(lg[:, j, 0:NBLK], vr[:, j, G * HD:NV], br_b[:], ALU.add)
                last.then_inc(S["lg"], 1)
                dve.wait_ge(S["lg"], it)
                hold()
                for j in range(NJ):
                    last = dve.max(top[:, j, :], lg[:, j, 0:NBLK])
                last.then_inc(S["top"], 1)
                dve.wait_ge(S["top"], it)
                dve.memset(top[:, :, TOPK:8], LOW).then_inc(S["top4"], 1)
                dve.wait_ge(S["top4"], it)
                hold()
                for j in range(NJ):
                    last = dve.match_replace(rep[:, j, :], top[:, j, :], lg[:, j, :], HIGH)
                last.then_inc(S["rep"], 1)
                dve.wait_ge(S["rep"], it)
                tt(mask[:], rep[:, :, 0:NBLK], lg[:, :, 0:NBLK], ALU.is_gt).then_inc(S["mask"], 1)

            def a_masked(b, i):
                dve.wait_ge(S["m_ps"], b * 4 + (i + 1))
                dve.wait_ge(S["hg"], b * 4 + (i + 1))
                if i >= 2:
                    dve.wait_ge(S["h_lo"], b * 4 + (i - 1))
                tt(hm[i % 2], bank[4][:], hg[i % 2], ALU.mult).then_inc(S["hm"], 1)

            def a_score_maxima(b, pair):
                for h in range(2 * pair, 2 * pair + 2):
                    dve.wait_ge(S["s_ps"], b * H + (h + 1))
                    dve.tensor_reduce(nm[:, :, h:h + 1], bank[3 * (h % 2)][:].rearrange("p (j t) -> p j t", j=NJ), AX.X, ALU.max).then_inc(S["max"], 1)

            def a_maxima(b):
                dve.wait_ge(S["max"], (b + 1) * H)
                ts(nm_sp[:, :, 0:H], nm[:], -1.0, None, ALU.mult).then_inc(S["nm_hi"], 1)
                dve.wait_ge(S["nm_hi"], b + 1)
                stt(nm_sp[:, :, H:2 * H], nm[:], -1.0, nm_sp[:, :, 0:H], ALU.mult, ALU.subtract).then_inc(S["nm_sp"], 1)

            def a_normalize(b):
                dve.wait_ge(S["ot_ps"], b + 1)
                for j in range(NJ):
                    o = bank[3 * j][:].rearrange("p (g h q e) -> p g h q e", g=G, h=2, q=4)
                    last = dve.reciprocal(rden[:, j, :].rearrange("p (g h q) -> p g h q", g=G, h=2), o[:, :, :, :, HD])
                last.then_inc(S["rden"], 1)
                dve.wait_ge(S["rden"], b + 1)
                for j in range(NJ):
                    o = bank[3 * j][:].rearrange("p (g h q e) -> p g h q e", g=G, h=2, q=4)
                    r = rden[:, j, :].rearrange("p (g h q) -> p g h q", g=G, h=2)
                    dst = cat[:, j * D:(j + 1) * D].rearrange("p (g q h d) -> p g h q d", g=G, q=4, h=2)
                    for g in range(G):
                        last = tt(dst[:, g], o[:, g, :, :, 0:HD], r[:, g].unsqueeze(3).to_broadcast([P, 2, 4, HD]), ALU.mult)
                last.then_inc(S["cat"], 1)

            def a_residual(b):
                x_b = x_all[:, bass.ds(b * NJ, NJ), :]
                dve.wait_ge(S["x_bo"], b + 1)
                dve.wait_ge(S["out0"], b + 1)
                tt(x_b, bank[1][:].rearrange("p (j d) -> p j d", j=NJ), x_b, ALU.add).then_inc(S["x1"], 1)

            def b_rotate(b):
                it = b + 1
                dve.wait_ge(S["silu"], it * 2 - 1)
                s, u, v, cos, sin = rotation(0)
                tt(u, s, cos, ALU.mult)
                for x, y in HALVES:
                    last = tt(v[:, :, :, x], s[:, :, :, y], sin[:, :, :, x], ALU.mult)
                last.then_inc(S["rot_uv"], 1)
                dve.wait_ge(S["g1_t"], it)
                dve.tensor_copy(lg1[:, :, 0:E], bank[6][:, 0:NJ * E].rearrange("p (j e) -> p j e", j=NJ)).then_inc(S["lg1"], 1)

            def b_rotate_sum(b):
                it = b + 1
                dve.wait_ge(S["rot_uv"], it)
                tt(c1[:, 0:512], c1[:, 0:512], b1[:, 0:512], ALU.add).then_inc(S["rot"], 1)

            def b_parts(b):
                it = b + 1
                dve.wait_ge(S["qt"], it * 2)
                dve.wait_ge(S["qt_hi"], it * 2)
                q = S["qk1_step"]
                tt(b1, a1, qk_sp[:, 0, :], ALU.subtract).then_inc(q, 1)
                dve.wait_ge(q, it * 2 - 1)
                dve.tensor_copy(qk_sp[:, 1, :], b1).then_inc(q, 1)
                dve.wait_ge(q, it * 2)
                tt(qk_sp[:, 2, :], b1, qk_sp[:, 1, :], ALU.subtract).then_inc(S["qk1_sp"], 1)
                dve.wait_ge(S["qk1_sp"], it)
                tt(qd.rearrange("p (c t) -> p c t", c=NC), a1[:, 0:512].rearrange("p (c t) -> p c t", c=NC)[:, :, P:T],
                   consts["decay_q"][:], ALU.mult).then_inc(S["qd"], 1)

            def b_combine(b):
                it = b + 1
                dve.wait_ge(S["lg1"], it)
                hold()
                for j in range(NJ):
                    last = dve.max(top[:, j, :], lg1[:, j, 0:E])
                last.then_inc(S["top_e"], 1)
                dve.wait_ge(S["top_e"], it)
                tt(cw[:, :, 2, 0:1], top[:, :, 0:1], top[:, :, 1:2], ALU.add).then_inc(S["top_sum"], 1)
                dve.wait_ge(S["top_sum"], it)
                dve.memset(top[:, :, TOPE:8], LOW).then_inc(S["top2"], 1)
                dve.wait_ge(S["top2"], it)
                hold()
                for j in range(NJ):
                    dve.match_replace(rep[:, j, 0:16], top[:, j, :], lg1[:, j, :], HIGH)
                    last = ts(cw[:, j, 0, :], lg1[:, j, 0:E], 2.0, cw[:, j, 2, 0:1], ALU.mult, ALU.subtract)
                last.then_inc(S["cw_d"], 1)
                dve.wait_ge(S["cw_d"], it)
                tt(cw[:, :, 2, :], rep[:, :, 0:E], lg1[:, :, 0:E], ALU.is_gt).then_inc(S["cw_sel"], 1)
                dve.wait_ge(S["cw_tanh"], it)
                ts(cw[:, :, 3, :], cw[:, :, 1, :], 0.5, 0.5, ALU.mult, ALU.add).then_inc(S["cw_sig"], 1)
                dve.wait_ge(S["cw_sig"], it)
                tt(cw[:, :, 0, :], cw[:, :, 3, :], cw[:, :, 2, :], ALU.mult).then_inc(S["cw"], 1)

            def b_state(b):
                dve.wait_ge(S["qd"], b + 1)
                dve.wait_ge(S["kv_ps"], b + 1)
                for c in range(NC):
                    last = tt(state[:, c * P:(c + 1) * P], bank[7][:, c * P:(c + 1) * P], consts["blockdiag"][:], ALU.mult)
                last.then_inc(S["state"], 1)

            def b_decay(b, a, z):
                for n in range(a, z):
                    four = n % 4
                    dve.wait_ge(S["s1_ps"], b * 8 + (n + 1))
                    if n >= 3:
                        dve.wait_ge(S["oi"], b * 8 + (n - 2))
                    tt(ring1[n % 3].rearrange("p (h t) -> p h t", h=4), bank[5 + n % 2][:].rearrange("p (h t) -> p h t", h=4),
                       consts["decay"][:, four * 4:(four + 1) * 4, :], ALU.mult).then_inc(S["sc"], 1)

            def b_sigmoid(b):
                dve.wait_ge(S["tg"], b + 1)
                ts(tg, tg, 0.5, 0.5, ALU.mult, ALU.add).then_inc(S["gate"], 1)

            def b_gated(b):
                it = b + 1
                o_sb = a1[:, 0:512]
                dve.wait_ge(S["oit_ps"], it)
                dve.wait_ge(S["inter"], it)
                dve.wait_ge(S["gate"], it)
                for j in range(NJ):
                    o = bank[5 + j][:].rearrange("p (h e) -> p h e", h=H)[:, :, 0:HD]
                    o_j = o_sb[:, j * D:(j + 1) * D].rearrange("p (h e) -> p h e", h=H)
                    if j == 0:
                        tt(o_j, o, tg[:, 0:D].rearrange("p (h e) -> p h e", h=H), ALU.mult).then_inc(S["gated"], 1)
                    else:
                        tt(o_j, o, inter.rearrange("p (h e) -> p h e", h=H), ALU.add).then_inc(S["o1_sum"], 1)
                dve.wait_ge(S["o1_sum"], it)
                tt(o_sb[:, D:2 * D], o_sb[:, D:2 * D], tg[:, D:2 * D], ALU.mult).then_inc(S["gated"], 1)
                dve.wait_ge(S["gated"], it * 2)
                tt(c1[:, 512:1024], o_sb, o_sb, ALU.mult).then_inc(S["sq"], 1)
                dve.wait_ge(S["sq"], it)
                dve.tensor_reduce(ms, c1[:, 512:1024].rearrange("p (h e) -> p h e", e=HD), AX.X, ALU.add).then_inc(S["ms"], 1)

            def b_mean_squares(b):
                dve.wait_ge(S["ms"], b + 1)
                ts(rs[:, 0, 0:NJ * H], ms, 1.0 / HD, EPS_RMS, ALU.mult, ALU.add).then_inc(S["ms_mean"], 1)
                dve.wait_ge(S["ms_mean"], b + 1)

            def b_gated_norm(b):
                it = b + 1
                o_sb, r = a1[:, 0:512], rs[:, 3, 0:NJ * H]
                tt(cat1.rearrange("p (h e) -> p h e", e=HD), o_sb.rearrange("p (h e) -> p h e", e=HD),
                   r.unsqueeze(2).to_broadcast([P, NJ * H, HD]), ALU.mult).then_inc(S["og"], 1)

            def b_low_cat(b):
                low_part(h_lo[:, 1, :], bank[7][:], h_hi[:, 1, :], "g_lo", "g_hi", b + 1)

            def b_residual(b):
                x_b = x_all[:, bass.ds(b * NJ, NJ), :]
                dve.wait_ge(S["out1"], b + 1)
                tt(x_b, bank[5][:].rearrange("p (j d) -> p j d", j=NJ), x_b, ALU.add).then_inc(S["x2"], 1)

            dve.wait_ge(S["x_in0"], 16)
            a_statistics(0, NJ, "first")
            a_normed(0)
            a, z = SPAN[0]
            dve.wait_ge(S["w_hi"], 1)
            tt(w_lo[:, a:z], arena[:, a:z], w_hi[:, a:z].bitcast(F32), ALU.subtract).then_inc(S["w_lo0"], 1)
            low_part(t_lo, bank[4][:], t_hi, "t_lo", "t_hi", 1)
            dve.wait_ge(S["c0_in"], 16 * len(EARLY))
            dve.wait_ge(S["b_in"], 16 * 2)
            a_rope(0, True)
            dve.wait_ge(S["ones"], 3)
            a_router(0, bank[0])
            dve.wait_ge(S["x_in1"], 16 * (B - 1))
            a_statistics(NJ, (B - 1) * NJ, "others")
            a_masked(0, 0)
            a_masked(0, 1)
            a_score_maxima(0, 0)
            a_score_maxima(0, 1)
            a_masked(0, 2)
            a_score_maxima(0, 2)
            a_score_maxima(0, 3)
            a_normed(1)
            a_masked(0, 3)
            a_score_maxima(0, 4)
            a_score_maxima(0, 5)
            a_score_maxima(0, 6)
            a_score_maxima(0, 7)
            a_maxima(0)
            low_part(t_lo, bank[4][:], t_hi, "t_lo", "t_hi", 2)
            a_rope(1, True)
            dve.wait_ge(S["c1_in"], 16 * (len(consts) - len(EARLY) + 2))
            a_normalize(0)
            a_router(1)
            low_part(h_lo[:, 0, :], bank[2][:], h_hi[:, 0, :], "c_lo", "c_hi", 1)
            a_residual(0)
            dve.wait_ge(S["x1"], 1)
            dve.wait_ge(S["w_lo"], len(GROUPS) - 1)
            dve.wait_ge(S["ones1"], 2)
            b_statistics(0)
            b_variance(0)
            a_masked(1, 0)
            rsqrt(NJ * H, NJ * H + NJ, 1, "start_rs")
            b_normed(0)
            low_part(t1_lo, bank[6][:], t1_hi, "t1_lo", "t1_hi", 1)
            a_masked(1, 1)
            a_score_maxima(1, 0)

            def expert_low(s):
                dve.wait_ge(S["e_hi"], s + 1)
                tt(e_lo[s % SLOTS], e_stage[:, (s + 1) % 2, :], e_hi[s % SLOTS].bitcast(F32), ALU.subtract).then_inc(S[f"e_split{s % 2}"], 1)

            def units(a, z):
                for n in range(a, z):
                    dve.wait_ge(S["e_p"], n + 1)
                    dve.wait_ge(S["h1_ps"], n + 1)
                    tt(e_p[n % 2], bank[(2 * n + 1) % 3][:], e_p[n % 2], ALU.mult).then_inc(S["e_m"], 1)
                    dve.wait_ge(S["eh_hi"], n + 1)
                    tt(h_lo[:, n % 2, :], e_p[n % 2], h_hi[:, n % 2, :].bitcast(F32), ALU.subtract).then_inc(S["eh_lo"], 1)
                    for s, at in SPLIT_AFTER:
                        if n == at:
                            expert_low(s)

            def two_layers(b, more):
                for pair in range(1, 4):
                    a_score_maxima(b, pair)
                b_rotate(b - 1)
                a_masked(b, 2)
                b_rotate_sum(b - 1)
                a_score_maxima(b, 4)
                a_masked(b, 3)
                a_score_maxima(b, 5)
                if more:
                    a_normed(b + 1)
                a_score_maxima(b, 6)
                a_score_maxima(b, 7)
                a_maxima(b)
                b_combine(b - 1)
                if more:
                    low_part(t_lo, bank[4][:], t_hi, "t_lo", "t_hi", b + 2)
                b_parts(b - 1)
                b_state(b - 1)
                if more:
                    a_rope(b + 1)
                b_decay(b - 1, 0, 8)
                a_normalize(b)
                if more:
                    a_router(b + 1)
                low_part(h_lo[:, 0, :], bank[2][:], h_hi[:, 0, :], "c_lo", "c_hi", b + 1)
                b_sigmoid(b - 1)
                a_residual(b)
                dve.wait_ge(S["x1"], b + 1)
                b_statistics(b)
                b_variance(b)
                b_gated(b - 1)
                b_mean_squares(b - 1)
                if more:
                    a_masked(b + 1, 0)
                rsqrt(0, NJ * H + NJ, b, "rs")
                b_normed(b)
                b_gated_norm(b - 1)
                if more:
                    a_masked(b + 1, 1)
                low_part(t1_lo, bank[6][:], t1_hi, "t1_lo", "t1_hi", b + 1)
                b_low_cat(b - 1)
                if more:
                    a_score_maxima(b + 1, 0)
                else:
                    units(0, 1)
                b_residual(b - 1)

            with dve.Fori(1, B - 1) as b:
                two_layers(b, True)
            two_layers(B - 1, False)

            def result(half):
                dve.wait_ge(S["e_out"], E * NC * (half + 1))
                for i in range(B // 2):
                    at = (half * B // 2 + i) * NJ
                    x_i = x_all[:, at:at + NJ, :].rearrange("p j d -> p (j d)")
                    tt(x_i, bank[3 + 2 * half + i][:], x_i, ALU.add).then_inc(S["y"], 1)

            expert_low(1)
            units(1, 2)
            b_rotate(B - 1)
            b_rotate_sum(B - 1)
            expert_low(2)
            b_combine(B - 1)
            units(2, AT["qk"])
            b_parts(B - 1)
            units(AT["qk"], AT["state"])
            b_state(B - 1)
            units(AT["state"], AT["attend"])
            b_decay(B - 1, 0, 8)
            b_sigmoid(B - 1)
            units(AT["attend"], AT["gated"])
            b_gated(B - 1)
            units(AT["gated"], AT["roots"])
            b_mean_squares(B - 1)
            rsqrt(0, NJ * H, 1, "last_rs")
            units(AT["roots"], AT["roots"] + 1)
            b_gated_norm(B - 1)
            units(AT["roots"] + 1, AT["cat"])
            dve.wait_ge(S["t1_kept"], B * 2)
            low_part(t1_lo, bank[7][:], t1_hi, "g_lo", "g_hi", B)
            units(AT["cat"], AT["project"])
            b_residual(B - 1)
            dve.wait_ge(S["x2"], B)
            units(AT["project"], E * NC + 1)
            result(0)
            units(E * NC + 1, UNITS)
            result(1)


def constants():
    f, bf = np.float32, np.dtype(mybir.dt.np(BF16))
    c = {"ident_f": np.eye(P, dtype=f), "ident_b": np.eye(P, dtype=bf)}
    d = np.arange(P) % HD
    inv0 = (f(1.0) / np.power(f(1250), np.arange(0, HD, 2, dtype=f) / f(HD))).astype(f)
    ang0 = (np.arange(T, dtype=f)[:, None] * inv0[None, :]).astype(f)
    ang0 = np.concatenate([ang0, ang0], -1)
    c["cos0"] = np.cos(ang0).astype(f).T[d]
    c["sin0"] = (np.sin(ang0).astype(f) * np.where(np.arange(HD) < HD // 2, f(-1), f(1))).T[d]
    inv1 = np.power(f(10000.0), f(-2.0) * np.arange(HD // 2, dtype=f) / f(HD)).astype(f)
    ang1 = (np.arange(T, dtype=f)[:, None] * inv1[None, :]).astype(f)
    cos1, sin1 = np.cos(ang1).astype(f), np.sin(ang1).astype(f)

    def tokens(a):
        return a.reshape(NJ, P, HD).transpose(1, 0, 2)

    c["cos1"] = tokens(np.concatenate([cos1, cos1], -1))
    c["sin1"] = tokens(np.concatenate([-sin1, sin1], -1))
    lam = -(f(2.0) ** (f(-8.0) * (np.arange(H, dtype=f) + f(1.0)) / f(H)))
    i = np.arange(P, dtype=f)
    diff = i[None, :] - i[:, None]
    c["decay"] = np.where(diff[:, None, :] >= 0, np.exp(lam[None, :, None] * np.maximum(diff, 0)[:, None, :]), f(0))
    head = np.arange(D) // HD
    c["decay_q"] = np.exp(lam[head][:, None] * (i[None, :] + f(1))).reshape(NC, P, P).transpose(1, 0, 2)
    c["decay_k"] = np.exp(lam[head][None, :] * (f(P - 1) - i[:, None]))
    c["blockdiag"] = (np.arange(P)[:, None] // HD == np.arange(P)[None, :] // HD).astype(bf)
    blk = np.zeros((NBLK, FF // P, P))
    for m in range(FF // P):
        for p in range(P):
            blk[(m * P + p) // BS, m, p] = 1
    c["sel_blk"] = blk.astype(bf)
    return {"c_" + k: np.ascontiguousarray(v if v.dtype == bf else v.astype(f)) for k, v in c.items()}


def layout(x):
    x = {k: np.asarray(v) for k, v in x.items()}
    perm = np.arange(D).reshape(-1, 2, HD // 2)[:, ::-1].reshape(-1)
    permk = perm[:G * HD]
    wk, bk = x["L0_attn_wk"], x["L0_attn_bk"]
    bq = x["L0_attn_bq"]
    four = P // (G * HD)

    def bias(q, k):
        return np.stack([q[:P], q[P:], np.tile(k, four)], 1)

    ex = np.stack([x["L1_ffn_wi_0"], x["L1_ffn_wi_1"], x["L1_ffn_wo"]], 1)
    a = {
        "x": x["L0_attn_x"].reshape(NTOK, D),
        "wq": x["L0_attn_wq"], "wqp": x["L0_attn_wq"][:, perm],
        "wk": np.tile(wk, (1, four)), "wkp": np.tile(wk[:, permk], (1, four)),
        "wvr": np.concatenate([x["L0_attn_wv"], x["L0_ffn_Wr"].T], 1),
        "w1": x["L0_ffn_W1"].T, "w2": x["L0_ffn_W2"].T, "wo": x["L0_attn_wo"],
        "wq1": x["L1_attn_Wq"], "wk1": x["L1_attn_Wk"], "wv1": x["L1_attn_Wv"],
        "wg1": np.tile(x["L1_attn_Wg1"], (1, P // HD)), "gk": x["L1_ffn_gate_kernel"], "wo1": x["L1_attn_Wo"],
        "experts": ex.reshape(E, 3, NC, P, D).transpose(0, 3, 1, 2, 4).reshape(E, P, EW),
        "bv": x["L0_attn_bv"], "br": x["L0_ffn_br"], "bo": x["L0_attn_bo"], "nw": x["L1_attn_norm_weight"].reshape(NC, P).T,
        "c_bqk": bias(bq, bk), "c_bqkp": bias(bq[perm], bk[permk]), "c_wg2": x["L1_attn_Wg2"],
    }
    return {k: np.ascontiguousarray(v) for k, v in a.items()}


def kernel(**inputs):
    import concourse.bacc as _bacc
    from concourse.bass_utils import run_bass_kernel_spmd as _run

    arrays = {f"in_{k}": v for k, v in {**layout(inputs), **constants()}.items()}
    nc = _bacc.Bacc("TRN2", target_bir_lowering=False, num_devices=1)
    aps = {k[3:]: nc.dram_tensor(k, v.shape, mybir.dt.from_np(v.dtype), kind="ExternalInput").ap() for k, v in arrays.items()}
    out = nc.dram_tensor("out_0", (NTOK, D), F32, kind="ExternalOutput").ap()
    build(nc, aps, out)
    r = _run(nc, [arrays], core_ids=[0])
    return r.results[0]["out_0"].reshape(B, T, D)
```
